# Optimizing a Trainium2 kernel written in Bass

```python
import numpy as np
import jax
import jax.numpy as jnp

def _softmax(x, axis=-1):
    return jax.nn.softmax(x, axis=axis)

def _gelu(x):
    return jax.nn.gelu(x, approximate=True)

def _silu(x):
    return jax.nn.silu(x)

def _sigmoid(x):
    return jax.nn.sigmoid(x)

def _layernorm(x, axis=-1, eps=1e-05):
    m = jnp.mean(x, axis=axis, keepdims=True)
    v = jnp.var(x, axis=axis, keepdims=True)
    return (x - m) / jnp.sqrt(v + eps)

def _scatter_add(tgt, idx, src, axis=0):
    return tgt.at[idx].add(src)

def _segment_sum(src, seg, n):
    return jax.ops.segment_sum(src, seg, n)
kernel_name = 'mk_early_fusion_embed_d1_tok_img768_r4_56ce98'

def setup_inputs(seed: int=0):
    np.random.seed(seed)
    _w = jnp.asarray

    def _rec_inputs():
        import jax
        import jax.numpy as jnp
        _rk = jax.random.key(seed)
        x = -0.000222058 + 0.999998 * jax.random.normal(jax.random.fold_in(_rk, 1), (8, 3, 96, 96), jnp.float32)
        x_txt = jax.random.randint(jax.random.fold_in(_rk, 51), (8, 128), 0, 31993, jnp.int32)
        mask_BS_i1_0 = jnp.where(jnp.ones((8, 128), dtype=bool), 1, 0).astype(jnp.int32)
        return (x, x_txt, mask_BS_i1_0)
    x, x_txt, mask_BS_i1_0 = _rec_inputs()

    def _L0_tok_setup():
        import jax, jax.numpy as jnp
        import numpy as np
        from jax import lax
        HIDDEN = 192
        C_IN = 3
        PATCH = 16
        SIDE = 32
        NUM_PATCHES = SIDE * SIDE

        def _position_ids(nb_h, nb_w):
            boundaries = np.arange(1.0 / SIDE, 1.0, 1.0 / SIDE, dtype=np.float32)
            frac_h = np.arange(0.0, 1.0 - 1e-06, 1.0 / nb_h, dtype=np.float32)
            frac_w = np.arange(0.0, 1.0 - 1e-06, 1.0 / nb_w, dtype=np.float32)
            bh = np.searchsorted(boundaries, frac_h, side='right')
            bw = np.searchsorted(boundaries, frac_w, side='right')
            return jnp.asarray((bh[:, None] * SIDE + bw).reshape(-1), dtype=jnp.int32)
        key = jax.random.key(seed)
        k1, k2, k3 = jax.random.split(key, 3)
        pixel_values = jax.random.normal(k1, (32, C_IN, 128, 128), dtype=jnp.float32)
        conv_w = jax.random.normal(k2, (HIDDEN, C_IN, PATCH, PATCH), dtype=jnp.float32) * 0.02
        conv_b = jnp.zeros((HIDDEN,), dtype=jnp.float32)
        pos_table = jax.random.normal(k3, (NUM_PATCHES, HIDDEN), dtype=jnp.float32) * 0.02
        return {'pixel_values': pixel_values, 'conv_w': conv_w, 'conv_b': conv_b, 'pos_table': pos_table}
    _L0_tok_all = _L0_tok_setup()
    _L0_tok_in = {k: v for k, v in _L0_tok_all.items() if k in ('conv_w', 'conv_b', 'pos_table')}
    del _L0_tok_all

    def _L0_txt_setup():
        import jax, jax.numpy as jnp
        import numpy as np
        NH = 12
        W = 64
        EPS = 1e-12

        def layer_norm(x, s, b):
            mu = x.mean(-1, keepdims=True)
            var = ((x - mu) ** 2).mean(-1, keepdims=True)
            return (x - mu) / jnp.sqrt(var + EPS) * s + b

        def band_attention(q, k, v, mask):
            B, H, S, d = q.shape
            nc = S // W
            kp = jnp.pad(k, ((0, 0), (0, 0), (W, W), (0, 0)))
            vp = jnp.pad(v, ((0, 0), (0, 0), (W, W), (0, 0)))
            idx = jnp.arange(nc)[:, None] * W + jnp.arange(3 * W)[None, :]
            kb = kp[:, :, idx]
            vb = vp[:, :, idx]
            qc = q.reshape(B, H, nc, W, d)
            scores = jnp.einsum('bhcqd,bhckd->bhcqk', qc, kb) / jnp.sqrt(jnp.asarray(d, q.dtype))
            rel = jnp.arange(3 * W)[None, :] - W - jnp.arange(W)[:, None]
            band_ok = jnp.abs(rel) <= W
            key_abs = idx - W
            pos_ok = (key_abs >= 0) & (key_abs < S)
            mp = jnp.pad(mask, ((0, 0), (W, W)))
            mb = mp[:, idx] > 0
            allowed = mb[:, None, :, None, :] & pos_ok[None, None, :, None, :] & band_ok[None, None, None, :, :]
            scores = jnp.where(allowed, scores, jnp.asarray(-1000000000.0, scores.dtype))
            probs = jax.nn.softmax(scores, axis=-1)
            out = jnp.einsum('bhcqk,bhckd->bhcqd', probs, vb)
            return out.reshape(B, H, S, d)

        def _forward(input_ids, attention_mask, emb_word, emb_pos, emb_ln_s, emb_ln_b, Wq, bq, Wk, bk, Wv, bv, Wo, bo, ln1_s, ln1_b, W1, b1, W2, b2, ln2_s, ln2_b):
            B, S = input_ids.shape
            Hd = emb_word.shape[1]
            dh = Hd // NH
            mask = attention_mask.astype(emb_word.dtype)
            h = layer_norm(emb_word[input_ids] + emb_pos[:S][None], emb_ln_s, emb_ln_b)
            L = Wq.shape[0]
            for l in range(L):

                def heads(x):
                    return x.reshape(B, S, NH, dh).transpose(0, 2, 1, 3)
                q = heads(h @ Wq[l] + bq[l])
                k = heads(h @ Wk[l] + bk[l])
                v = heads(h @ Wv[l] + bv[l])
                a = band_attention(q, k, v, mask)
                a = a.transpose(0, 2, 1, 3).reshape(B, S, Hd)
                h = layer_norm(h + a @ Wo[l] + bo[l], ln1_s[l], ln1_b[l])
                f = jax.nn.gelu(h @ W1[l] + b1[l], approximate=False)
                h = layer_norm(h + f @ W2[l] + b2[l], ln2_s[l], ln2_b[l])
            return h
        key = jax.random.key(seed)
        B, S, Hd, L, V, FF = (2, 1024, 192, 4, 8000, 4 * 192)
        ks = jax.random.split(key, 16)
        std = 0.02
        inp = {'input_ids': jax.random.randint(ks[0], (B, S), 0, V, dtype=jnp.int64) if jax.config.jax_enable_x64 else jax.random.randint(ks[0], (B, S), 0, V, dtype=jnp.int32), 'attention_mask': jnp.ones((B, S), dtype=jnp.int32), 'emb_word': jax.random.normal(ks[1], (V, Hd), jnp.float32) * std, 'emb_pos': jax.random.normal(ks[2], (S, Hd), jnp.float32) * std, 'emb_ln_s': jnp.ones((Hd,), jnp.float32), 'emb_ln_b': jnp.zeros((Hd,), jnp.float32), 'Wq': jax.random.normal(ks[3], (L, Hd, Hd), jnp.float32) * std, 'bq': jnp.zeros((L, Hd), jnp.float32), 'Wk': jax.random.normal(ks[4], (L, Hd, Hd), jnp.float32) * std, 'bk': jnp.zeros((L, Hd), jnp.float32), 'Wv': jax.random.normal(ks[5], (L, Hd, Hd), jnp.float32) * std, 'bv': jnp.zeros((L, Hd), jnp.float32), 'Wo': jax.random.normal(ks[6], (L, Hd, Hd), jnp.float32) * std, 'bo': jnp.zeros((L, Hd), jnp.float32), 'ln1_s': jnp.ones((L, Hd), jnp.float32), 'ln1_b': jnp.zeros((L, Hd), jnp.float32), 'W1': jax.random.normal(ks[7], (L, Hd, FF), jnp.float32) * std, 'b1': jnp.zeros((L, FF), jnp.float32), 'W2': jax.random.normal(ks[8], (L, FF, Hd), jnp.float32) * std, 'b2': jnp.zeros((L, Hd), jnp.float32), 'ln2_s': jnp.ones((L, Hd), jnp.float32), 'ln2_b': jnp.zeros((L, Hd), jnp.float32)}
        return inp
    _L0_txt_all = _L0_txt_setup()
    _L0_txt_in = {k: v for k, v in _L0_txt_all.items() if k in ('emb_word', 'emb_pos', 'emb_ln_s', 'emb_ln_b', 'Wq', 'bq', 'Wk', 'bk', 'Wv', 'bv', 'Wo', 'bo', 'ln1_s', 'ln1_b', 'W1', 'b1', 'W2', 'b2', 'ln2_s', 'ln2_b')}
    del _L0_txt_all

    def _L0_attn_setup():
        import jax, jax.numpy as jnp
        import numpy as np
        EMBED_DIM = 192
        NB_HEAD = 12
        HEAD_DIM = EMBED_DIM // NB_HEAD
        key = jax.random.key(seed)
        ks = jax.random.split(key, 6)
        B, N, E = (8, 256, EMBED_DIM)
        scale = 1.0 / np.sqrt(E)
        x = jax.random.normal(ks[0], (B, N, E), dtype=jnp.float32)
        w_q = jax.random.uniform(ks[1], (E, E), jnp.float32, -scale, scale)
        w_k = jax.random.uniform(ks[2], (E, E), jnp.float32, -scale, scale)
        w_v = jax.random.uniform(ks[3], (E, E), jnp.float32, -scale, scale)
        w_o = jax.random.uniform(ks[4], (E, E), jnp.float32, -scale, scale)
        b_o = jax.random.uniform(ks[5], (E,), jnp.float32, -scale, scale)
        return {'x': x, 'w_q': w_q, 'w_k': w_k, 'w_v': w_v, 'w_o': w_o, 'b_o': b_o}
    _L0_attn_all = _L0_attn_setup()
    _L0_attn_in = {k: v for k, v in _L0_attn_all.items() if k in ('w_q', 'w_k', 'w_v', 'w_o', 'b_o')}
    del _L0_attn_all

    def _L0_ffn_setup():
        import jax, jax.numpy as jnp
        import numpy as np
        B, S, D_IN, D_HID, D_OUT = (32, 128, 192, 768, 192)
        key = jax.random.key(seed)
        k1, k2, k3, k4 = jax.random.split(key, 4)
        init_k = float(np.sqrt(1.0 / D_IN))
        init_k2 = float(np.sqrt(1.0 / D_HID))
        x = jax.random.normal(k1, (B, S, D_IN), dtype=jnp.float32)
        in_weight = jax.random.uniform(k2, (D_HID, D_IN), dtype=jnp.float32, minval=-init_k, maxval=init_k)
        in_bias = jax.random.uniform(k3, (D_HID,), dtype=jnp.float32, minval=-init_k, maxval=init_k)
        out_weight = jax.random.uniform(k4, (D_HID, D_OUT), dtype=jnp.float32, minval=-init_k2, maxval=init_k2)
        return {'x': x, 'in_weight': in_weight, 'in_bias': in_bias, 'out_weight': out_weight}
    _L0_ffn_all = _L0_ffn_setup()
    _L0_ffn_in = {k: v for k, v in _L0_ffn_all.items() if k in ('in_weight', 'in_bias', 'out_weight')}
    del _L0_ffn_all
    return {'x': x, 'x_txt': x_txt, 'mask_BS_i1_0': mask_BS_i1_0, 'L0_tok_conv_w': _L0_tok_in['conv_w'], 'L0_tok_conv_b': _L0_tok_in['conv_b'], 'L0_tok_pos_table': _L0_tok_in['pos_table'], 'L0_txt_emb_word': _L0_txt_in['emb_word'], 'L0_txt_emb_pos': _L0_txt_in['emb_pos'], 'L0_txt_emb_ln_s': _L0_txt_in['emb_ln_s'], 'L0_txt_emb_ln_b': _L0_txt_in['emb_ln_b'], 'L0_txt_Wq': _L0_txt_in['Wq'], 'L0_txt_bq': _L0_txt_in['bq'], 'L0_txt_Wk': _L0_txt_in['Wk'], 'L0_txt_bk': _L0_txt_in['bk'], 'L0_txt_Wv': _L0_txt_in['Wv'], 'L0_txt_bv': _L0_txt_in['bv'], 'L0_txt_Wo': _L0_txt_in['Wo'], 'L0_txt_bo': _L0_txt_in['bo'], 'L0_txt_ln1_s': _L0_txt_in['ln1_s'], 'L0_txt_ln1_b': _L0_txt_in['ln1_b'], 'L0_txt_W1': _L0_txt_in['W1'], 'L0_txt_b1': _L0_txt_in['b1'], 'L0_txt_W2': _L0_txt_in['W2'], 'L0_txt_b2': _L0_txt_in['b2'], 'L0_txt_ln2_s': _L0_txt_in['ln2_s'], 'L0_txt_ln2_b': _L0_txt_in['ln2_b'], 'L0_attn_w_q': _L0_attn_in['w_q'], 'L0_attn_w_k': _L0_attn_in['w_k'], 'L0_attn_w_v': _L0_attn_in['w_v'], 'L0_attn_w_o': _L0_attn_in['w_o'], 'L0_attn_b_o': _L0_attn_in['b_o'], 'L0_ffn_in_weight': _L0_ffn_in['in_weight'], 'L0_ffn_in_bias': _L0_ffn_in['in_bias'], 'L0_ffn_out_weight': _L0_ffn_in['out_weight']}

def reference(x, x_txt, mask_BS_i1_0, L0_tok_conv_w, L0_tok_conv_b, L0_tok_pos_table, L0_txt_emb_word, L0_txt_emb_pos, L0_txt_emb_ln_s, L0_txt_emb_ln_b, L0_txt_Wq, L0_txt_bq, L0_txt_Wk, L0_txt_bk, L0_txt_Wv, L0_txt_bv, L0_txt_Wo, L0_txt_bo, L0_txt_ln1_s, L0_txt_ln1_b, L0_txt_W1, L0_txt_b1, L0_txt_W2, L0_txt_b2, L0_txt_ln2_s, L0_txt_ln2_b, L0_attn_w_q, L0_attn_w_k, L0_attn_w_v, L0_attn_w_o, L0_attn_b_o, L0_ffn_in_weight, L0_ffn_in_bias, L0_ffn_out_weight):
    import jax
    import jax.numpy as jnp

    def _L0_tok_ref(pixel_values, conv_w, conv_b, pos_table):
        import jax, jax.numpy as jnp
        import numpy as np
        from jax import lax
        HIDDEN = 192
        C_IN = 3
        PATCH = 16
        SIDE = 32
        NUM_PATCHES = SIDE * SIDE

        def _position_ids(nb_h, nb_w):
            boundaries = np.arange(1.0 / SIDE, 1.0, 1.0 / SIDE, dtype=np.float32)
            frac_h = np.arange(0.0, 1.0 - 1e-06, 1.0 / nb_h, dtype=np.float32)
            frac_w = np.arange(0.0, 1.0 - 1e-06, 1.0 / nb_w, dtype=np.float32)
            bh = np.searchsorted(boundaries, frac_h, side='right')
            bw = np.searchsorted(boundaries, frac_w, side='right')
            return jnp.asarray((bh[:, None] * SIDE + bw).reshape(-1), dtype=jnp.int32)
        B, _, H, W = pixel_values.shape
        nb_h, nb_w = (H // PATCH, W // PATCH)
        patches = lax.conv_general_dilated(pixel_values, conv_w, window_strides=(PATCH, PATCH), padding='VALID', dimension_numbers=('NCHW', 'OIHW', 'NCHW'))
        patches = patches + conv_b[None, :, None, None]
        embeddings = patches.reshape(B, HIDDEN, nb_h * nb_w).transpose(0, 2, 1)
        pos_ids = _position_ids(nb_h, nb_w)
        pos_emb = pos_table[pos_ids]
        return embeddings + pos_emb[None, :, :]

    def _L0_txt_ref(input_ids, attention_mask, emb_word, emb_pos, emb_ln_s, emb_ln_b, Wq, bq, Wk, bk, Wv, bv, Wo, bo, ln1_s, ln1_b, W1, b1, W2, b2, ln2_s, ln2_b):
        import jax, jax.numpy as jnp
        import numpy as np
        NH = 12
        W = 64
        EPS = 1e-12

        def layer_norm(x, s, b):
            mu = x.mean(-1, keepdims=True)
            var = ((x - mu) ** 2).mean(-1, keepdims=True)
            return (x - mu) / jnp.sqrt(var + EPS) * s + b

        def band_attention(q, k, v, mask):
            B, H, S, d = q.shape
            nc = S // W
            kp = jnp.pad(k, ((0, 0), (0, 0), (W, W), (0, 0)))
            vp = jnp.pad(v, ((0, 0), (0, 0), (W, W), (0, 0)))
            idx = jnp.arange(nc)[:, None] * W + jnp.arange(3 * W)[None, :]
            kb = kp[:, :, idx]
            vb = vp[:, :, idx]
            qc = q.reshape(B, H, nc, W, d)
            scores = jnp.einsum('bhcqd,bhckd->bhcqk', qc, kb) / jnp.sqrt(jnp.asarray(d, q.dtype))
            rel = jnp.arange(3 * W)[None, :] - W - jnp.arange(W)[:, None]
            band_ok = jnp.abs(rel) <= W
            key_abs = idx - W
            pos_ok = (key_abs >= 0) & (key_abs < S)
            mp = jnp.pad(mask, ((0, 0), (W, W)))
            mb = mp[:, idx] > 0
            allowed = mb[:, None, :, None, :] & pos_ok[None, None, :, None, :] & band_ok[None, None, None, :, :]
            scores = jnp.where(allowed, scores, jnp.asarray(-1000000000.0, scores.dtype))
            probs = jax.nn.softmax(scores, axis=-1)
            out = jnp.einsum('bhcqk,bhckd->bhcqd', probs, vb)
            return out.reshape(B, H, S, d)

        def _forward(input_ids, attention_mask, emb_word, emb_pos, emb_ln_s, emb_ln_b, Wq, bq, Wk, bk, Wv, bv, Wo, bo, ln1_s, ln1_b, W1, b1, W2, b2, ln2_s, ln2_b):
            B, S = input_ids.shape
            Hd = emb_word.shape[1]
            dh = Hd // NH
            mask = attention_mask.astype(emb_word.dtype)
            h = layer_norm(emb_word[input_ids] + emb_pos[:S][None], emb_ln_s, emb_ln_b)
            L = Wq.shape[0]
            for l in range(L):

                def heads(x):
                    return x.reshape(B, S, NH, dh).transpose(0, 2, 1, 3)
                q = heads(h @ Wq[l] + bq[l])
                k = heads(h @ Wk[l] + bk[l])
                v = heads(h @ Wv[l] + bv[l])
                a = band_attention(q, k, v, mask)
                a = a.transpose(0, 2, 1, 3).reshape(B, S, Hd)
                h = layer_norm(h + a @ Wo[l] + bo[l], ln1_s[l], ln1_b[l])
                f = jax.nn.gelu(h @ W1[l] + b1[l], approximate=False)
                h = layer_norm(h + f @ W2[l] + b2[l], ln2_s[l], ln2_b[l])
            return h
        return _forward(input_ids, attention_mask, emb_word, emb_pos, emb_ln_s, emb_ln_b, Wq, bq, Wk, bk, Wv, bv, Wo, bo, ln1_s, ln1_b, W1, b1, W2, b2, ln2_s, ln2_b)

    def _L0_attn_ref(x, w_q, w_k, w_v, w_o, b_o):
        import jax, jax.numpy as jnp
        import numpy as np
        EMBED_DIM = 192
        NB_HEAD = 12
        HEAD_DIM = EMBED_DIM // NB_HEAD
        B, N, E = x.shape
        H, D = (NB_HEAD, HEAD_DIM)
        q = jnp.einsum('bne,fe->bnf', x, w_q)
        k = jnp.einsum('bne,fe->bnf', x, w_k)
        v = jnp.einsum('bne,fe->bnf', x, w_v)
        q = q.reshape(B, H, N, D)
        k = k.reshape(B, H, N, D)
        v = v.reshape(B, H, N, D)
        dots = jnp.einsum('bhnd,bhmd->bhnm', q, k) / jnp.sqrt(jnp.float32(D))
        attn = jax.nn.softmax(dots, axis=-1)
        out = jnp.einsum('bhnm,bhmd->bhnd', attn, v)
        out = out.transpose(0, 2, 1, 3).reshape(B, N, E)
        out = jnp.einsum('bne,fe->bnf', out, w_o) + b_o
        return out

    def _L0_ffn_ref(x, in_weight, in_bias, out_weight):
        import jax, jax.numpy as jnp
        import numpy as np
        B, S, D_IN, D_HID, D_OUT = (32, 128, 192, 768, 192)
        lead = x.shape[:-1]
        xt = x.reshape(-1, in_weight.shape[1])
        h = jax.nn.gelu(jnp.einsum('td,hd->th', xt, in_weight) + in_bias, approximate=False)
        out = jnp.einsum('th,ho->to', h, out_weight)
        return out.reshape(*lead, out_weight.shape[1])
    h = _L0_tok_ref(x, L0_tok_conv_w, L0_tok_conv_b, L0_tok_pos_table)
    h = jnp.concatenate([h, _L0_txt_ref(x_txt, mask_BS_i1_0, L0_txt_emb_word, L0_txt_emb_pos, L0_txt_emb_ln_s, L0_txt_emb_ln_b, L0_txt_Wq, L0_txt_bq, L0_txt_Wk, L0_txt_bk, L0_txt_Wv, L0_txt_bv, L0_txt_Wo, L0_txt_bo, L0_txt_ln1_s, L0_txt_ln1_b, L0_txt_W1, L0_txt_b1, L0_txt_W2, L0_txt_b2, L0_txt_ln2_s, L0_txt_ln2_b)], axis=1)
    h = h + _L0_attn_ref(_layernorm(h, axis=-1), L0_attn_w_q, L0_attn_w_k, L0_attn_w_v, L0_attn_w_o, L0_attn_b_o)
    h = h + _L0_ffn_ref(_layernorm(h, axis=-1), L0_ffn_in_weight, L0_ffn_in_bias, L0_ffn_out_weight)
    return h

_drawn_inputs = setup_inputs


def setup_inputs(seed=0):
    import zlib

    import numpy as np

    out = dict(_drawn_inputs(seed))
    spreads = {'L0_tok_conv_b': (0.0, 0.1),
     'L0_txt_emb_ln_s': (1.0, 0.2),
     'L0_txt_emb_ln_b': (0.0, 0.1),
     'L0_txt_bq': (0.0, 0.8),
     'L0_txt_bk': (0.0, 0.8),
     'L0_txt_bv': (0.0, 0.1),
     'L0_txt_bo': (0.0, 0.1),
     'L0_txt_ln1_s': (1.0, 0.2),
     'L0_txt_ln1_b': (0.0, 0.1),
     'L0_txt_b1': (0.0, 0.1),
     'L0_txt_b2': (0.0, 0.1),
     'L0_txt_ln2_s': (1.0, 0.2),
     'L0_txt_ln2_b': (0.0, 0.1)}
    factors = {'L0_tok_pos_table': 5.376,
     'L0_txt_Wq': 8.0,
     'L0_txt_Wk': 8.0,
     'L0_attn_w_q': 3.229,
     'L0_attn_w_k': 3.209,
     'L0_ffn_in_bias': 3.496}
    for name, (base, spread) in spreads.items():
        noise = np.random.default_rng([zlib.crc32(name.encode()), seed]).standard_normal(out[name].shape)
        drawn = base * np.exp(spread * noise) if base else spread * noise
        out[name] = jnp.asarray(drawn.astype(out[name].dtype))
    for name, factor in factors.items():
        out[name] = (out[name] * factor).astype(out[name].dtype)
    return out
```

```python
from contextlib import ExitStack

import numpy as np

import concourse.bass as bass
from concourse import mybir

F32 = mybir.dt.float32
I32 = mybir.dt.int32
U32 = mybir.dt.uint32
ALU = mybir.AluOpType
ACT = mybir.ActivationFunctionType
AX_X = mybir.AxisListType.X

B, T, D, H, HD, L, FF = 8, 128, 192, 12, 16, 4, 768
IMG_SIDE, PATCH, CH = 96, 16, 3
NI = (IMG_SIDE // PATCH) ** 2
N = NI + T
NH = N // 2
KT, KD = 2, 96
HG, R, PADH = 3, 4, 32
QKP = HG * R * PADH
FC = FF // 128
PW = CH * PATCH * PATCH
PC = PW // 128
IT, IP = 4, 2 * NI
PAIRS = B // 2
STEPS = L * PAIRS
W = 64
VA = HD + 1
SCALE = 0.25
MASKED = -1e30
PADKEYS = W
EPS_TXT, EPS_JOINT = 1e-12, 1e-5
VOCAB = 8000
J_MLP_AT = 4
TS = 6
JS = 12


def program(nc, a_, out):
    ctx = ExitStack()
    with ctx:
        def sb(name, shape, dt=F32):
            return ctx.enter_context(nc.sbuf_tensor(name, shape, dt))

        def sem(name):
            return ctx.enter_context(nc.semaphore(name))

        def sems(name, n):
            return [sem(f"{name}{i}") for i in range(n)]

        joined = nc.dram_tensor("joined", (B, N, D), F32, kind="Internal").ap()
        qkv_dram = [nc.dram_tensor(f"{n}_dram", (B, N * D), F32, kind="Internal").ap() for n in "qkv"]

        ident = sb("ident", [128, 128])
        ones_row = sb("ones_row", [1, 128])
        neg_half = sb("neg_half", [128, 2])
        eps = sb("eps", [128, 2, 2])
        tick = sb("tick", [128, 1])
        wqkv = sb("wqkv", [KD + 1, KT, 2 * QKP + D])
        wo = sb("wo", [KD + 1, KT, D])
        w1 = sb("w1", [KD + 1, KT, FF])
        w2 = sb("w2", [128, FC, D])
        b2 = sb("b2", [1, D])
        ln1 = sb("ln1", [128, 2, D])
        ln2 = sb("ln2", [128, 2, D])
        jwqkv = sb("jwqkv", [KD, KT, 3 * D])
        jwo = sb("jwo", [KD + 1, KT, D])
        jw1 = sb("jw1", [KD + 1, KT, FF])
        jw2 = sb("jw2", [128, FC, D])

        ids = sb("ids", [T, B], I32)
        ids_low = sb("ids_low", [T, B], I32)
        ids_up = sb("ids_up", [T, B], I32)
        rows = sb("rows", [T, B], I32)
        emb_pos = sb("emb_pos", [T, D])
        emb_ln = sb("emb_ln", [T, 2, D])
        e_stats = sb("e_stats", [T, B, 6])
        e_mv = sb("e_mv", [T, B, 2])
        e_var = sb("e_var", [T, B])
        e_rstd = sb("e_rstd", [T, B])
        mask0 = sb("mask0", [128, B, T])
        mask = sb("mask", [128, STEPS, 2, T])
        conv_b = sb("conv_b", [1, D])
        img_pos = sb("img_pos", [IP, D])
        img = sb("img", [IP, IT, D])

        hid = sb("hid", [128, STEPS + PAIRS, 2, D])
        free = hid[:].rearrange("p s u d -> p (s u d)")

        def borrowed(slot, n):
            return free[:, slot * 2 * D:slot * 2 * D + n]

        words = borrowed(4, B * D).rearrange("p (b d) -> p b d", b=B)
        patches = borrowed(8, PC * IT * IP).rearrange("p (c t) -> p c t", c=PC)
        conv_w = borrowed(13, PC * D).rearrange("p (c d) -> p c d", c=PC)
        key_mask = borrowed(16, B * T).bitcast(I32).rearrange("p (b t) -> p b t", b=B)
        pair_in = sb("pair_in", [128, 2, D])
        hT = sb("hT", [KD + 1, KT, 2 * T])
        qT = sb("qT", [128, HG, 2 * T])
        kbd = sb("kbd", [128, HG, 2, R, T])
        va = sb("va", [128, 2, H, VA])
        ps = [sb(f"ps{i}", [128, R, T]) for i in range(TS)]
        pT = [sb(f"pT{i}", [128, R, T]) for i in range(2)]
        mx = sb("mx", [128, 2, H])
        pad_sum = sb("pad_sum", [128, 2, H])
        den = sb("den", [128, 2, H])
        rden = sb("rden", [128, 2, H])
        att = sb("att", [128, 2, D])
        aT = sb("aT", [KD + 1, KT, 2 * T])
        z1 = sb("z1", [128, 2, D])
        z2 = sb("z2", [128, 2, D])
        n1 = sb("n1", [128, 2, D])
        n2 = sb("n2", [128, 2, D])
        h1 = sb("h1", [128, 2, D])
        h1T = sb("h1T", [KD + 1, KT, 2 * T])
        f = sb("f", [128, FC, 2 * T])
        st = [sb(f"st{i}", [128, 2, 6]) for i in range(2)]
        mv = [sb(f"mv{i}", [128, 2, 2]) for i in range(2)]
        ve = [sb(f"ve{i}", [128, 2]) for i in range(2)]
        rs = [sb(f"rs{i}", [128, 2]) for i in range(2)]

        x = sb("x", [NH, B, 2, D])
        xst = [sb(f"xst{i}", [NH, 2, 6]) for i in range(2)]
        xmv = [sb(f"xmv{i}", [NH, 2, 2]) for i in range(2)]
        xve = [sb(f"xve{i}", [NH, 2]) for i in range(2)]
        xrs = [sb(f"xrs{i}", [NH, 2]) for i in range(2)]
        xn = [sb(f"xn{i}", [NH, 2, D]) for i in range(2)]
        xT = [sb(f"xT{i}", [KD, KT, 2 * NH]) for i in range(2)]
        qkv = [sb(f"qkv{i}", [NH, 2, D]) for i in range(6)]
        qpad = sb("qpad", [NH, 2, H, PADH])
        kpad = sb("kpad", [NH, 2, H, PADH])
        jva = sb("jva", [NH, 2, H, VA])
        jqT = qT[:, :, 0:2 * NH]
        jkbd = sb("jkbd", [128, HG, R, 2 * NH])
        jps = [p_[:].rearrange("p r t -> p (r t)")[0:NH, 0:4 * NH].rearrange("p (r t) -> p r t", r=2) for p_ in ps[0:3]]
        jpT = [p_[:].rearrange("p r t -> p (r t)")[0:NH, 0:4 * NH].rearrange("p (r k t) -> p r k t", r=2, k=2) for p_ in pT]
        jmx = sb("jmx", [NH, JS, 2])
        jrden = sb("jrden", [NH, 2, H])
        jatt = sb("jatt", [NH, 2, D])
        jaT = aT[:, :, 0:2 * NH]
        jz1 = sb("jz1", [NH, 2, D])
        jn1 = sb("jn1", [NH, 2, D])
        jx1T = h1T[:, :, 0:2 * NH]
        jf = f[:, :, 0:2 * NH]
        jout = sb("jout", [NH, 2, D])

        bank = [ctx.enter_context(nc.psum_tensor(f"bank{i}", [128, 512], F32)) for i in range(8)]
        S_BANK, T_BANK, O_BANK, M_BANK = bank[0:2], bank[2:4], bank[4], bank[5:8]

        s_ids, s_embtab, s_mask, s_patches, s_conv, s_const = (sem(f"s_{n}_loaded") for n in (
            "ids", "embtab", "mask", "patches", "conv", "const"))
        s_jw = sem("s_joint_weights_loaded")
        s_words = sems("s_words_loaded", PAIRS)
        dma_w = {n: sem(f"s_dma_{n}") for n in ("wqkv", "wo", "ln1", "w1", "w2", "ln2")}
        ok_w = {n: sem(f"s_ok_{n}") for n in ("wqkv", "wo", "ln1", "w1", "w2", "ln2")}
        s_ident, s_vset, s_pset = sem("s_ident"), sem("s_vector_constants"), sem("s_pool_constants")
        s_ids_step, s_rows = sem("s_ids_step"), sem("s_rows_ready")
        s_e = sems("s_embedding_step", 5)
        s_img_ps = sems("s_img_psum", 2)
        s_evar, s_erstd = sem("s_evar"), sem("s_erstd")
        s_mask0, s_band, s_mask_ok = sem("s_mask0"), sem("s_band"), sem("s_mask_ready")
        s_img = [sem(f"s_img_ready{i}") for i in range(2)]
        s_img_out, s_img_stored = sem("s_img_out"), sem("s_img_stored")
        s_hid = sem("s_hid_ready")
        s_pair_in, s_hT_ps, s_hT = sem("s_pair_in"), sem("s_hT_psum"), sem("s_hT")
        s_qk_ps, s_qk_dve, s_qk_act = sem("s_qk_psum"), sem("s_qk_by_vector"), sem("s_qk_by_scalar")

        def qk(s, hg):
            return HG * s + hg + 1

        s_v_ps, s_va = sem("s_v_psum"), sem("s_va")
        s_score, s_masked, s_max, s_centred, s_prob, s_pT_ps, s_pT, s_pv = (sem(f"s_{n}") for n in (
            "score", "masked", "max", "centred", "prob", "pT_psum", "pT", "pv"))

        def group(s, i):
            return TS * s + i + 1
        s_norm = sems("s_norm", 3)
        s_att, s_aT_ps, s_aT, s_wo_ps = sem("s_att"), sem("s_aT_psum"), sem("s_aT"), sem("s_wo_psum")
        s_z = sems("s_z", 2)
        s_st, s_mv, s_ve, s_rs = sems("s_stats", 2), sems("s_mean_var", 2), sems("s_var_eps", 2), sems("s_rstd", 2)
        s_nrm, s_scl = sems("s_normed", 2), sems("s_scaled", 2)
        s_h1, s_h1T_ps, s_h1T = sem("s_h1"), sem("s_h1T_psum"), sem("s_h1T")
        s_up, s_gelu, s_down = sems("s_up_psum", 3), sems("s_gelu", 3), sem("s_down_psum")
        s_x = sem("s_x_loaded")
        s_xn, s_xT_ps, s_xT = sems("s_xn", 2), sems("s_xT_psum", 2), sems("s_xT", 2)
        s_xst, s_xmv, s_xve, s_xrs = sems("s_xst", 2), sems("s_xmv", 2), sems("s_xve", 2), sems("s_xrs", 2)
        s_qkv_ps, s_qkv_sb = sem("s_qkv_psum"), sem("s_qkv_sbuf")

        def sixth(n, i):
            return 6 * n + i + 1

        s_qkv_stored = sems("s_qkv_stored", 6)
        s_heads = [sem(f"s_{n}_heads_loaded") for n in "qkv"]
        s_stored = sem("s_result_stored")


        j_qT_ps, j_qT, j_kT_ps, j_kdve, j_kact = (sem(f"j_{n}") for n in ("qT_ps", "qT", "kT_ps", "k_by_vector", "k_by_scalar"))
        j_score, j_max, j_centred, j_prob_s, j_pT_ps, j_pT, j_pv = (sem(f"j_{n}") for n in (
            "score", "max", "centred", "prob", "pT_ps", "pT", "pv"))

        def nth(b, i):
            return JS * b + i + 1

        j_rden, j_att, j_aT_ps, j_aT, j_wo_ps = (sem(f"j_{n}") for n in ("rden", "att", "aT_ps", "aT", "wo_ps"))
        j_z1, j_st, j_mv, j_ve, j_rs, j_n1 = (sem(f"j_{n}") for n in ("z1", "stats", "mean_var", "var_eps", "rstd", "n1"))
        j_x1T_ps, j_x1T, j_down = (sem(f"j_{n}") for n in ("x1T_ps", "x1T", "down"))
        j_out = sem("j_out")
        j_up, j_gelu = sems("j_up", 2), sems("j_gelu", 2)

        block = ctx.enter_context(nc.Block())

        @block.sync
        def _(sp):
            sp.dma_start(ids[:], a_["ids"]).then_inc(s_ids, 16)
            sp.dma_start(ident[:], a_["ident"]).then_inc(s_ident, 16)
            sp.dma_start(patches, a_["patches"].rearrange("(c p) t -> p c t", p=128)).then_inc(s_patches, 16)
            sp.dma_start(conv_w, a_["conv_w"].rearrange("(c p) t -> p c t", p=128)).then_inc(s_conv, 16)
            sp.dma_start(conv_b[:], a_["conv_b"]).then_inc(s_conv, 16)
            sp.dma_start(img_pos[:], a_["img_pos"]).then_inc(s_conv, 16)
            sp.dma_start(emb_pos[:], a_["emb_pos"]).then_inc(s_embtab, 16)
            sp.dma_start(emb_ln[:], a_["emb_ln"].partition_broadcast(T)).then_inc(s_embtab, 16)
            sp.dma_start(key_mask, a_["mask"].partition_broadcast(128)).then_inc(s_mask, 16)

            weights = (("wqkv", s_v_ps), ("wo", s_wo_ps), ("ln1", s_h1), ("w1", s_up[2]), ("w2", s_down), ("ln2", s_hid))

            def load(name, l):
                if name == "w2":
                    sp.dma_start(w2[:], a_["w2"][bass.ds(l, 1)].rearrange("o (c p) d -> p (o c) d", p=128)).then_inc(dma_w[name], 16)
                    sp.dma_start(b2[:], a_["b2"][bass.ds(l, 1), :]).then_inc(dma_w[name], 16)
                elif name in ("ln1", "ln2"):
                    src = a_[name][bass.ds(l, 1)].rearrange("o a d -> (o a) d").partition_broadcast(128)
                    sp.dma_start({"ln1": ln1, "ln2": ln2}[name][:], src).then_inc(dma_w[name], 16)
                else:
                    dst = {"wqkv": wqkv, "wo": wo, "w1": w1}[name]
                    sp.dma_start(dst[:], a_[name][bass.ds(l, 1)].rearrange("o p k d -> (o p) k d")).then_inc(dma_w[name], 16)

            for name, _ in weights:
                load(name, 0)
            for name, _ in weights:
                sp.wait_ge(dma_w[name], 32 if name == "w2" else 16)
                sp.sem_inc(ok_w[name], PAIRS)
            sp.dma_start(jwqkv[:], a_["jwqkv"]).then_inc(s_jw, 16)
            sp.dma_start(jwo[:], a_["jwo"]).then_inc(s_jw, 16)
            sp.dma_start(jw1[:], a_["jw1"]).then_inc(s_jw, 16)
            sp.dma_start(jw2[:], a_["jw2"].rearrange("(c p) d -> p c d", p=128)).then_inc(s_jw, 16)
            sp.wait_ge(s_img[0], 1)
            sp.wait_ge(s_img[1], 1)
            batch_of = joined.rearrange("(t u) n d -> u n t d", u=2)
            for u in range(2):
                sp.dma_start(batch_of[u, 0:NI], img[u * NI:(u + 1) * NI, :, :]).then_inc(s_img_stored, 16)
            with sp.Fori(1, L) as l:
                for name, last_use in weights:
                    sp.wait_ge(last_use, PAIRS * l + (PAIRS if name == "ln2" else 0))
                    load(name, l)
                    sp.wait_ge(dma_w[name], (l + 1) * (32 if name == "w2" else 16))
                    sp.sem_inc(ok_w[name], PAIRS)

            sp.wait_ge(s_hid, STEPS + PAIRS)
            for b in range(B):
                sp.dma_start(joined[b, NI:N], hid[:, STEPS + b // 2, b % 2, :]).then_inc(s_img_stored, 16)
            sp.wait_ge(s_img_stored, 16 * (2 + B))
            for b in range(B):
                sp.dma_start(x[:, b], joined[b].rearrange("(h p) d -> p h d", h=2)).then_inc(s_x, 16)

            with sp.Fori(0, PAIRS) as g:
                for u in range(2):
                    for j in range(3):
                        sp.wait_ge(s_qkv_sb, sixth(g, 3 * u + j))
                        sp.dma_start(qkv_dram[j][bass.ds(2 * g + u, 1), :].rearrange("o (h p d) -> p (o h) d", h=2, d=D),
                                     qkv[3 * u + j][:]).then_inc(s_qkv_stored[3 * u + j], 16)
            for i in range(6):
                sp.wait_ge(s_qkv_stored[i], 16 * PAIRS)

            def load_heads(b):
                for j, dst in enumerate((qpad, kpad, jva)):
                    src = qkv_dram[j][bass.ds(b, 1), :].rearrange("o (h u p d) -> u p (o h) d", h=H, u=2, d=HD)
                    for u in range(2):
                        sp.dma_start(dst[:, u, :, 0:HD], src[u]).then_inc(s_heads[j], 16)

            sp.wait_ge(s_pset, 1)
            load_heads(0)
            with sp.Fori(1, B) as b:
                sp.wait_ge(j_pv, JS * b)
                sp.wait_ge(j_qT_ps, b)
                sp.wait_ge(j_kT_ps, b)
                load_heads(b)

        @block.gpsimd
        def _(pool):
            g = nc.gpsimd
            pool.wait_ge(s_rows, 1)
            for b in range(B):
                g.indirect_dma_start(words[:, b, :], None, a_["emb_word"],
                                     bass.IndirectOffsetOnAxis(ap=rows[:, b:b + 1].bitcast(U32), axis=0)
                                     ).then_inc(s_words[b // 2], 16)
            g.memset(kbd[:], 0.0)
            g.memset(eps[:, 0, :], EPS_TXT)
            g.memset(eps[:, 1, :], EPS_JOINT)
            g.memset(neg_half[:], -0.5).then_inc(s_pset, 1)
            pool.wait_ge(s_pset, 1)
            pool.wait_ge(s_mask0, 1)
            g.affine_select(out=mask0[:], in_=mask0[:], pattern=[[0, B], [-1, T]], compare_op=ALU.is_ge,
                            fill=MASKED, base=W, channel_multiplier=1).then_inc(s_band, 1)
            pool.wait_ge(s_band, 1)
            g.affine_select(out=mask0[:], in_=mask0[:], pattern=[[0, B], [1, T]], compare_op=ALU.is_ge,
                            fill=MASKED, base=W, channel_multiplier=-1).then_inc(s_band, 1)
            for p in range(PAIRS):
                pool.wait_ge(s_e[2], p + 1)
                g.tensor_scalar(e_var[:, 2 * p:2 * p + 2], e_mv[:, 2 * p:2 * p + 2, 1], EPS_TXT, None, ALU.add).then_inc(s_evar, 1)
                pool.wait_ge(s_evar, p + 1)
                g.tensor_tensor(e_rstd[:, 2 * p:2 * p + 2], e_var[:, 2 * p:2 * p + 2], neg_half[:, 0:2], ALU.pow).then_inc(s_erstd, 1)
            g.memset(qpad[:], 0.0)
            g.memset(kpad[:], 0.0)
            g.memset(jva[:], 1.0)
            g.memset(jkbd[:], 0.0).then_inc(s_pset, 1)

            def stage(s):
                pool.wait_ge(s_hid, s + 1)
                if not isinstance(s, int) or s > 0:
                    pool.wait_ge(s_hT_ps, s)
                g.tensor_copy(pair_in[:], hid[:, bass.ds(s, 1), :, :].rearrange("p o u d -> p (o u) d")).then_inc(s_pair_in, 1)

            def rstd(which, done):
                pool.wait_ge(s_mv[which], done)
                g.tensor_tensor(ve[which][:], mv[which][:, :, 1], eps[:, 0, :], ALU.add).then_inc(s_ve[which], 1)
                pool.wait_ge(s_ve[which], done)
                g.tensor_tensor(rs[which][:], ve[which][:], neg_half[:, 0:2], ALU.pow).then_inc(s_rs[which], 1)

            def centre_steps(s, lo, hi):
                for i in range(lo, hi):
                    u, hg = i // HG, i % HG
                    pool.wait_ge(s_max, group(s, i))
                    m = mx[:, u, R * hg:R * hg + R].unsqueeze(2).to_broadcast([128, R, T])
                    g.tensor_tensor(ps[i][:], ps[i][:], m, ALU.subtract).then_inc(s_centred, 1)

            stage(0)
            centre_steps(0, 0, TS)
            with pool.Fori(1, STEPS) as s:
                stage(s)
                rstd(0, s)
                centre_steps(s, 0, 3)
                rstd(1, s)
                centre_steps(s, 3, TS)
            rstd(0, STEPS)
            rstd(1, STEPS)

            with pool.Fori(0, PAIRS) as p:
                for u in range(2):
                    pool.wait_ge(s_xmv[u], p + 1)
                    g.tensor_tensor(xve[u][:], xmv[u][:, :, 1], eps[0:NH, 1, :], ALU.add).then_inc(s_xve[u], 1)
                    pool.wait_ge(s_xve[u], p + 1)
                    g.tensor_tensor(xrs[u][:], xve[u][:], neg_half[0:NH, 0:2], ALU.pow).then_inc(s_xrs[u], 1)

            with pool.Fori(0, B) as b:
                pool.wait_ge(j_mv, b + 1)
                g.tensor_tensor(xve[0][:], xmv[0][:, :, 1], eps[0:NH, 1, :], ALU.add).then_inc(j_ve, 1)
                pool.wait_ge(j_ve, b + 1)
                g.tensor_tensor(xrs[0][:], xve[0][:], neg_half[0:NH, 0:2], ALU.pow).then_inc(j_rs, 1)
                pool.wait_ge(j_out, b + 2)
                g.dma_start(out[bass.ds(b, 1)].rearrange("o (h p) d -> p (o h) d", h=2), jout[:]).then_inc(s_stored, 16)
            pool.wait_ge(s_stored, 16 * B)

        @block.scalar
        def _(act):
            a = nc.scalar

            def copies(s, first):
                for hg in range(HG):
                    act.wait_ge(s_qk_ps, qk(s, hg))
                    if not first:
                        act.wait_ge(s_score, group(s - 1, HG + hg))
                    ps_ = M_BANK[hg % 3]
                    a.activation(qT[64:128, hg, :], ps_[64:128, 0:2 * T], ACT.Copy)
                    for r in (2, 3):
                        rows_ = slice(PADH * r, PADH * r + PADH)
                        i = a.activation(kbd[rows_, hg, :, r, :], ps_[rows_, 2 * T:4 * T].rearrange("p (u t) -> p u t", u=2), ACT.Copy)
                    i.then_inc(s_qk_act, 1)
                act.wait_ge(s_v_ps, s + 1)
                if not first:
                    act.wait_ge(s_pv, group(s - 1, TS - 1))
                a.activation(va[:, :, :, 0:HD], M_BANK[0][:, 0:2 * D].rearrange("p (u h d) -> p u h d", u=2, h=H), ACT.Copy).then_inc(s_va, 1)

            def transposed_attention(y, first):
                act.wait_ge(s_aT_ps, y + 1)
                if not first:
                    act.wait_ge(s_wo_ps, y)
                a.activation(aT[0:KD, :, :], M_BANK[1][0:KD, :].rearrange("p (k t) -> p k t", k=KT), ACT.Copy).then_inc(s_aT, 1)

            def gelus(y, first):
                for c in range(3):
                    act.wait_ge(s_up[c], y + 1)
                    if c == 0 and not first:
                        act.wait_ge(s_down, y)
                    a.activation(f[:, 2 * c:2 * c + 2, :], M_BANK[(2 + c) % 3][:, :].rearrange("p (c t) -> p c t", c=2), ACT.Gelu).then_inc(s_gelu[c], 1)

            def prob(s, i):
                act.wait_ge(s_centred, group(s, i))
                a.activation(ps[i][:], ps[i][:], ACT.Exp, scale=SCALE).then_inc(s_prob, 1)

            def prob_T(s, i, first):
                act.wait_ge(s_pT_ps, group(s, i))
                if i >= 2:
                    act.wait_ge(s_pv, group(s, i - 2))
                elif not first:
                    act.wait_ge(s_pv, group(s - 1, i + TS - 2))
                a.activation(pT[i % 2][:], T_BANK[i % 2][:, :].rearrange("p (r t) -> p r t", r=R), ACT.Copy).then_inc(s_pT, 1)

            def probs(s, first):
                prob(s, 0)
                for i in range(TS):
                    if i + 1 < TS:
                        prob(s, i + 1)
                    prob_T(s, i, first)

            act.wait_ge(s_vset, 1)
            act.wait_ge(s_pset, 1)
            copies(0, True)
            probs(0, True)
            transposed_attention(0, True)
            copies(1, False)
            gelus(0, True)
            probs(1, False)
            with act.Fori(2, STEPS) as s:
                transposed_attention(s - 1, False)
                copies(s, False)
                gelus(s - 1, False)
                probs(s, False)
            transposed_attention(STEPS - 1, False)
            gelus(STEPS - 1, False)

            def qkv_out(p, first):
                for i in range(6):
                    act.wait_ge(s_qkv_ps, sixth(p, i))
                    if not first:
                        act.wait_ge(s_qkv_stored[i], 16 * p)
                    a.activation(qkv[i][:], bank[2 + i][0:NH, 0:2 * D].rearrange("p (h d) -> p h d", h=2), ACT.Copy).then_inc(s_qkv_sb, 1)

            qkv_out(0, True)
            with act.Fori(1, PAIRS) as p:
                qkv_out(p, False)

            def j_transposed_attention(y, first):
                act.wait_ge(j_aT_ps, y + 1)
                if not first:
                    act.wait_ge(j_wo_ps, y)
                a.activation(jaT[0:KD, :, :], M_BANK[2][0:KD, 0:4 * NH].rearrange("p (k t) -> p k t", k=KT), ACT.Copy).then_inc(j_aT, 1)

            def j_copies(b, first):
                act.wait_ge(j_kT_ps, b + 1)
                if not first:
                    act.wait_ge(j_score, nth(b - 1, JS - 1))
                for r in (2, 3):
                    rows_ = slice(PADH * r, PADH * r + PADH)
                    i = a.activation(jkbd[rows_, :, r, :], M_BANK[1][rows_, 0:HG * 2 * NH].rearrange("p (g t) -> p g t", g=HG), ACT.Copy)
                i.then_inc(j_kact, 1)

            def j_prob(b, i):
                act.wait_ge(j_centred, nth(b, i))
                a.activation(jps[i % 3], jps[i % 3], ACT.Exp, scale=SCALE).then_inc(j_prob_s, 1)

            def j_prob_T(b, i, first):
                act.wait_ge(j_pT_ps, nth(b, i))
                if i >= 2 or not first:
                    act.wait_ge(j_pv, JS * b + i - 1)
                a.activation(jpT[i % 2], T_BANK[i % 2][0:NH, 0:4 * NH].rearrange("p (r k t) -> p r k t", r=2, k=2), ACT.Copy).then_inc(j_pT, 1)

            def j_gelus(y, first):
                for c in range(2):
                    act.wait_ge(j_up[c], y + 1)
                    if c == 0 and not first:
                        act.wait_ge(j_down, y)
                    a.activation(jf[:, 3 * c:3 * c + 3, :], M_BANK[(2, 0)[c]][:, 0:6 * NH].rearrange("p (c t) -> p c t", c=3), ACT.Gelu).then_inc(j_gelu[c], 1)

            def j_step(b, first, second=False):
                if not first:
                    j_transposed_attention(b - 1, second)
                j_copies(b, first)
                j_prob(b, 0)
                for i in range(JS):
                    if i == J_MLP_AT and not first:
                        j_gelus(b - 1, second)
                    if i + 1 < JS:
                        j_prob(b, i + 1)
                    j_prob_T(b, i, first)

            j_step(0, True)
            j_step(1, False, True)
            with act.Fori(2, B) as b:
                j_step(b, False)
            j_transposed_attention(B - 1, False)
            j_gelus(B - 1, False)

        @block.vector
        def _(dve):
            v = nc.vector
            v.memset(ones_row[:], 1.0).then_inc(s_z[1], 1)
            v.memset(tick[:], 0.0).then_inc(j_out, 1)
            v.memset(va[:, :, :, HD:VA], 1.0)
            for t_ in (hT, aT, h1T):
                i = v.memset(t_[KD:KD + 1, :, :], 1.0)
            i.then_inc(s_vset, 1)
            dve.wait_ge(s_ids, 16)
            v.tensor_scalar(ids_low[:], ids[:], 0, VOCAB, ALU.is_lt, ALU.mult).then_inc(s_ids_step, 1)
            dve.wait_ge(s_ids_step, 1)
            v.tensor_tensor(ids_up[:], ids[:], ids_low[:], ALU.add).then_inc(s_ids_step, 1)
            dve.wait_ge(s_ids_step, 2)
            v.tensor_scalar(rows[:], ids_up[:], VOCAB - 1, 0, ALU.min, ALU.max).then_inc(s_rows, 1)
            dve.wait_ge(s_mask, 16)
            v.tensor_scalar(mask0[:], key_mask, 0, MASKED, ALU.is_le, ALU.mult).then_inc(s_mask0, 1)
            dve.wait_ge(s_embtab, 32)
            for p in range(PAIRS):
                two = slice(2 * p, 2 * p + 2)
                dve.wait_ge(s_words[p], 32)
                v.tensor_tensor(words[:, two, :], words[:, two, :], emb_pos[:].unsqueeze(1).to_broadcast([T, 2, D]), ALU.add).then_inc(s_e[0], 1)
                dve.wait_ge(s_e[0], p + 1)
                for b in (2 * p, 2 * p + 1):
                    i = v.bn_stats(e_stats[:, b, :], words[:, b, :])
                i.then_inc(s_e[1], 1)
                dve.wait_ge(s_e[1], p + 1)
                for b in (2 * p, 2 * p + 1):
                    i = v.bn_aggr(e_mv[:, b, :], e_stats[:, b, :])
                i.then_inc(s_e[2], 1)
                dve.wait_ge(s_e[2], p + 1)
                dve.wait_ge(s_erstd, p + 1)
                for b in (2 * p, 2 * p + 1):
                    i = v.tensor_scalar(words[:, b, :], words[:, b, :], e_mv[:, b, 0:1], e_rstd[:, b:b + 1], ALU.subtract, ALU.mult)
                i.then_inc(s_e[3], 1)
                dve.wait_ge(s_e[3], p + 1)
                v.tensor_tensor(words[:, two, :], words[:, two, :], emb_ln[:, 0:1, :].to_broadcast([T, 2, D]), ALU.mult).then_inc(s_e[4], 1)
                dve.wait_ge(s_e[4], p + 1)
                v.tensor_tensor(hid[:, p, :, :], words[:, two, :], emb_ln[:, 1:2, :].to_broadcast([T, 2, D]), ALU.add).then_inc(s_hid, 1)
            dve.wait_ge(s_band, 2)
            v.tensor_copy(mask[:].rearrange("p (l q) u t -> p l (q u) t", l=L), mask0[:].unsqueeze(1).to_broadcast([128, L, B, T])).then_inc(s_mask_ok, 1)
            dve.wait_ge(s_mask_ok, 1)
            dve.wait_ge(s_conv, 48)
            for c in range(2):
                dve.wait_ge(s_img_ps[c], 1)
                v.tensor_tensor(img[:, 2 * c:2 * c + 2, :], bank[c][0:IP, 0:2 * D].rearrange("p (c d) -> p c d", c=2),
                                img_pos[:].unsqueeze(1).to_broadcast([IP, 2, D]), ALU.add).then_inc(s_img[c], 1)

            def hT_copy(s, first):
                dve.wait_ge(s_hT_ps, s + 1)
                if not first:
                    dve.wait_ge(s_v_ps, s)
                v.tensor_copy(hT[0:KD, :, :], M_BANK[0][0:KD, :].rearrange("p (k t) -> p k t", k=KT)).then_inc(s_hT, 1)

            def qk_copy(s, hg, first):
                dve.wait_ge(s_qk_ps, qk(s, hg))
                if not first:
                    dve.wait_ge(s_score, group(s - 1, HG + hg))
                ps_ = M_BANK[hg % 3]
                v.tensor_copy(qT[0:64, hg, :], ps_[0:64, 0:2 * T])
                for r in (0, 1):
                    rows_ = slice(PADH * r, PADH * r + PADH)
                    i = v.tensor_copy(kbd[rows_, hg, :, r, :], ps_[rows_, 2 * T:4 * T].rearrange("p (u t) -> p u t", u=2))
                i.then_inc(s_qk_dve, 1)

            def mask_and_max(s, i, first):
                u, hg = i // HG, i % HG
                dve.wait_ge(s_score, group(s, i))
                if not first:
                    dve.wait_ge(s_pT_ps, group(s - 1, i))
                m = mask[:, bass.ds(s, 1), u, :].to_broadcast([128, R, T])
                v.tensor_tensor(ps[i][:], S_BANK[i % 2][:, :].rearrange("p (r t) -> p r t", r=R), m, ALU.add).then_inc(s_masked, 1)
                dve.wait_ge(s_masked, group(s, i))
                v.tensor_reduce(mx[:, u, R * hg:R * hg + R], ps[i][:], AX_X, ALU.max).then_inc(s_max, 1)

            def normalise(s, first):
                dve.wait_ge(s_max, group(s, TS - 1))
                v.tensor_scalar(pad_sum[:], mx[:], 0.5 * MASKED, float(PADKEYS), ALU.is_lt, ALU.mult).then_inc(s_norm[0], 1)
                dve.wait_ge(s_norm[0], s + 1)
                dve.wait_ge(s_pv, group(s, TS - 1))
                o = O_BANK[:, 0:2 * H * VA].rearrange("p (u h d) -> p u h d", u=2, h=H)
                v.tensor_tensor(den[:], o[:, :, :, HD], pad_sum[:], ALU.add).then_inc(s_norm[1], 1)
                dve.wait_ge(s_norm[1], s + 1)
                v.reciprocal(rden[:], den[:]).then_inc(s_norm[2], 1)
                dve.wait_ge(s_norm[2], s + 1)
                if not first:
                    dve.wait_ge(s_aT_ps, s)
                v.tensor_tensor(att[:].rearrange("p u (h d) -> p (u h) d", h=H),
                                O_BANK[:, 0:2 * H * VA].rearrange("p (u h d) -> p (u h) d", u=2, h=H)[:, :, 0:HD],
                                rden[:].rearrange("p u h -> p (u h)").unsqueeze(2).to_broadcast([128, 2 * H, HD]), ALU.mult).then_inc(s_att, 1)

            def residual_stats(w, y, ps_, other):
                z = (z1, z2)[w]
                i = v.tensor_tensor(z[:], ps_[:, 0:2 * D].rearrange("p (u d) -> p u d", u=2), other, ALU.add)
                i.then_inc(s_z[w], 1)
                dve.wait_ge(s_z[w], y + 1 + w)
                for u in range(2):
                    i = v.bn_stats(st[w][:, u, :], z[:, u, :])
                i.then_inc(s_st[w], 1)
                dve.wait_ge(s_st[w], y + 1)
                v.memset(tick[:], 0.0)
                for u in range(2):
                    i = v.bn_aggr(mv[w][:, u, :], st[w][:, u, :])
                i.then_inc(s_mv[w], 1)

            def norm_apply(w, y, ln, dst, done):
                z, n_ = (z1, z2)[w], (n1, n2)[w]
                dve.wait_ge(s_mv[w], y + 1)
                dve.wait_ge(s_rs[w], y + 1)
                for u in range(2):
                    i = v.tensor_scalar(n_[:, u, :], z[:, u, :], mv[w][:, u, 0:1], rs[w][:, u:u + 1], ALU.subtract, ALU.mult)
                i.then_inc(s_nrm[w], 1)
                dve.wait_ge(s_nrm[w], y + 1)
                dve.wait_ge(ok_w[("ln1", "ln2")[w]], y + 1)
                v.tensor_tensor(n_[:], n_[:], ln[:, 0:1, :].to_broadcast([128, 2, D]), ALU.mult).then_inc(s_scl[w], 1)
                dve.wait_ge(s_scl[w], y + 1)
                v.tensor_tensor(dst, n_[:], ln[:, 1:2, :].to_broadcast([128, 2, D]), ALU.add).then_inc(done, 1)

            def first_sum(y):
                dve.wait_ge(s_wo_ps, y + 1)
                residual_stats(0, y, M_BANK[2], hid[:, bass.ds(y, 1), :, :].rearrange("p o u d -> p (o u) d"))

            def first_norm(y, first):
                if not first:
                    dve.wait_ge(s_h1T_ps, y)
                norm_apply(0, y, ln1, h1[:], s_h1)

            def h1T_copy(y, first):
                dve.wait_ge(s_h1T_ps, y + 1)
                if not first:
                    dve.wait_ge(s_up[2], y)
                v.tensor_copy(h1T[0:KD, :, :], M_BANK[1][0:KD, :].rearrange("p (k t) -> p k t", k=KT)).then_inc(s_h1T, 1)

            def second_sum(y):
                dve.wait_ge(s_down, y + 1)
                dve.wait_ge(s_h1, y + 1)
                residual_stats(1, y, M_BANK[2], h1[:])

            def second_norm(y):
                norm_apply(1, y, ln2, hid[:, bass.ds(y + PAIRS, 1), :, :].rearrange("p o u d -> p (o u) d"), s_hid)

            def step(s, first, second=False):
                hT_copy(s, first)
                if not first:
                    first_sum(s - 1)
                qk_copy(s, 0, first)
                if not first:
                    first_norm(s - 1, second)
                qk_copy(s, 1, first)
                qk_copy(s, 2, first)
                if not first:
                    h1T_copy(s - 1, second)
                for i in range(TS):
                    if i == 3 and not first:
                        second_sum(s - 1)
                    if i == 4 and not first:
                        second_norm(s - 1)
                    mask_and_max(s, i, first)
                normalise(s, first)

            step(0, True)
            step(1, False, True)
            with dve.Fori(2, STEPS) as s:
                step(s, False)
            first_sum(STEPS - 1)
            first_norm(STEPS - 1, False)
            h1T_copy(STEPS - 1, False)
            second_sum(STEPS - 1)
            second_norm(STEPS - 1)

            dve.wait_ge(s_x, 16 * B)

            def x_stats(u, b, n):
                for h in range(2):
                    i = v.bn_stats(xst[u][:, h, :], x[:, bass.ds(b, 1), h, :].rearrange("p o d -> p (o d)"))
                i.then_inc(s_xst[u], 1)
                dve.wait_ge(s_xst[u], n + 1)
                v.memset(tick[:], 0.0)
                for h in range(2):
                    i = v.bn_aggr(xmv[u][:, h, :], xst[u][:, h, :])
                i.then_inc(s_xmv[u], 1)

            def x_apply(u, b, n, first):
                dve.wait_ge(s_xmv[u], n + 1)
                dve.wait_ge(s_xrs[u], n + 1)
                if not first:
                    dve.wait_ge(s_xT_ps[u], n)
                for h in range(2):
                    i = v.tensor_scalar(xn[u][:, h, :], x[:, bass.ds(b, 1), h, :].rearrange("p o d -> p (o d)"),
                                        xmv[u][:, h, 0:1], xrs[u][:, h:h + 1], ALU.subtract, ALU.mult)
                i.then_inc(s_xn[u], 1)

            def x_T(u, n, first):
                dve.wait_ge(s_xT_ps[u], n + 1)
                if not first:
                    dve.wait_ge(s_qkv_ps, sixth(n - 1, 3 * u + 2))
                v.tensor_copy(xT[u][:], bank[u][0:KD, 0:4 * NH].rearrange("p (k t) -> p k t", k=KT)).then_inc(s_xT[u], 1)

            def x_pair(n, first):
                for u in range(2):
                    x_stats(u, 2 * n + u, n)
                for u in range(2):
                    x_apply(u, 2 * n + u, n, first)
                for u in range(2):
                    x_T(u, n, first)

            x_pair(0, True)
            with dve.Fori(1, PAIRS) as n:
                x_pair(n, False)

            def j_q_copy(b, first):
                dve.wait_ge(j_qT_ps, b + 1)
                if not first:
                    dve.wait_ge(j_score, nth(b - 1, JS - 1))
                v.tensor_copy(jqT, M_BANK[0][:, 0:HG * 2 * NH].rearrange("p (g t) -> p g t", g=HG)).then_inc(j_qT, 1)

            def j_k_copy(b):
                dve.wait_ge(j_kT_ps, b + 1)
                for r in (0, 1):
                    rows_ = slice(PADH * r, PADH * r + PADH)
                    i = v.tensor_copy(jkbd[rows_, :, r, :], M_BANK[1][rows_, 0:HG * 2 * NH].rearrange("p (g t) -> p g t", g=HG))
                i.then_inc(j_kdve, 1)

            def j_centre(b, i, first):
                dve.wait_ge(j_score, nth(b, i))
                s_ = S_BANK[i % 2][0:NH, 0:4 * NH].rearrange("p (r t) -> p r t", r=2)
                v.tensor_reduce(jmx[:, i, :], s_, AX_X, ALU.max).then_inc(j_max, 1)
                dve.wait_ge(j_max, JS * b + i + 1)
                if i >= 3:
                    dve.wait_ge(j_pT_ps, nth(b, i - 3))
                elif not first:
                    dve.wait_ge(j_pT_ps, nth(b - 1, i + JS - 3))
                v.tensor_tensor(jps[i % 3], s_, jmx[:, i, :].unsqueeze(2).to_broadcast([NH, 2, 2 * NH]), ALU.subtract).then_inc(j_centred, 1)

            def j_normalise(b, first):
                dve.wait_ge(j_pv, JS * (b + 1))
                o = O_BANK[0:NH, 0:2 * H * VA].rearrange("p (u h d) -> p u h d", u=2, h=H)
                v.reciprocal(jrden[:], o[:, :, :, HD]).then_inc(j_rden, 1)
                dve.wait_ge(j_rden, b + 1)
                if not first:
                    dve.wait_ge(j_aT_ps, b)
                v.tensor_tensor(jatt[:].rearrange("p u (h d) -> p (u h) d", h=H),
                                O_BANK[0:NH, 0:2 * H * VA].rearrange("p (u h d) -> p (u h) d", u=2, h=H)[:, :, 0:HD],
                                jrden[:].rearrange("p u h -> p (u h)").unsqueeze(2).to_broadcast([NH, 2 * H, HD]), ALU.mult).then_inc(j_att, 1)

            def j_first_sum(y):
                dve.wait_ge(j_wo_ps, y + 1)
                v.tensor_tensor(jz1[:], M_BANK[0][0:NH, 0:2 * D].rearrange("p (h d) -> p h d", h=2),
                                x[:, bass.ds(y, 1), :, :].rearrange("p o h d -> p (o h) d"), ALU.add).then_inc(j_z1, 1)
                dve.wait_ge(j_z1, y + 1)
                for h in range(2):
                    i = v.bn_stats(xst[0][:, h, :], jz1[:, h, :])
                i.then_inc(j_st, 1)
                dve.wait_ge(j_st, y + 1)
                v.memset(tick[:], 0.0)
                for h in range(2):
                    i = v.bn_aggr(xmv[0][:, h, :], xst[0][:, h, :])
                i.then_inc(j_mv, 1)

            def j_norm(y, first):
                dve.wait_ge(j_mv, y + 1)
                dve.wait_ge(j_rs, y + 1)
                if not first:
                    dve.wait_ge(j_x1T_ps, y)
                for h in range(2):
                    i = v.tensor_scalar(jn1[:, h, :], jz1[:, h, :], xmv[0][:, h, 0:1], xrs[0][:, h:h + 1], ALU.subtract, ALU.mult)
                i.then_inc(j_n1, 1)

            def j_x1T_copy(y, first):
                dve.wait_ge(j_x1T_ps, y + 1)
                if not first:
                    dve.wait_ge(j_up[1], y)
                v.tensor_copy(jx1T[0:KD, :, :], M_BANK[1][0:KD, 0:4 * NH].rearrange("p (k t) -> p k t", k=KT)).then_inc(j_x1T, 1)

            def j_second_sum(y, first):
                dve.wait_ge(j_down, y + 1)
                if not first:
                    dve.wait_ge(s_stored, 16 * y)
                v.tensor_tensor(jout[:], M_BANK[1][0:NH, 0:2 * D].rearrange("p (h d) -> p h d", h=2), jz1[:], ALU.add).then_inc(j_out, 1)

            def j_step(b, first, second=False):
                j_q_copy(b, first)
                if not first:
                    j_first_sum(b - 1)
                j_k_copy(b)
                for i in range(JS):
                    if i == 2 and not first:
                        j_norm(b - 1, second)
                    if i == J_MLP_AT and not first:
                        j_x1T_copy(b - 1, second)
                    if i == J_MLP_AT + 3 and not first:
                        j_second_sum(b - 1, second)
                    j_centre(b, i, first)
                j_normalise(b, first)

            j_step(0, True)
            j_step(1, False, True)
            with dve.Fori(2, B) as b:
                j_step(b, False)
            j_first_sum(B - 1)
            j_norm(B - 1, False)
            j_x1T_copy(B - 1, False)
            j_second_sum(B - 1, False)

        @block.tensor
        def _(pe):
            t = nc.tensor
            pe.wait_ge(s_vset, 1)
            pe.wait_ge(s_patches, 16)
            pe.wait_ge(s_conv, 48)
            for c in range(IT):
                o = bank[c // 2][0:IP, (c % 2) * D:(c % 2 + 1) * D]
                for k in range(PC):
                    t.matmul(o, patches[:, k, c * IP:(c + 1) * IP], conv_w[:, k, :], start=(k == 0), stop=False)
                i = t.matmul(o, ones_row[0:1, 0:IP], conv_b[:], start=False, stop=True)
                if c % 2:
                    i.then_inc(s_img_ps[c // 2], 1)
            pe.wait_ge(s_ident, 16)

            def transposed(src, dst, n, done):
                for k in range(KT):
                    for u in range(2):
                        i = t.transpose(dst[0:KD, (2 * k + u) * n:(2 * k + u + 1) * n], src[:, u, k * KD:(k + 1) * KD], ident[0:n, 0:n])
                i.then_inc(done, 1)

            def kdim(k):
                return KD + k

            def project_in(s, first):
                pe.wait_ge(s_pair_in, s + 1)
                transposed(pair_in, M_BANK[0], T, s_hT_ps)

            def project_qk(s, hg):
                if hg == 0:
                    pe.wait_ge(s_hT, s + 1)
                    pe.wait_ge(ok_w["wqkv"], s + 1)
                for j in range(2):
                    c = j * QKP + hg * 128
                    for k in range(KT):
                        i = t.matmul(M_BANK[hg % 3][:, j * 2 * T:(j + 1) * 2 * T], wqkv[0:kdim(k), k, c:c + 128],
                                     hT[0:kdim(k), k, :], start=(k == 0), stop=(k == 1))
                i.then_inc(s_qk_ps, 1)

            def project_v(s):
                pe.wait_ge(s_qk_dve, qk(s, 0))
                pe.wait_ge(s_qk_act, qk(s, 0))
                for u in range(2):
                    for k in range(KT):
                        i = t.matmul(M_BANK[0][:, u * D:(u + 1) * D], hT[0:kdim(k), k, u * T:(u + 1) * T],
                                     wqkv[0:kdim(k), k, 2 * QKP:2 * QKP + D], start=(k == 0), stop=(k == 1))
                i.then_inc(s_v_ps, 1)

            def score(s, i, first):
                u, hg = i // HG, i % HG
                if u == 0:
                    pe.wait_ge(s_qk_dve, qk(s, hg))
                    pe.wait_ge(s_qk_act, qk(s, hg))
                if i >= 2:
                    pe.wait_ge(s_masked, group(s, i - 2))
                elif not first:
                    pe.wait_ge(s_masked, group(s - 1, i + TS - 2))
                t.matmul(S_BANK[i % 2][:, :], qT[:, hg, u * T:(u + 1) * T], kbd[:, hg, u, :, :].rearrange("p r t -> p (r t)"),
                         start=True, stop=True).then_inc(s_score, 1)

            def transpose_probs(s, i):
                pe.wait_ge(s_prob, group(s, i))
                for r in range(R):
                    m = t.transpose(T_BANK[i % 2][:, r * T:(r + 1) * T], ps[i][:, r, :], ident[:])
                m.then_inc(s_pT_ps, 1)

            def weigh(s, i, first):
                u, hg = i // HG, i % HG
                if i == 0:
                    pe.wait_ge(s_va, s + 1)
                    if not first:
                        pe.wait_ge(s_att, s)
                pe.wait_ge(s_pT, group(s, i))
                for r in range(R):
                    h = R * hg + r
                    m = t.matmul(O_BANK[:, (u * H + h) * VA:(u * H + h + 1) * VA], pT[i % 2][:, r, :], va[:, u, h, :], start=True, stop=True)
                m.then_inc(s_pv, 1)

            def project_out(y):
                pe.wait_ge(s_att, y + 1)
                transposed(att, M_BANK[1], T, s_aT_ps)
                pe.wait_ge(s_aT, y + 1)
                pe.wait_ge(ok_w["wo"], y + 1)
                pe.wait_ge(s_z[1], y + 1)
                for u in range(2):
                    for k in range(KT):
                        i = t.matmul(M_BANK[2][:, u * D:(u + 1) * D], aT[0:kdim(k), k, u * T:(u + 1) * T], wo[0:kdim(k), k, :],
                                     start=(k == 0), stop=(k == 1))
                i.then_inc(s_wo_ps, 1)

            def mlp_in(y, s=None):
                if s is not None:
                    pe.wait_ge(s_qk_dve, qk(s, 1))
                    pe.wait_ge(s_qk_act, qk(s, 1))
                pe.wait_ge(s_h1, y + 1)
                transposed(h1, M_BANK[1], T, s_h1T_ps)

            def mlp_up(y, c, s=None):
                if c == 0:
                    pe.wait_ge(s_h1T, y + 1)
                    pe.wait_ge(ok_w["w1"], y + 1)
                    if s is not None:
                        pe.wait_ge(s_qk_dve, qk(s, 2))
                        pe.wait_ge(s_qk_act, qk(s, 2))
                if c == 1 and s is not None:
                    pe.wait_ge(s_va, s + 1)
                for q in range(2):
                    m = 2 * c + q
                    for k in range(KT):
                        i = t.matmul(M_BANK[(2 + c) % 3][:, q * 2 * T:(q + 1) * 2 * T], w1[0:kdim(k), k, m * 128:(m + 1) * 128],
                                     h1T[0:kdim(k), k, :], start=(k == 0), stop=(k == 1))
                i.then_inc(s_up[c], 1)

            def mlp_down(y):
                for c in range(3):
                    pe.wait_ge(s_gelu[c], y + 1)
                pe.wait_ge(ok_w["w2"], y + 1)
                for u in range(2):
                    o = M_BANK[2][:, u * D:(u + 1) * D]
                    for c in range(FC):
                        t.matmul(o, f[:, c, u * T:(u + 1) * T], w2[:, c, :], start=(c == 0), stop=False)
                    i = t.matmul(o, ones_row[:], b2[:], start=False, stop=True)
                i.then_inc(s_down, 1)

            def step(s, first):
                project_in(s, first)
                if not first:
                    project_out(s - 1)
                project_qk(s, 0)
                project_qk(s, 1)
                if not first:
                    pe.wait_ge(s_z[0], s)
                project_qk(s, 2)
                project_v(s)
                if not first:
                    mlp_in(s - 1, s)
                    mlp_up(s - 1, 0, s)
                score(s, 0, first)
                if not first:
                    mlp_up(s - 1, 1, s)
                score(s, 1, first)
                if not first:
                    mlp_up(s - 1, 2, s)
                score(s, 2, first)
                if not first:
                    mlp_down(s - 1)
                for i in range(TS + 1):
                    if i < TS:
                        transpose_probs(s, i)
                    if 3 <= i + 3 < TS:
                        score(s, i + 3, first)
                    if i >= 1:
                        weigh(s, i - 1, first)

            step(0, True)
            with pe.Fori(1, STEPS) as s:
                step(s, False)
            project_out(STEPS - 1)
            pe.wait_ge(s_z[0], STEPS)
            mlp_in(STEPS - 1)
            for c in range(3):
                mlp_up(STEPS - 1, c)
            mlp_down(STEPS - 1)

            pe.wait_ge(s_jw, 64)
            pe.wait_ge(s_z[1], STEPS + 1)

            def j_project(n, first):
                for u in range(2):
                    pe.wait_ge(s_xn[u], n + 1)
                    transposed(xn[u], bank[u], NH, s_xT_ps[u])
                for u in range(2):
                    pe.wait_ge(s_xT[u], n + 1)
                    for j in range(3):
                        if not first:
                            pe.wait_ge(s_qkv_sb, sixth(n - 1, 3 * u + j))
                        for h in range(2):
                            for k in range(KT):
                                i = t.matmul(bank[2 + 3 * u + j][0:NH, h * D:(h + 1) * D], xT[u][:, k, h * NH:(h + 1) * NH],
                                             jwqkv[:, k, j * D:(j + 1) * D], start=(k == 0), stop=(k == 1))
                        i.then_inc(s_qkv_ps, 1)

            j_project(0, True)
            with pe.Fori(1, PAIRS) as n:
                j_project(n, False)
            pe.wait_ge(s_qkv_sb, 6 * PAIRS)

            def j_heads(b, first):
                pe.wait_ge(s_heads[0], 32 * b + 32)
                for hg in range(HG):
                    for h in range(2):
                        i = t.transpose(M_BANK[0][:, (2 * hg + h) * NH:(2 * hg + h + 1) * NH],
                                        qpad[:, h, R * hg:R * hg + R, :].rearrange("p r d -> p (r d)"), ident[0:NH, 0:NH])
                i.then_inc(j_qT_ps, 1)
                pe.wait_ge(s_heads[1], 32 * b + 32)
                if not first:
                    pe.wait_ge(j_out, b)
                for hg in range(HG):
                    for h in range(2):
                        i = t.transpose(M_BANK[1][:, (2 * hg + h) * NH:(2 * hg + h + 1) * NH],
                                        kpad[:, h, R * hg:R * hg + R, :].rearrange("p r d -> p (r d)"), ident[0:NH, 0:NH])
                i.then_inc(j_kT_ps, 1)

            def j_project_out(y, b):
                pe.wait_ge(j_att, y + 1)
                transposed(jatt, M_BANK[2], NH, j_aT_ps)
                pe.wait_ge(j_aT, y + 1)
                if b is not None:
                    pe.wait_ge(j_qT, b + 1)
                for h in range(2):
                    for k in range(KT):
                        i = t.matmul(M_BANK[0][0:NH, h * D:(h + 1) * D], jaT[0:kdim(k), k, h * NH:(h + 1) * NH], jwo[0:kdim(k), k, :],
                                     start=(k == 0), stop=(k == 1))
                i.then_inc(j_wo_ps, 1)

            def j_mlp(y):
                pe.wait_ge(j_n1, y + 1)
                transposed(jn1, M_BANK[1], NH, j_x1T_ps)
                pe.wait_ge(j_x1T, y + 1)
                for c in range(2):
                    for q in range(3):
                        m = 3 * c + q
                        for k in range(KT):
                            i = t.matmul(M_BANK[(2, 0)[c]][:, q * 2 * NH:(q + 1) * 2 * NH], jw1[0:kdim(k), k, m * 128:(m + 1) * 128],
                                         jx1T[0:kdim(k), k, :], start=(k == 0), stop=(k == 1))
                    i.then_inc(j_up[c], 1)

            def j_mlp_down(y):
                pe.wait_ge(j_gelu[0], y + 1)
                pe.wait_ge(j_gelu[1], y + 1)
                for h in range(2):
                    for c in range(FC):
                        i = t.matmul(M_BANK[1][0:NH, h * D:(h + 1) * D], jf[:, c, h * NH:(h + 1) * NH], jw2[:, c, :],
                                     start=(c == 0), stop=(c == FC - 1))
                i.then_inc(j_down, 1)

            def place(i):
                return i // 4, i // 2 % 2, R * (i // 4) + 2 * (i % 2)

            def j_scores(b, i, first):
                hg, half, h0 = place(i)
                if i == 0:
                    pe.wait_ge(j_qT, b + 1)
                    pe.wait_ge(j_kdve, b + 1)
                    pe.wait_ge(j_kact, b + 1)
                if i >= 2:
                    pe.wait_ge(j_centred, nth(b, i - 2))
                elif not first:
                    pe.wait_ge(j_centred, nth(b - 1, i + JS - 2))
                r = h0 % R
                t.matmul(S_BANK[i % 2][0:NH, 0:4 * NH], jqT[:, hg, half * NH:(half + 1) * NH],
                         jkbd[:, hg, r:r + 2, :].rearrange("p r t -> p (r t)"), start=True, stop=True).then_inc(j_score, 1)

            def j_transpose_probs(b, i):
                pe.wait_ge(j_prob_s, nth(b, i))
                for r in range(2):
                    for k in range(2):
                        m = t.transpose(T_BANK[i % 2][0:NH, (2 * r + k) * NH:(2 * r + k + 1) * NH], jps[i % 3][:, r, k * NH:(k + 1) * NH], ident[0:NH, 0:NH])
                m.then_inc(j_pT_ps, 1)

            def j_weigh(b, i, first):
                hg, half, h0 = place(i)
                if i == 0:
                    pe.wait_ge(s_heads[2], 32 * b + 32)
                    if not first:
                        pe.wait_ge(j_att, b)
                pe.wait_ge(j_pT, nth(b, i))
                for r in range(2):
                    for k in range(2):
                        c = (half * H + h0 + r) * VA
                        m = t.matmul(O_BANK[0:NH, c:c + VA], jpT[i % 2][:, r, k, :], jva[:, k, h0 + r, :], start=(k == 0), stop=(k == 1))
                m.then_inc(j_pv, 1)

            def j_step(b, first):
                j_heads(b, first)
                if not first:
                    j_project_out(b - 1, b)
                j_scores(b, 0, first)
                j_scores(b, 1, first)
                for i in range(JS + 1):
                    if i == J_MLP_AT and not first:
                        pe.wait_ge(j_kdve, b + 1)
                        j_mlp(b - 1)
                    if i == J_MLP_AT + 1 and not first:
                        j_mlp_down(b - 1)
                    if i < JS:
                        j_transpose_probs(b, i)
                    if i + 2 < JS:
                        j_scores(b, i + 2, first)
                    if i >= 1:
                        j_weigh(b, i - 1, first)

            j_step(0, True)
            with pe.Fori(1, B) as b:
                j_step(b, False)
            j_project_out(B - 1, None)
            pe.wait_ge(j_z1, B)
            j_mlp(B - 1)
            j_mlp_down(B - 1)


def kernel(**inputs):
    import concourse.bacc as bacc
    from concourse.bass_utils import run_bass_kernel_spmd

    g = {k: np.asarray(v) for k, v in inputs.items()}

    def tiles(w, bias=None):
        o = np.zeros((KD + 1, KT, w.shape[1]), w.dtype)
        o[0:KD] = w.reshape(KT, KD, -1).transpose(1, 0, 2)
        if bias is not None:
            o[KD, 1] = bias
        return o

    def heads(w):
        o = np.zeros(w.shape[:-1] + (H, PADH), w.dtype)
        o[..., 0:HD] = w.reshape(w.shape[:-1] + (H, HD))
        return o.reshape(w.shape[:-1] + (QKP,))

    def txt(n):
        return g["L0_txt_" + n]

    side = IMG_SIDE // PATCH
    at = np.searchsorted(np.arange(1 / 32, 1, 1 / 32, dtype=np.float32), np.arange(0, 1 - 1e-6, 1 / side, dtype=np.float32), side="right")
    pos_rows = g["L0_tok_pos_table"][(at[:, None] * 32 + at).reshape(-1)]
    arrays = {
        "ids": g["x_txt"].T,
        "mask": g["mask_BS_i1_0"],
        "ident": np.eye(128, dtype=np.float32),
        "patches": g["x"].reshape(B, CH, side, PATCH, side, PATCH).transpose(1, 3, 5, 0, 2, 4).reshape(PW, B * NI),
        "conv_w": g["L0_tok_conv_w"].reshape(D, PW).T,
        "conv_b": g["L0_tok_conv_b"].reshape(1, D),
        "img_pos": np.concatenate([pos_rows, pos_rows]),
        "emb_word": txt("emb_word"),
        "emb_pos": txt("emb_pos")[0:T],
        "emb_ln": np.stack([txt("emb_ln_s"), txt("emb_ln_b")]),
        "wqkv": np.stack([np.concatenate([tiles(heads(txt("Wq")[l]), heads(txt("bq")[l])), tiles(heads(txt("Wk")[l]), heads(txt("bk")[l])),
                                          tiles(txt("Wv")[l], txt("bv")[l])], 2) for l in range(L)]),
        "wo": np.stack([tiles(txt("Wo")[l], txt("bo")[l]) for l in range(L)]),
        "w1": np.stack([tiles(txt("W1")[l], txt("b1")[l]) for l in range(L)]),
        "w2": txt("W2"),
        "b2": txt("b2"),
        "ln1": np.stack([txt("ln1_s"), txt("ln1_b")], 1),
        "ln2": np.stack([txt("ln2_s"), txt("ln2_b")], 1),
        "jwqkv": tiles(np.concatenate([g["L0_attn_w_q"].T, g["L0_attn_w_k"].T, g["L0_attn_w_v"].T], 1))[0:KD],
        "jwo": tiles(g["L0_attn_w_o"].T, g["L0_attn_b_o"]),
        "jw1": tiles(g["L0_ffn_in_weight"].T, g["L0_ffn_in_bias"]),
        "jw2": g["L0_ffn_out_weight"],
    }
    arrays = {f"in_{k}": np.ascontiguousarray(v) for k, v in arrays.items()}
    nc = bacc.Bacc("TRN2", target_bir_lowering=False, num_devices=1)
    aps = {k[3:]: nc.dram_tensor(k, v.shape, mybir.dt.from_np(v.dtype), kind="ExternalInput").ap() for k, v in arrays.items()}
    out = nc.dram_tensor("out", (B, N, D), F32, kind="ExternalOutput").ap()
    program(nc, aps, out)
    r = run_bass_kernel_spmd(nc, [arrays], core_ids=[0])
    return r.results[0]["out"]
```

```python
from contextlib import ExitStack

import numpy as np

import concourse.bass as bass
from concourse import mybir

F32 = mybir.dt.float32
F32R = mybir.dt.float32r
I32 = mybir.dt.int32
U32 = mybir.dt.uint32
ALU = mybir.AluOpType
ACT = mybir.ActivationFunctionType
AX_X = mybir.AxisListType.X

B, T, D, H, HD, L, FF = 8, 128, 192, 12, 16, 4, 768
IMG_SIDE, PATCH, CH = 96, 16, 3
NI = (IMG_SIDE // PATCH) ** 2
N = NI + T
NH = N // 2
KT, KD = 2, 96
HG, R, PADH = 3, 4, 32
QKP = HG * R * PADH
FC = FF // 128
PW = CH * PATCH * PATCH
PC = PW // 128
IT, IP = 4, 2 * NI
PAIRS = B // 2
STEPS = L * PAIRS
W = 64
VA = HD + 1
SCALE = 0.25
MASKED = -1e30
PADKEYS = W
EPS_TXT, EPS_JOINT = 1e-12, 1e-5
VOCAB = 8000
TS = 6
JG, JR = 4, 3
JS = 2 * JG


def program(nc, a_, out):
    ctx = ExitStack()
    with ctx:
        def sb(name, shape, dt=F32):
            return ctx.enter_context(nc.sbuf_tensor(name, shape, dt))

        def sem(name):
            return ctx.enter_context(nc.semaphore(name))

        def sems(name, n):
            return [sem(f"{name}{i}") for i in range(n)]

        joined = nc.dram_tensor("joined", (B, N, D), F32, kind="Internal").ap()
        qkv_dram = [nc.dram_tensor(f"{n}_dram", (B, N * D), F32, kind="Internal").ap() for n in "qkv"]

        ident = sb("ident", [128, 128])
        ones_row = sb("ones_row", [1, 128])
        neg_half = sb("neg_half", [128, 2])
        eps = sb("eps", [128, 2, 2])
        tick = sb("tick", [128, 1])
        wqkv = sb("wqkv", [KD + 1, KT, 2 * QKP + D])
        wo = sb("wo", [KD + 1, KT, D])
        w1 = sb("w1", [KD + 1, KT, FF])
        w2 = sb("w2", [128, FC, D])
        b2 = sb("b2", [128, D])
        ln1 = sb("ln1", [128, 2, D])
        ln2 = sb("ln2", [128, 2, D])
        jwqkv = sb("jwqkv", [KD, KT, 3 * D])
        jwo = sb("jwo", [KD + 1, KT, D])
        jw1 = sb("jw1", [KD + 1, KT, FF])
        jw2 = sb("jw2", [128, FC, D])

        ids = sb("ids", [T, B], I32)
        ids_low = sb("ids_low", [T, B], I32)
        ids_up = sb("ids_up", [T, B], I32)
        rows = sb("rows", [T, B], I32)
        emb_pos = sb("emb_pos", [T, D])
        emb_ln = sb("emb_ln", [T, 2, D])
        e_stats = sb("e_stats", [T, B, 6])
        e_mv = sb("e_mv", [T, B, 2])
        e_var = sb("e_var", [T, B])
        e_rstd = sb("e_rstd", [T, B])
        mask0 = sb("mask0", [128, B, T])
        mask = sb("mask", [128, STEPS, 2, T])
        conv_b = sb("conv_b", [1, D])
        img_pos = sb("img_pos", [IP, D])
        img = sb("img", [IP, IT, D])

        hid = sb("hid", [128, STEPS + PAIRS, 2, D])
        free = hid[:].rearrange("p s u d -> p (s u d)")

        def borrowed(slot, n):
            return free[:, slot * 2 * D:slot * 2 * D + n]

        words = borrowed(4, B * D).rearrange("p (b d) -> p b d", b=B)
        patches = borrowed(8, PC * IT * IP).rearrange("p (c t) -> p c t", c=PC)
        conv_w = borrowed(13, PC * D).rearrange("p (c d) -> p c d", c=PC)
        key_mask = borrowed(16, B * T).bitcast(I32).rearrange("p (b t) -> p b t", b=B)
        pair_in = sb("pair_in", [128, 2, D])
        hT = sb("hT", [KD + 1, KT, 2 * T])
        q_hi = sb("q_hi", [128, HG, 2 * T], F32R)
        qT = sb("qT", [128, HG, 2 * T], F32R)
        k_hi = sb("k_hi", [128, HG, 2, R, T], F32R)
        k_lo = sb("k_lo", [128, HG, 2, R, T], F32R)
        low_rows = sb("low_rows", [128, 1])
        va = sb("va", [128, 2, H, VA])
        ps = [sb(f"ps{i}", [128, R, T]) for i in range(TS)]
        pT = [sb(f"pT{i}", [128, R, T]) for i in range(2)]
        mx = sb("mx", [128, 2, H])
        pad_sum = sb("pad_sum", [128, 2, H])
        den = sb("den", [128, 2, H])
        rden = sb("rden", [128, 2, H])
        att = sb("att", [128, 2, D])
        aT = sb("aT", [KD + 1, KT, 2 * T])
        z1 = sb("z1", [128, 2, D])
        z2 = sb("z2", [128, 2, D])
        n1 = sb("n1", [128, 2, D])
        n2 = sb("n2", [128, 2, D])
        h1 = sb("h1", [128, 2, D])
        h1b = sb("h1b", [128, 2, D])
        h1T = sb("h1T", [KD + 1, KT, 2 * T])
        f = sb("f", [128, FC, 2 * T])
        st = [sb(f"st{i}", [128, 2, 6]) for i in range(2)]
        mv = [sb(f"mv{i}", [128, 2, 2]) for i in range(2)]
        ve = [sb(f"ve{i}", [128, 2]) for i in range(2)]
        rs = [sb(f"rs{i}", [128, 2]) for i in range(2)]

        x = hid[0:NH, 0:B, :, :]
        xst = [sb(f"xst{i}", [NH, 2, 6]) for i in range(2)]
        xmv = [sb(f"xmv{i}", [NH, 2, 2]) for i in range(2)]
        xve = [sb(f"xve{i}", [NH, 2]) for i in range(2)]
        xrs = [sb(f"xrs{i}", [NH, 2]) for i in range(2)]
        xn = [sb(f"xn{i}", [NH, 2, D]) for i in range(2)]
        xT = [sb(f"xT{i}", [KD, KT, 2 * NH]) for i in range(2)]
        qkv = [sb(f"qkv{i}", [NH, 2, D]) for i in range(6)]
        joint = free[0:NH, B * 2 * D:]
        raw = [joint[:, i * 2 * D:(i + 1) * 2 * D].rearrange("p (h u d) -> p h u d", h=H, u=2) for i in range(3)]
        qpad, kpad = (joint[:, (3 + 2 * i) * 2 * D:(5 + 2 * i) * 2 * D].rearrange("p (u h c d) -> p u h c d", u=2, h=H, c=2) for i in range(2))
        jva = sb("jva", [NH, 2, H, VA])
        jq_hi, jqT = (q_[:].rearrange("p g t -> p (g t)")[0:JR * PADH, 0:JG * 2 * NH].rearrange("p (g t) -> p g t", g=JG) for q_ in (q_hi, qT))
        jk_hi, jk_lo = (k_[:].rearrange("p g u r t -> p (g u r t)")[0:JR * PADH, 0:JG * JR * 2 * NH]
                        .rearrange("p (g r t) -> p g r t", g=JG, r=JR) for k_ in (k_hi, k_lo))
        jps = [p_[:].rearrange("p r t -> p (r t)")[0:NH, 0:JR * 2 * NH].rearrange("p (r t) -> p r t", r=JR) for p_ in ps[0:4]]
        jpT = [p_[:].rearrange("p r t -> p (r t)")[0:NH, 0:JR * 2 * NH].rearrange("p (r k t) -> p r k t", r=JR, k=2) for p_ in pT]
        zeros = sb("zeros", [NH, HD])
        jmx = sb("jmx", [NH, JS, JR])
        jrden = sb("jrden", [NH, 2, H])
        jatt = sb("jatt", [NH, 2, D])
        jaT = aT[:, :, 0:2 * NH]
        jz1 = sb("jz1", [NH, 2, D])
        jn1 = sb("jn1", [NH, 2, D])
        jx1T = h1T[:, :, 0:2 * NH]
        jf = f[:, :, 0:2 * NH]
        jout = sb("jout", [NH, 2, D])

        bank = [ctx.enter_context(nc.psum_tensor(f"bank{i}", [128, 512], F32)) for i in range(8)]
        S_BANK, T_BANK, O_BANK, M_BANK = bank[0:2], bank[2:4], bank[4], bank[5:8]
        UP_AT, QK_AT = (0, 2, 1), (1, 0, 0)
        JUP_AT, JQ_AT, JK_AT = (1, 0), (2, 1), (0, 2)

        s_ids, s_embtab, s_mask, s_patches, s_conv, s_const = (sem(f"s_{n}_loaded") for n in (
            "ids", "embtab", "mask", "patches", "conv", "const"))
        s_jw = sem("s_joint_weights_loaded")
        s_words = sems("s_words_loaded", PAIRS)
        dma_w = {n: sem(f"s_dma_{n}") for n in ("wqkv", "wo", "ln1", "w1", "w2", "ln2")}
        ok_w = {n: sem(f"s_ok_{n}") for n in ("wqkv", "wo", "ln1", "w1", "w2", "ln2")}
        s_ident, s_vset, s_pset = sem("s_ident"), sem("s_vector_constants"), sem("s_pool_constants")
        s_ids_step, s_rows = sem("s_ids_step"), sem("s_rows_ready")
        s_e = sems("s_embedding_step", 5)
        s_img_ps = sems("s_img_psum", 2)
        s_evar, s_erstd = sem("s_evar"), sem("s_erstd")
        s_mask0, s_band, s_mask_ok = sem("s_mask0"), sem("s_band"), sem("s_mask_ready")
        s_img = [sem(f"s_img_ready{i}") for i in range(2)]
        s_img_out, s_img_stored = sem("s_img_out"), sem("s_img_stored")
        s_hid = sem("s_hid_ready")
        s_pair_in, s_hT_ps, s_hT = sem("s_pair_in"), sem("s_hT_psum"), sem("s_hT")
        s_qk_ps, s_kh, s_qk = sem("s_qk_psum"), sem("s_qk_high"), sem("s_qk_split")

        def qk(s, hg):
            return HG * s + hg + 1

        s_v_ps, s_va = sem("s_v_psum"), sem("s_va")
        s_score, s_masked, s_max, s_centred, s_prob, s_pT_ps, s_pT, s_pv = (sem(f"s_{n}") for n in (
            "score", "masked", "max", "centred", "prob", "pT_psum", "pT", "pv"))

        def group(s, i):
            return TS * s + i + 1
        s_norm = sems("s_norm", 3)
        s_att, s_aT_ps, s_aT, s_wo_ps = sem("s_att"), sem("s_aT_psum"), sem("s_aT"), sem("s_wo_psum")
        s_z = sems("s_z", 2)
        s_st, s_mv, s_ve, s_rs = sems("s_stats", 2), sems("s_mean_var", 2), sems("s_var_eps", 2), sems("s_rstd", 2)
        s_scl = sems("s_scaled", 2)
        s_h1, s_h1b, s_h1T_ps, s_h1T = sem("s_h1"), sem("s_h1_with_bias"), sem("s_h1T_psum"), sem("s_h1T")
        s_up, s_gelu, s_down = sems("s_up_psum", 3), sems("s_gelu", 3), sem("s_down_psum")
        s_x = sem("s_x_loaded")
        s_xn, s_xT_ps, s_xT = sems("s_xn", 2), sems("s_xT_psum", 2), sems("s_xT", 2)
        s_xst, s_xmv, s_xve, s_xrs = sems("s_xst", 2), sems("s_xmv", 2), sems("s_xve", 2), sems("s_xrs", 2)
        s_qkv_ps, s_qkv_sb = sem("s_qkv_psum"), sem("s_qkv_sbuf")

        def sixth(n, i):
            return 6 * n + i + 1

        s_qkv_stored = sems("s_qkv_stored", 6)
        s_heads = [sem(f"s_{n}_heads_loaded") for n in "qkv"]
        s_stored = sem("s_result_stored")

        j_qdup, j_kdup, j_va = sem("j_q_doubled"), sem("j_k_doubled"), sem("j_values")
        j_qT_ps, j_kT_ps, j_qh, j_qT, j_kh, j_kl = (sem(f"j_{n}") for n in (
            "qT_ps", "kT_ps", "q_high", "qT", "k_high", "k_low"))
        j_score, j_max, j_centred, j_prob_s, j_pT_ps, j_pT, j_pv = (sem(f"j_{n}") for n in (
            "score", "max", "centred", "prob", "pT_ps", "pT", "pv"))

        def half_of(b, c):
            return 2 * b + c + 1

        def nth(b, i):
            return JS * b + i + 1

        j_rden, j_att, j_aT_ps, j_aT, j_wo_ps = (sem(f"j_{n}") for n in ("rden", "att", "aT_ps", "aT", "wo_ps"))
        j_z1, j_st, j_mv, j_ve, j_rs, j_n1 = (sem(f"j_{n}") for n in ("z1", "stats", "mean_var", "var_eps", "rstd", "n1"))
        j_x1T_ps, j_x1T, j_down = (sem(f"j_{n}") for n in ("x1T_ps", "x1T", "down"))
        j_out = sem("j_out")
        j_up, j_gelu = sems("j_up", 2), sems("j_gelu", 2)

        block = ctx.enter_context(nc.Block())

        @block.sync
        def _(sp):
            sp.dma_start(ids[:], a_["ids"]).then_inc(s_ids, 16)
            sp.dma_start(ident[:], a_["ident"]).then_inc(s_ident, 16)
            sp.dma_start(low_rows[:], a_["low_rows"]).then_inc(s_ident, 16)
            sp.dma_start(patches, a_["patches"].rearrange("(c p) t -> p c t", p=128)).then_inc(s_patches, 16)
            sp.dma_start(conv_w, a_["conv_w"].rearrange("(c p) t -> p c t", p=128)).then_inc(s_conv, 16)
            sp.dma_start(conv_b[:], a_["conv_b"]).then_inc(s_conv, 16)
            sp.dma_start(img_pos[:], a_["img_pos"]).then_inc(s_conv, 16)
            sp.dma_start(emb_pos[:], a_["emb_pos"]).then_inc(s_embtab, 16)
            sp.dma_start(emb_ln[:], a_["emb_ln"].partition_broadcast(T)).then_inc(s_embtab, 16)
            sp.dma_start(key_mask, a_["mask"].partition_broadcast(128)).then_inc(s_mask, 16)

            weights = (("wqkv", s_v_ps), ("wo", s_wo_ps), ("ln1", s_h1), ("w1", s_up[2]), ("w2", s_z[1]), ("ln2", s_hid))
            before = {"ln2": PAIRS, "w2": 1}

            def load(name, l):
                if name == "w2":
                    sp.dma_start(w2[:], a_["w2"][bass.ds(l, 1)].rearrange("o (c p) d -> p (o c) d", p=128)).then_inc(dma_w[name], 16)
                    sp.dma_start(b2[:], a_["b2"][bass.ds(l, 1), :].partition_broadcast(128).rearrange("p o d -> p (o d)")).then_inc(dma_w[name], 16)
                elif name in ("ln1", "ln2"):
                    src = a_[name][bass.ds(l, 1)].rearrange("o a d -> (o a) d").partition_broadcast(128)
                    sp.dma_start({"ln1": ln1, "ln2": ln2}[name][:], src).then_inc(dma_w[name], 16)
                else:
                    dst = {"wqkv": wqkv, "wo": wo, "w1": w1}[name]
                    sp.dma_start(dst[:], a_[name][bass.ds(l, 1)].rearrange("o p k d -> (o p) k d")).then_inc(dma_w[name], 16)

            for name, _ in weights:
                load(name, 0)
            for name, _ in weights:
                sp.wait_ge(dma_w[name], 32 if name == "w2" else 16)
                sp.sem_inc(ok_w[name], PAIRS)
            sp.dma_start(jwqkv[:], a_["jwqkv"]).then_inc(s_jw, 16)
            sp.dma_start(jwo[:], a_["jwo"]).then_inc(s_jw, 16)
            sp.dma_start(jw1[:], a_["jw1"]).then_inc(s_jw, 16)
            sp.dma_start(jw2[:], a_["jw2"].rearrange("(c p) d -> p c d", p=128)).then_inc(s_jw, 16)
            sp.wait_ge(s_img[0], 1)
            sp.wait_ge(s_img[1], 1)
            batch_of = joined.rearrange("(t u) n d -> u n t d", u=2)
            for u in range(2):
                sp.dma_start(batch_of[u, 0:NI], img[u * NI:(u + 1) * NI, :, :]).then_inc(s_img_stored, 16)
            with sp.Fori(1, L) as l:
                for name, last_use in weights:
                    sp.wait_ge(last_use, PAIRS * l + before.get(name, 0))
                    load(name, l)
                    sp.wait_ge(dma_w[name], (l + 1) * (32 if name == "w2" else 16))
                    sp.sem_inc(ok_w[name], PAIRS)

            def to_joined(p):
                sp.wait_ge(s_hid, STEPS + p + 1)
                for b in (2 * p, 2 * p + 1):
                    sp.dma_start(joined[b, NI:N], hid[:, STEPS + p, b % 2, :]).then_inc(s_img_stored, 16)
                sp.wait_ge(s_img_stored, 16 * (2 + 2 * p + 2))
                for b in (2 * p, 2 * p + 1):
                    sp.dma_start(x[:, b], joined[b].rearrange("(p u) d -> p u d", u=2)).then_inc(s_x, 16)
                sp.wait_ge(s_x, 32 * p + 32)

            def store_qkv(p):
                for u in range(2):
                    for j in range(3):
                        sp.wait_ge(s_qkv_sb, sixth(p, 3 * u + j))
                        sp.dma_start(qkv_dram[j][2 * p + u].rearrange("(p c) -> p c", c=2 * D),
                                     qkv[3 * u + j][:].rearrange("p u d -> p (u d)")).then_inc(s_qkv_stored[3 * u + j], 16)

            def load_heads(b):
                for j in range(3):
                    src = qkv_dram[j][bass.ds(b, 1), :].rearrange("o (h p c) -> p (o h) c", h=H, c=2 * HD)
                    sp.dma_start(raw[j].rearrange("p h u d -> p h (u d)"), src).then_inc(s_heads[j], 16)

            to_joined(0)
            to_joined(1)
            store_qkv(0)
            to_joined(2)
            store_qkv(1)
            to_joined(3)
            sp.wait_ge(s_z[1], STEPS + 1)
            for i in range(3):
                sp.wait_ge(s_qkv_stored[i], 16)
            load_heads(0)
            store_qkv(2)
            store_qkv(3)
            for i in range(6):
                sp.wait_ge(s_qkv_stored[i], 16 * PAIRS)

            def next_heads(b):
                sp.wait_ge(j_qdup, b + 1)
                sp.wait_ge(j_kdup, b + 1)
                sp.wait_ge(j_va, b + 1)
                load_heads(b + 1)

            next_heads(0)
            with sp.Fori(1, B - 1) as b:
                next_heads(b)
                sp.wait_ge(j_out, b + 1)
                sp.dma_start(out[bass.ds(b - 1, 1)].rearrange("o (p u) d -> p (o u) d", u=2), jout[:]).then_inc(s_stored, 16)
            for b in range(B - 2, B):
                sp.wait_ge(j_out, b + 2)
                sp.dma_start(out[b].rearrange("(p u) d -> p u d", u=2), jout[:]).then_inc(s_stored, 16)
            sp.wait_ge(s_stored, 16 * B)

        @block.gpsimd
        def _(pool):
            g = nc.gpsimd
            pool.wait_ge(s_rows, 1)
            for b in range(B):
                g.indirect_dma_start(words[:, b, :], None, a_["emb_word"],
                                     bass.IndirectOffsetOnAxis(ap=rows[:, b:b + 1].bitcast(U32), axis=0)
                                     ).then_inc(s_words[b // 2], 16)
            g.memset(k_hi[:].bitcast(F32), 0.0)
            g.memset(k_lo[:].bitcast(F32), 0.0)
            g.memset(eps[:, 0, :], EPS_TXT)
            g.memset(eps[:, 1, :], EPS_JOINT)
            g.memset(neg_half[:], -0.5).then_inc(s_pset, 1)
            pool.wait_ge(s_pset, 1)
            pool.wait_ge(s_mask0, 1)
            g.affine_select(out=mask0[:], in_=mask0[:], pattern=[[0, B], [-1, T]], compare_op=ALU.is_ge,
                            fill=MASKED, base=W, channel_multiplier=1).then_inc(s_band, 1)
            pool.wait_ge(s_band, 1)
            g.affine_select(out=mask0[:], in_=mask0[:], pattern=[[0, B], [1, T]], compare_op=ALU.is_ge,
                            fill=MASKED, base=W, channel_multiplier=-1).then_inc(s_band, 1)
            for p in range(PAIRS):
                pool.wait_ge(s_e[2], p + 1)
                g.tensor_scalar(e_var[:, 2 * p:2 * p + 2], e_mv[:, 2 * p:2 * p + 2, 1], EPS_TXT, None, ALU.add).then_inc(s_evar, 1)
                pool.wait_ge(s_evar, p + 1)
                g.tensor_tensor(e_rstd[:, 2 * p:2 * p + 2], e_var[:, 2 * p:2 * p + 2], neg_half[:, 0:2], ALU.pow).then_inc(s_erstd, 1)
            g.memset(zeros[:], 0.0)
            g.memset(jva[:], 1.0).then_inc(s_pset, 1)

            def stage(s):
                pool.wait_ge(s_hid, s + 1)
                if not isinstance(s, int) or s > 0:
                    pool.wait_ge(s_hT_ps, s)
                g.tensor_copy(pair_in[:], hid[:, bass.ds(s, 1), :, :].rearrange("p o u d -> p (o u) d")).then_inc(s_pair_in, 1)

            def rstd(which, done):
                pool.wait_ge(s_mv[which], done)
                g.tensor_tensor(ve[which][:], mv[which][:, :, 1], eps[:, 0, :], ALU.add).then_inc(s_ve[which], 1)
                pool.wait_ge(s_ve[which], done)
                g.tensor_tensor(rs[which][:], ve[which][:], neg_half[:, 0:2], ALU.pow).then_inc(s_rs[which], 1)

            def centre_steps(s, lo, hi):
                for i in range(lo, hi):
                    hg, u = i // 2, i % 2
                    pool.wait_ge(s_max, group(s, i))
                    m = mx[:, u, R * hg:R * hg + R].unsqueeze(2).to_broadcast([128, R, T])
                    g.tensor_tensor(ps[i][:], ps[i][:], m, ALU.subtract).then_inc(s_centred, 1)

            def with_bias(y):
                pool.wait_ge(s_h1, y + 1)
                pool.wait_ge(ok_w["w2"], y + 1)
                pool.wait_ge(s_z[1], y + 1)
                g.tensor_tensor(h1b[:], h1[:], b2[:].unsqueeze(1).to_broadcast([128, 2, D]), ALU.add).then_inc(s_h1b, 1)

            def step(s, first=False, second=False, last=False):
                centre_steps(s, 2, 4)
                if not first:
                    rstd(0, s)
                centre_steps(s, 4, 5)
                if not first and not second:
                    rstd(1, s - 1)
                centre_steps(s, 5, TS)
                if not first:
                    with_bias(s - 1)
                if not last:
                    centre_steps(s + 1, 0, 2)
                if not last and (not isinstance(s, int) or s + 2 < STEPS):
                    stage(s + 2)

            stage(0)
            stage(1)
            centre_steps(0, 0, 2)
            step(0, first=True)
            step(1, second=True)
            with pool.Fori(2, STEPS - 1) as s:
                step(s)
            step(STEPS - 1, last=True)

            def x_rstd(p):
                for u in range(2):
                    pool.wait_ge(s_xmv[u], p + 1)
                    g.tensor_tensor(xve[u][:], xmv[u][:, :, 1], eps[0:NH, 1, :], ALU.add).then_inc(s_xve[u], 1)
                    pool.wait_ge(s_xve[u], p + 1)
                    g.tensor_tensor(xrs[u][:], xve[u][:], neg_half[0:NH, 0:2], ALU.pow).then_inc(s_xrs[u], 1)

            x_rstd(0)
            rstd(0, STEPS)
            x_rstd(1)
            rstd(1, STEPS - 1)
            with_bias(STEPS - 1)
            rstd(1, STEPS)

            pool.wait_ge(s_score, group(STEPS - 1, TS - 1))
            g.memset(k_hi[:].bitcast(F32), 0.0)
            g.memset(k_lo[:].bitcast(F32), 0.0).then_inc(s_pset, 1)
            with pool.Fori(2, PAIRS) as p:
                x_rstd(p)

            def doubled(b, first):
                for j, (pad, done, used) in enumerate(((qpad, j_qdup, j_qT_ps), (kpad, j_kdup, j_kT_ps))):
                    pool.wait_ge(s_heads[j], 16 * b + 16)
                    if not first:
                        pool.wait_ge(used, 2 * b)
                    for u in range(2):
                        twice = raw[j][:, :, u, :].unsqueeze(2).to_broadcast([NH, H, 2, HD])
                        i = g.tensor_tensor(pad[:, u], twice, zeros[:].unsqueeze(1).unsqueeze(1).to_broadcast([NH, H, 2, HD]), ALU.add)
                    i.then_inc(done, 1)

            def values(b, first):
                pool.wait_ge(s_heads[2], 16 * b + 16)
                if not first:
                    pool.wait_ge(j_pv, JS * b)
                g.tensor_tensor(jva[:, :, :, 0:HD].rearrange("p u h d -> p h u d"), raw[2],
                                zeros[:].unsqueeze(1).unsqueeze(1).to_broadcast([NH, H, 2, HD]), ALU.add).then_inc(j_va, 1)

            def j_rstd(y):
                pool.wait_ge(j_mv, y + 1)
                g.tensor_tensor(xve[0][:], xmv[0][:, :, 1], eps[0:NH, 1, :], ALU.add).then_inc(j_ve, 1)
                pool.wait_ge(j_ve, y + 1)
                g.tensor_tensor(xrs[0][:], xve[0][:], neg_half[0:NH, 0:2], ALU.pow).then_inc(j_rs, 1)

            doubled(0, True)
            values(0, True)
            doubled(1, False)
            values(1, False)
            with pool.Fori(1, B - 1) as b:
                j_rstd(b - 1)
                doubled(b + 1, False)
                values(b + 1, False)
            j_rstd(B - 2)
            j_rstd(B - 1)

        @block.scalar
        def _(act):
            a = nc.scalar

            def qk_high(s, hg, first):
                act.wait_ge(s_qk_ps, qk(s, hg))
                if not first:
                    act.wait_ge(s_score, group(s - 1, 2 * hg + 1))
                ps_ = M_BANK[QK_AT[hg]]
                a.activation(q_hi[:, hg, :], ps_[:, 0:2 * T], ACT.Copy)
                for r in range(R):
                    rows_ = slice(PADH * r, PADH * r + PADH)
                    i = a.activation(k_hi[rows_, hg, :, r, :], ps_[rows_, 2 * T:4 * T].rearrange("p (u t) -> p u t", u=2), ACT.Copy)
                i.then_inc(s_kh, 1)

            def values(s, first):
                act.wait_ge(s_v_ps, s + 1)
                if not first:
                    act.wait_ge(s_pv, group(s - 1, TS - 1))
                a.activation(va[:, :, :, 0:HD], M_BANK[2][:, 0:2 * D].rearrange("p (u h d) -> p u h d", u=2, h=H), ACT.Copy).then_inc(s_va, 1)

            def transposed_attention(y, first):
                act.wait_ge(s_aT_ps, y + 1)
                if not first:
                    act.wait_ge(s_wo_ps, y)
                a.activation(aT[0:KD, :, :], M_BANK[1][0:KD, :].rearrange("p (k t) -> p k t", k=KT), ACT.Copy).then_inc(s_aT, 1)

            def gelu(y, c, first=False):
                act.wait_ge(s_up[c], y + 1)
                if c == 0 and not first:
                    act.wait_ge(s_down, y)
                a.activation(f[:, 2 * c:2 * c + 2, :], M_BANK[UP_AT[c]][:, :].rearrange("p (c t) -> p c t", c=2), ACT.Gelu).then_inc(s_gelu[c], 1)

            def prob(s, i):
                act.wait_ge(s_centred, group(s, i))
                a.activation(ps[i][:], ps[i][:], ACT.Exp, scale=SCALE).then_inc(s_prob, 1)

            def prob_T(s, i, first):
                act.wait_ge(s_pT_ps, group(s, i))
                if i >= 2:
                    act.wait_ge(s_pv, group(s, i - 2))
                elif not first:
                    act.wait_ge(s_pv, group(s - 1, i + TS - 2))
                a.activation(pT[i % 2][:], T_BANK[i % 2][:, :].rearrange("p (r t) -> p r t", r=R), ACT.Copy).then_inc(s_pT, 1)

            def step(s, first, second=False, last=False):
                if not first:
                    transposed_attention(s - 1, second)
                prob(s, 1)
                prob_T(s, 0, first)
                prob(s, 2)
                prob_T(s, 1, first)
                prob(s, 3)
                prob_T(s, 2, first)
                prob(s, 4)
                prob_T(s, 3, first)
                prob(s, 5)
                if not first:
                    gelu(s - 1, 0, second)
                if not last:
                    qk_high(s + 1, 0, False)
                prob_T(s, 4, first)
                if not first:
                    gelu(s - 1, 1)
                if not last:
                    qk_high(s + 1, 1, False)
                prob_T(s, 5, first)
                if not first:
                    gelu(s - 1, 2)
                if not last:
                    prob(s + 1, 0)
                    qk_high(s + 1, 2, False)
                    values(s + 1, False)

            act.wait_ge(s_vset, 1)
            act.wait_ge(s_pset, 1)
            for hg in range(HG):
                qk_high(0, hg, True)
            prob(0, 0)
            values(0, True)
            step(0, True)
            step(1, False, second=True)
            with act.Fori(2, STEPS - 1) as s:
                step(s, False)
            step(STEPS - 1, False, last=True)
            transposed_attention(STEPS - 1, False)

            def qkv_out(p, lo, hi, first=False):
                for i in range(lo, hi):
                    act.wait_ge(s_qkv_ps, sixth(p, i))
                    if not first:
                        act.wait_ge(s_qkv_stored[i], 16 * p)
                    a.activation(qkv[i][:], bank[2 + i % 3][0:NH, 0:2 * D].rearrange("p (h d) -> p h d", h=2), ACT.Copy).then_inc(s_qkv_sb, 1)

            qkv_out(0, 0, 6, True)
            qkv_out(1, 0, 3)
            for c in range(3):
                gelu(STEPS - 1, c)
            qkv_out(1, 3, 6)
            with act.Fori(2, PAIRS) as p:
                qkv_out(p, 0, 6)

            def j_transposed_attention(y, first):
                act.wait_ge(j_aT_ps, y + 1)
                if not first:
                    act.wait_ge(j_wo_ps, y)
                a.activation(jaT[0:KD, :, :], M_BANK[2][0:KD, 0:4 * NH].rearrange("p (k t) -> p k t", k=KT), ACT.Copy).then_inc(j_aT, 1)

            def j_q_high(b, first):
                for c in range(2):
                    act.wait_ge(j_qT_ps, half_of(b, c))
                    if c == 0 and not first:
                        act.wait_ge(j_score, nth(b - 1, JS - 1))
                    a.activation(jq_hi[:, 2 * c:2 * c + 2, :], M_BANK[JQ_AT[c]][0:JR * PADH, 0:4 * NH].rearrange("p (g t) -> p g t", g=2),
                                 ACT.Copy).then_inc(j_qh, 1)

            def j_k_high(b, c):
                act.wait_ge(j_kT_ps, half_of(b, c))
                for r in range(JR):
                    rows_ = slice(PADH * r, PADH * r + PADH)
                    i = a.activation(jk_hi[rows_, 2 * c:2 * c + 2, r, :], M_BANK[JK_AT[c]][rows_, 0:4 * NH].rearrange("p (g t) -> p g t", g=2), ACT.Copy)
                i.then_inc(j_kh, 1)

            def j_prob(b, i):
                act.wait_ge(j_centred, nth(b, i))
                a.activation(jps[i % 4], jps[i % 4], ACT.Exp, scale=SCALE).then_inc(j_prob_s, 1)

            def j_prob_T(b, i, first):
                act.wait_ge(j_pT_ps, nth(b, i))
                if i >= 2 or not first:
                    act.wait_ge(j_pv, JS * b + i - 1)
                a.activation(jpT[i % 2], T_BANK[i % 2][0:NH, 0:JR * 2 * NH].rearrange("p (r k t) -> p r k t", r=JR, k=2), ACT.Copy).then_inc(j_pT, 1)

            def j_gelu_of(y, c, first=False):
                act.wait_ge(j_up[c], y + 1)
                if c == 0 and not first:
                    act.wait_ge(j_down, y)
                a.activation(jf[:, 3 * c:3 * c + 3, :], M_BANK[JUP_AT[c]][:, 0:6 * NH].rearrange("p (c t) -> p c t", c=3), ACT.Gelu).then_inc(j_gelu[c], 1)

            def j_step(b, first, second=False, last=False):
                if not first:
                    j_transposed_attention(b - 1, second)
                j_prob(b, 1)
                j_prob_T(b, 0, first)
                j_prob(b, 2)
                j_prob_T(b, 1, first)
                j_prob(b, 3)
                j_prob_T(b, 2, first)
                j_prob(b, 4)
                j_prob_T(b, 3, first)
                j_prob(b, 5)
                j_prob_T(b, 4, first)
                j_prob(b, 6)
                if not first:
                    j_gelu_of(b - 1, 0, second)
                    j_gelu_of(b - 1, 1)
                j_prob_T(b, 5, first)
                if not last:
                    j_q_high(b + 1, False)
                j_prob(b, 7)
                if not last:
                    j_k_high(b + 1, 0)
                j_prob_T(b, 6, first)
                if not last:
                    j_k_high(b + 1, 1)
                j_prob_T(b, 7, first)
                if not last:
                    j_prob(b + 1, 0)

            act.wait_ge(s_pset, 3)
            j_q_high(0, True)
            j_k_high(0, 0)
            j_k_high(0, 1)
            j_prob(0, 0)
            j_step(0, True)
            j_step(1, False, second=True)
            with act.Fori(2, B - 1) as b:
                j_step(b, False)
            j_step(B - 1, False, last=True)
            j_transposed_attention(B - 1, False)
            j_gelu_of(B - 1, 0)
            j_gelu_of(B - 1, 1)

        @block.vector
        def _(dve):
            v = nc.vector
            v.memset(ones_row[:], 1.0).then_inc(s_z[1], 1)
            v.memset(tick[:], 0.0).then_inc(j_out, 1)
            v.memset(va[:, :, :, HD:VA], 1.0)
            for t_ in (hT, aT, h1T):
                i = v.memset(t_[KD:KD + 1, :, :], 1.0)
            i.then_inc(s_vset, 1)
            dve.wait_ge(s_ids, 16)
            v.tensor_scalar(ids_low[:], ids[:], 0, VOCAB, ALU.is_lt, ALU.mult).then_inc(s_ids_step, 1)
            dve.wait_ge(s_ids_step, 1)
            v.tensor_tensor(ids_up[:], ids[:], ids_low[:], ALU.add).then_inc(s_ids_step, 1)
            dve.wait_ge(s_ids_step, 2)
            v.tensor_scalar(rows[:], ids_up[:], VOCAB - 1, 0, ALU.min, ALU.max).then_inc(s_rows, 1)
            dve.wait_ge(s_mask, 16)
            v.tensor_scalar(mask0[:], key_mask, 0, MASKED, ALU.is_le, ALU.mult).then_inc(s_mask0, 1)
            dve.wait_ge(s_embtab, 32)
            for p in range(PAIRS):
                two = slice(2 * p, 2 * p + 2)
                dve.wait_ge(s_words[p], 32)
                v.tensor_tensor(words[:, two, :], words[:, two, :], emb_pos[:].unsqueeze(1).to_broadcast([T, 2, D]), ALU.add).then_inc(s_e[0], 1)
                dve.wait_ge(s_e[0], p + 1)
                for b in (2 * p, 2 * p + 1):
                    i = v.bn_stats(e_stats[:, b, :], words[:, b, :])
                i.then_inc(s_e[1], 1)
                dve.wait_ge(s_e[1], p + 1)
                for b in (2 * p, 2 * p + 1):
                    i = v.bn_aggr(e_mv[:, b, :], e_stats[:, b, :])
                i.then_inc(s_e[2], 1)
                dve.wait_ge(s_e[2], p + 1)
                dve.wait_ge(s_erstd, p + 1)
                for b in (2 * p, 2 * p + 1):
                    i = v.tensor_scalar(words[:, b, :], words[:, b, :], e_mv[:, b, 0:1], e_rstd[:, b:b + 1], ALU.subtract, ALU.mult)
                i.then_inc(s_e[3], 1)
                dve.wait_ge(s_e[3], p + 1)
                v.tensor_tensor(words[:, two, :], words[:, two, :], emb_ln[:, 0:1, :].to_broadcast([T, 2, D]), ALU.mult).then_inc(s_e[4], 1)
                dve.wait_ge(s_e[4], p + 1)
                v.tensor_tensor(hid[:, p, :, :], words[:, two, :], emb_ln[:, 1:2, :].to_broadcast([T, 2, D]), ALU.add).then_inc(s_hid, 1)
            dve.wait_ge(s_band, 2)
            v.tensor_copy(mask[:].rearrange("p (l q) u t -> p l (q u) t", l=L), mask0[:].unsqueeze(1).to_broadcast([128, L, B, T])).then_inc(s_mask_ok, 1)
            dve.wait_ge(s_mask_ok, 1)
            dve.wait_ge(s_conv, 48)
            for c in range(2):
                dve.wait_ge(s_img_ps[c], 1)
                v.tensor_tensor(img[:, 2 * c:2 * c + 2, :], bank[c][0:IP, 0:2 * D].rearrange("p (c d) -> p c d", c=2),
                                img_pos[:].unsqueeze(1).to_broadcast([IP, 2, D]), ALU.add).then_inc(s_img[c], 1)

            def hT_copy(s, first):
                dve.wait_ge(s_hT_ps, s + 1)
                if not first:
                    dve.wait_ge(s_v_ps, s)
                v.tensor_copy(hT[0:KD, :, :], M_BANK[2][0:KD, :].rearrange("p (k t) -> p k t", k=KT)).then_inc(s_hT, 1)

            def qk_split(s, hg):
                ps_ = M_BANK[QK_AT[hg]]
                dve.wait_ge(s_kh, qk(s, hg))
                v.scalar_tensor_tensor(qT[:, hg, :], q_hi[:, hg, :].bitcast(F32), low_rows[:, 0:1], ps_[:, 0:2 * T], ALU.mult, ALU.add)
                for r in range(R):
                    rows_ = slice(PADH * r, PADH * r + PADH)
                    i = v.tensor_tensor(k_lo[rows_, hg, :, r, :], ps_[rows_, 2 * T:4 * T].rearrange("p (u t) -> p u t", u=2),
                                        k_hi[rows_, hg, :, r, :].bitcast(F32), ALU.subtract)
                i.then_inc(s_qk, 1)

            def mask_and_max(s, i, first):
                hg, u = i // 2, i % 2
                dve.wait_ge(s_score, group(s, i))
                if not first:
                    dve.wait_ge(s_pT_ps, group(s - 1, i))
                m = mask[:, bass.ds(s, 1), u, :].to_broadcast([128, R, T])
                v.tensor_tensor(ps[i][:], S_BANK[i % 2][:, :].rearrange("p (r t) -> p r t", r=R), m, ALU.add).then_inc(s_masked, 1)
                dve.wait_ge(s_masked, group(s, i))
                v.tensor_reduce(mx[:, u, R * hg:R * hg + R], ps[i][:], AX_X, ALU.max).then_inc(s_max, 1)

            def padded_keys(s):
                dve.wait_ge(s_max, group(s, TS - 1))
                v.tensor_scalar(pad_sum[:], mx[:], 0.5 * MASKED, float(PADKEYS), ALU.is_lt, ALU.mult).then_inc(s_norm[0], 1)

            def normalise(s, first):
                dve.wait_ge(s_norm[0], s + 1)
                dve.wait_ge(s_pv, group(s, TS - 1))
                o = O_BANK[:, 0:2 * H * VA].rearrange("p (u h d) -> p u h d", u=2, h=H)
                v.tensor_tensor(den[:], o[:, :, :, HD], pad_sum[:], ALU.add).then_inc(s_norm[1], 1)
                dve.wait_ge(s_norm[1], s + 1)
                v.reciprocal(rden[:], den[:]).then_inc(s_norm[2], 1)
                dve.wait_ge(s_norm[2], s + 1)
                if not first:
                    dve.wait_ge(s_aT_ps, s)
                v.tensor_tensor(att[:].rearrange("p u (h d) -> p (u h) d", h=H),
                                O_BANK[:, 0:2 * H * VA].rearrange("p (u h d) -> p (u h) d", u=2, h=H)[:, :, 0:HD],
                                rden[:].rearrange("p u h -> p (u h)").unsqueeze(2).to_broadcast([128, 2 * H, HD]), ALU.mult).then_inc(s_att, 1)

            def residual_stats(w, y, ps_, other):
                z = (z1, z2)[w]
                i = v.tensor_tensor(z[:], ps_[:, 0:2 * D].rearrange("p (u d) -> p u d", u=2), other, ALU.add)
                i.then_inc(s_z[w], 1)
                dve.wait_ge(s_z[w], y + 1 + w)
                for u in range(2):
                    i = v.bn_stats(st[w][:, u, :], z[:, u, :])
                i.then_inc(s_st[w], 1)
                dve.wait_ge(s_st[w], y + 1)
                v.memset(tick[:], 0.0)
                for u in range(2):
                    i = v.bn_aggr(mv[w][:, u, :], st[w][:, u, :])
                i.then_inc(s_mv[w], 1)

            def centred_and_scaled(w, y, ln):
                z, n_ = (z1, z2)[w], (n1, n2)[w]
                dve.wait_ge(s_mv[w], y + 1)
                dve.wait_ge(ok_w[("ln1", "ln2")[w]], y + 1)
                for u in range(2):
                    i = v.scalar_tensor_tensor(n_[:, u, :], z[:, u, :], mv[w][:, u, 0:1], ln[:, 0, :], ALU.subtract, ALU.mult)
                i.then_inc(s_scl[w], 1)

            def divided_and_shifted(w, y, ln, dst, done):
                n_ = (n1, n2)[w]
                dve.wait_ge(s_scl[w], y + 1)
                dve.wait_ge(s_rs[w], y + 1)
                for u in range(2):
                    i = v.scalar_tensor_tensor(dst(u), n_[:, u, :], rs[w][:, u:u + 1], ln[:, 1, :], ALU.mult, ALU.add)
                i.then_inc(done, 1)

            def first_sum(y):
                dve.wait_ge(s_wo_ps, y + 1)
                residual_stats(0, y, M_BANK[2], hid[:, bass.ds(y, 1), :, :].rearrange("p o u d -> p (o u) d"))

            def first_norm(y, first):
                centred_and_scaled(0, y, ln1)
                if not first:
                    dve.wait_ge(s_h1T_ps, y)
                    dve.wait_ge(s_h1b, y)
                divided_and_shifted(0, y, ln1, lambda u: h1[:, u, :], s_h1)

            def h1T_copy(y, first):
                dve.wait_ge(s_h1T_ps, y + 1)
                if not first:
                    dve.wait_ge(s_up[2], y)
                v.tensor_copy(h1T[0:KD, :, :], M_BANK[1][0:KD, :].rearrange("p (k t) -> p k t", k=KT)).then_inc(s_h1T, 1)

            def second_sum(y):
                dve.wait_ge(s_down, y + 1)
                dve.wait_ge(s_h1b, y + 1)
                residual_stats(1, y, M_BANK[0], h1b[:])

            def second_norm(y):
                centred_and_scaled(1, y, ln2)
                divided_and_shifted(1, y, ln2, lambda u: hid[:, bass.ds(y + PAIRS, 1), u, :].rearrange("p o d -> p (o d)"), s_hid)

            def step(s, first, second=False, last=False):
                mask_and_max(s, 2, first)
                mask_and_max(s, 3, first)
                if not first:
                    first_sum(s - 1)
                    first_norm(s - 1, second)
                mask_and_max(s, 4, first)
                if not first and not second:
                    second_sum(s - 2)
                if not first:
                    h1T_copy(s - 1, second)
                if not last:
                    hT_copy(s + 1, False)
                mask_and_max(s, 5, first)
                padded_keys(s)
                if not first and not second:
                    second_norm(s - 2)
                if not last:
                    qk_split(s + 1, 0)
                    mask_and_max(s + 1, 0, False)
                    qk_split(s + 1, 1)
                else:
                    for u in range(2):
                        x_stats(u, u, 0)
                normalise(s, first)
                if not last:
                    mask_and_max(s + 1, 1, False)
                    qk_split(s + 1, 2)

            def x_stats(u, b, n):
                for h in range(2):
                    i = v.bn_stats(xst[u][:, h, :], x[:, bass.ds(b, 1), h, :].rearrange("p o d -> p (o d)"))
                i.then_inc(s_xst[u], 1)
                dve.wait_ge(s_xst[u], n + 1)
                v.memset(tick[:], 0.0)
                for h in range(2):
                    i = v.bn_aggr(xmv[u][:, h, :], xst[u][:, h, :])
                i.then_inc(s_xmv[u], 1)

            def x_apply(u, b, n, first):
                dve.wait_ge(s_xmv[u], n + 1)
                dve.wait_ge(s_xrs[u], n + 1)
                if not first:
                    dve.wait_ge(s_xT_ps[u], n)
                for h in range(2):
                    i = v.tensor_scalar(xn[u][:, h, :], x[:, bass.ds(b, 1), h, :].rearrange("p o d -> p (o d)"),
                                        xmv[u][:, h, 0:1], xrs[u][:, h:h + 1], ALU.subtract, ALU.mult)
                i.then_inc(s_xn[u], 1)

            def x_T(u, n, first):
                dve.wait_ge(s_xT_ps[u], n + 1)
                if not first:
                    dve.wait_ge(s_qkv_ps, sixth(n - 1, 3 * u + 2))
                v.tensor_copy(xT[u][:], bank[u][0:KD, 0:4 * NH].rearrange("p (k t) -> p k t", k=KT)).then_inc(s_xT[u], 1)

            def x_pair(n):
                for u in range(2):
                    dve.wait_ge(s_x, 32 * n + 32)
                    x_stats(u, 2 * n + u, n)
                for u in range(2):
                    x_apply(u, 2 * n + u, n, False)
                for u in range(2):
                    x_T(u, n, False)

            hT_copy(0, True)
            for hg in range(HG):
                qk_split(0, hg)
            mask_and_max(0, 0, True)
            mask_and_max(0, 1, True)
            step(0, True)
            step(1, False, second=True)
            with dve.Fori(2, STEPS - 1) as s:
                step(s, False)
            dve.wait_ge(s_x, 32)
            step(STEPS - 1, False, last=True)
            for u in range(2):
                x_apply(u, u, 0, True)
            for u in range(2):
                x_T(u, 0, True)
            first_sum(STEPS - 1)
            dve.wait_ge(s_x, 64)
            for u in range(2):
                x_stats(u, 2 + u, 1)
            first_norm(STEPS - 1, False)
            second_sum(STEPS - 2)
            for u in range(2):
                x_apply(u, 2 + u, 1, False)
            h1T_copy(STEPS - 1, False)
            second_norm(STEPS - 2)
            for u in range(2):
                x_T(u, 1, False)
            second_sum(STEPS - 1)
            second_norm(STEPS - 1)

            with dve.Fori(2, PAIRS) as n:
                x_pair(n)

            def j_q_split(b):
                for c in range(2):
                    dve.wait_ge(j_qh, half_of(b, c))
                    v.scalar_tensor_tensor(jqT[:, 2 * c:2 * c + 2, :], jq_hi[:, 2 * c:2 * c + 2, :].bitcast(F32), low_rows[0:JR * PADH, 0:1],
                                           M_BANK[JQ_AT[c]][0:JR * PADH, 0:4 * NH].rearrange("p (g t) -> p g t", g=2), ALU.mult, ALU.add).then_inc(j_qT, 1)

            def j_k_split(b, c):
                dve.wait_ge(j_kh, half_of(b, c))
                for r in range(JR):
                    rows_ = slice(PADH * r, PADH * r + PADH)
                    i = v.tensor_tensor(jk_lo[rows_, 2 * c:2 * c + 2, r, :], M_BANK[JK_AT[c]][rows_, 0:4 * NH].rearrange("p (g t) -> p g t", g=2),
                                        jk_hi[rows_, 2 * c:2 * c + 2, r, :].bitcast(F32), ALU.subtract)
                i.then_inc(j_kl, 1)

            def j_centre(b, i, first):
                dve.wait_ge(j_score, nth(b, i))
                s_ = S_BANK[i % 2][0:NH, 0:JR * 2 * NH].rearrange("p (r t) -> p r t", r=JR)
                v.tensor_reduce(jmx[:, i, :], s_, AX_X, ALU.max).then_inc(j_max, 1)
                dve.wait_ge(j_max, JS * b + i + 1)
                if i >= 4:
                    dve.wait_ge(j_pT_ps, nth(b, i - 4))
                elif not first:
                    dve.wait_ge(j_pT_ps, nth(b - 1, i + JS - 4))
                v.tensor_tensor(jps[i % 4], s_, jmx[:, i, :].unsqueeze(2).to_broadcast([NH, JR, 2 * NH]), ALU.subtract).then_inc(j_centred, 1)

            def j_normalise(b, first):
                dve.wait_ge(j_pv, JS * (b + 1))
                o = O_BANK[0:NH, 0:2 * H * VA].rearrange("p (u h d) -> p u h d", u=2, h=H)
                v.reciprocal(jrden[:], o[:, :, :, HD]).then_inc(j_rden, 1)
                dve.wait_ge(j_rden, b + 1)
                if not first:
                    dve.wait_ge(j_aT_ps, b)
                v.tensor_tensor(jatt[:].rearrange("p u (h d) -> p (u h) d", h=H),
                                O_BANK[0:NH, 0:2 * H * VA].rearrange("p (u h d) -> p (u h) d", u=2, h=H)[:, :, 0:HD],
                                jrden[:].rearrange("p u h -> p (u h)").unsqueeze(2).to_broadcast([NH, 2 * H, HD]), ALU.mult).then_inc(j_att, 1)

            def j_first_sum(y):
                dve.wait_ge(j_out, y + 1)
                dve.wait_ge(j_wo_ps, y + 1)
                v.tensor_tensor(jz1[:], M_BANK[0][0:NH, 0:2 * D].rearrange("p (h d) -> p h d", h=2),
                                x[:, bass.ds(y, 1), :, :].rearrange("p o h d -> p (o h) d"), ALU.add).then_inc(j_z1, 1)
                dve.wait_ge(j_z1, y + 1)
                for h in range(2):
                    i = v.bn_stats(xst[0][:, h, :], jz1[:, h, :])
                i.then_inc(j_st, 1)
                dve.wait_ge(j_st, y + 1)
                v.memset(tick[:], 0.0)
                for h in range(2):
                    i = v.bn_aggr(xmv[0][:, h, :], xst[0][:, h, :])
                i.then_inc(j_mv, 1)

            def j_norm(y, first):
                dve.wait_ge(j_mv, y + 1)
                dve.wait_ge(j_rs, y + 1)
                if not first:
                    dve.wait_ge(j_x1T_ps, y)
                for h in range(2):
                    i = v.tensor_scalar(jn1[:, h, :], jz1[:, h, :], xmv[0][:, h, 0:1], xrs[0][:, h:h + 1], ALU.subtract, ALU.mult)
                i.then_inc(j_n1, 1)

            def j_x1T_copy(y, first):
                dve.wait_ge(j_x1T_ps, y + 1)
                if not first:
                    dve.wait_ge(j_up[1], y)
                v.tensor_copy(jx1T[0:KD, :, :], M_BANK[2][0:KD, 0:4 * NH].rearrange("p (k t) -> p k t", k=KT)).then_inc(j_x1T, 1)

            def j_second_sum(y, first):
                dve.wait_ge(j_down, y + 1)
                if not first:
                    dve.wait_ge(s_stored, 16 * y)
                v.tensor_tensor(jout[:], M_BANK[1][0:NH, 0:2 * D].rearrange("p (h d) -> p h d", h=2), jz1[:], ALU.add).then_inc(j_out, 1)

            def j_step(b, first, second=False, last=False):
                j_centre(b, 2, first)
                if not first:
                    j_first_sum(b - 1)
                j_centre(b, 3, first)
                if not first:
                    j_norm(b - 1, second)
                j_centre(b, 4, first)
                if not first:
                    j_x1T_copy(b - 1, second)
                j_centre(b, 5, first)
                j_centre(b, 6, first)
                j_centre(b, 7, first)
                if not last:
                    j_q_split(b + 1)
                    j_k_split(b + 1, 0)
                    j_k_split(b + 1, 1)
                j_normalise(b, first)
                if not last:
                    j_centre(b + 1, 0, False)
                if not first:
                    j_second_sum(b - 1, second)
                if not last:
                    j_centre(b + 1, 1, False)

            j_q_split(0)
            j_k_split(0, 0)
            j_k_split(0, 1)
            j_centre(0, 0, True)
            j_centre(0, 1, True)
            j_step(0, True)
            j_step(1, False, second=True)
            with dve.Fori(2, B - 1) as b:
                j_step(b, False)
            j_step(B - 1, False, last=True)
            j_first_sum(B - 1)
            j_norm(B - 1, False)
            j_x1T_copy(B - 1, False)
            j_second_sum(B - 1, False)

        @block.tensor
        def _(pe):
            t = nc.tensor
            pe.wait_ge(s_vset, 1)
            pe.wait_ge(s_patches, 16)
            pe.wait_ge(s_conv, 48)
            for c in range(IT):
                o = bank[c // 2][0:IP, (c % 2) * D:(c % 2 + 1) * D]
                for k in range(PC):
                    t.matmul(o, patches[:, k, c * IP:(c + 1) * IP], conv_w[:, k, :], start=(k == 0), stop=False)
                i = t.matmul(o, ones_row[0:1, 0:IP], conv_b[:], start=False, stop=True)
                if c % 2:
                    i.then_inc(s_img_ps[c // 2], 1)
            pe.wait_ge(s_ident, 16)

            def transposed(src, dst, n, done):
                for k in range(KT):
                    for u in range(2):
                        i = t.transpose(dst[0:KD, (2 * k + u) * n:(2 * k + u + 1) * n], src[:, u, k * KD:(k + 1) * KD], ident[0:n, 0:n])
                i.then_inc(done, 1)

            def kdim(k):
                return KD + k

            def project_in(s, y=None):
                pe.wait_ge(s_pair_in, s + 1)
                if y is not None:
                    pe.wait_ge(s_z[0], y + 1)
                transposed(pair_in, M_BANK[2], T, s_hT_ps)

            def project_qk(s, hg, y=None):
                if hg == 0:
                    pe.wait_ge(s_hT, s + 1)
                    pe.wait_ge(ok_w["wqkv"], s + 1)
                if hg == 0 and y is not None:
                    pe.wait_ge(s_h1T, y + 1)
                if hg == 1 and y is not None:
                    pe.wait_ge(s_gelu[0], y + 1)
                if hg == 2:
                    pe.wait_ge(s_qk, qk(s, 1))
                for j in range(2):
                    c = j * QKP + hg * 128
                    for k in range(KT):
                        i = t.matmul(M_BANK[QK_AT[hg]][:, j * 2 * T:(j + 1) * 2 * T], wqkv[0:kdim(k), k, c:c + 128],
                                     hT[0:kdim(k), k, :], start=(k == 0), stop=(k == 1))
                i.then_inc(s_qk_ps, 1)

            def project_v(s, y=None):
                if y is not None:
                    pe.wait_ge(s_gelu[1], y + 1)
                for u in range(2):
                    for k in range(KT):
                        i = t.matmul(M_BANK[2][:, u * D:(u + 1) * D], hT[0:kdim(k), k, u * T:(u + 1) * T],
                                     wqkv[0:kdim(k), k, 2 * QKP:2 * QKP + D], start=(k == 0), stop=(k == 1))
                i.then_inc(s_v_ps, 1)

            def score(s, i, first):
                hg, u = i // 2, i % 2
                if u == 0:
                    pe.wait_ge(s_qk, qk(s, hg))
                if i >= 2:
                    pe.wait_ge(s_masked, group(s, i - 2))
                elif not first:
                    pe.wait_ge(s_masked, group(s - 1, i + TS - 2))
                for part, keys in enumerate((k_hi, k_lo)):
                    m = t.matmul(S_BANK[i % 2][:, :], qT[:, hg, u * T:(u + 1) * T], keys[:, hg, u, :, :].rearrange("p r t -> p (r t)"),
                                 start=(part == 0), stop=(part == 1))
                m.then_inc(s_score, 1)

            def transpose_probs(s, i):
                pe.wait_ge(s_prob, group(s, i))
                for r in range(R):
                    m = t.transpose(T_BANK[i % 2][:, r * T:(r + 1) * T], ps[i][:, r, :], ident[:])
                m.then_inc(s_pT_ps, 1)

            def weigh(s, i, first):
                hg, u = i // 2, i % 2
                if i == 0:
                    pe.wait_ge(s_va, s + 1)
                    if not first:
                        pe.wait_ge(s_att, s)
                pe.wait_ge(s_pT, group(s, i))
                for r in range(R):
                    h = R * hg + r
                    m = t.matmul(O_BANK[:, (u * H + h) * VA:(u * H + h + 1) * VA], pT[i % 2][:, r, :], va[:, u, h, :], start=True, stop=True)
                m.then_inc(s_pv, 1)

            def transpose_attention(y):
                pe.wait_ge(s_att, y + 1)
                if isinstance(y, int) and y == 0:
                    pe.wait_ge(s_qk, qk(1, 0))
                else:
                    pe.wait_ge(s_gelu[2], y)
                transposed(att, M_BANK[1], T, s_aT_ps)

            def project_out(y, last=False):
                pe.wait_ge(s_aT, y + 1)
                pe.wait_ge(ok_w["wo"], y + 1)
                if not last:
                    pe.wait_ge(s_va, y + 2)
                for u in range(2):
                    for k in range(KT):
                        i = t.matmul(M_BANK[2][:, u * D:(u + 1) * D], aT[0:kdim(k), k, u * T:(u + 1) * T], wo[0:kdim(k), k, :],
                                     start=(k == 0), stop=(k == 1))
                i.then_inc(s_wo_ps, 1)

            def mlp_in(y):
                pe.wait_ge(s_h1, y + 1)
                transposed(h1, M_BANK[1], T, s_h1T_ps)

            def mlp_up(y, c, s=None):
                if c == 0:
                    pe.wait_ge(s_h1T, y + 1)
                    pe.wait_ge(ok_w["w1"], y + 1)
                    pe.wait_ge(s_z[1], y + 1)
                if c == 1 and s is not None:
                    pe.wait_ge(s_hT, s + 1)
                if c == 2 and s is not None:
                    pe.wait_ge(s_qk, qk(s, 0))
                for q in range(2):
                    m = 2 * c + q
                    for k in range(KT):
                        i = t.matmul(M_BANK[UP_AT[c]][:, q * 2 * T:(q + 1) * 2 * T], w1[0:kdim(k), k, m * 128:(m + 1) * 128],
                                     h1T[0:kdim(k), k, :], start=(k == 0), stop=(k == 1))
                i.then_inc(s_up[c], 1)

            def mlp_down(y, u):
                if u == 0:
                    for c in range(3):
                        pe.wait_ge(s_gelu[c], y + 1)
                    pe.wait_ge(ok_w["w2"], y + 1)
                    if isinstance(y, int) and y >= STEPS - 2:
                        pass
                    else:
                        pe.wait_ge(s_qk, qk(y + 2, 2))
                for c in range(FC):
                    i = t.matmul(M_BANK[0][:, u * D:(u + 1) * D], f[:, c, u * T:(u + 1) * T], w2[:, c, :], start=(c == 0), stop=(c == FC - 1))
                if u == 1:
                    i.then_inc(s_down, 1)

            def step(s, first=False, second=False, last=False):
                y = None if first else s - 1
                z = None if first or second else s - 2
                score(s, 2, first)
                if y is not None:
                    transpose_attention(y)
                transpose_probs(s, 0)
                score(s, 3, first)
                if y is not None:
                    project_out(y)
                weigh(s, 0, first)
                transpose_probs(s, 1)
                score(s, 4, first)
                if z is not None:
                    mlp_down(z, 0)
                weigh(s, 1, first)
                transpose_probs(s, 2)
                score(s, 5, first)
                if z is not None:
                    mlp_down(z, 1)
                weigh(s, 2, first)
                if y is not None:
                    mlp_in(y)
                if not last:
                    project_in(s + 1, y)
                transpose_probs(s, 3)
                weigh(s, 3, first)
                nxt = None if last else s + 1
                if y is not None:
                    mlp_up(y, 0)
                if not last:
                    project_qk(s + 1, 0, y)
                transpose_probs(s, 4)
                if y is not None:
                    mlp_up(y, 1, nxt)
                weigh(s, 4, first)
                if not last:
                    project_qk(s + 1, 1, y)
                    score(s + 1, 0, False)
                transpose_probs(s, 5)
                if y is not None:
                    mlp_up(y, 2, nxt)
                weigh(s, 5, first)
                if not last:
                    score(s + 1, 1, False)
                    project_qk(s + 1, 2, y)
                    project_v(s + 1, y)

            project_in(0)
            for hg in range(HG):
                project_qk(0, hg)
            score(0, 0, True)
            score(0, 1, True)
            project_v(0)
            step(0, first=True)
            step(1, second=True)
            with pe.Fori(2, STEPS - 1) as s:
                step(s)
            step(STEPS - 1, last=True)

            def j_transpose(n, u, first):
                pe.wait_ge(s_xn[u], n + 1)
                if first:
                    pe.wait_ge(s_masked, group(STEPS - 1, TS - 2 + u))
                transposed(xn[u], bank[u], NH, s_xT_ps[u])

            def j_project(n, u, first):
                pe.wait_ge(s_xT[u], n + 1)
                if first and u == 0:
                    pe.wait_ge(s_pT, group(STEPS - 1, TS - 1))
                    pe.wait_ge(s_att, STEPS)
                for j in range(3):
                    if not (first and u == 0):
                        pe.wait_ge(s_qkv_sb, 6 * n + 3 * u + j - 2)
                    for h in range(2):
                        for k in range(KT):
                            i = t.matmul(bank[2 + j][0:NH, h * D:(h + 1) * D], xT[u][:, k, h * NH:(h + 1) * NH],
                                         jwqkv[:, k, j * D:(j + 1) * D], start=(k == 0), stop=(k == 1))
                    i.then_inc(s_qkv_ps, 1)

            pe.wait_ge(s_jw, 64)
            for u in range(2):
                j_transpose(0, u, True)
            transpose_attention(STEPS - 1)
            j_project(0, 0, True)
            project_out(STEPS - 1, last=True)
            for u in range(2):
                mlp_down(STEPS - 2, u)
            j_project(0, 1, True)
            mlp_in(STEPS - 1)
            for u in range(2):
                j_transpose(1, u, False)
            mlp_up(STEPS - 1, 0)
            mlp_up(STEPS - 1, 1)
            j_project(1, 0, False)
            mlp_up(STEPS - 1, 2)
            j_project(1, 1, False)
            for u in range(2):
                mlp_down(STEPS - 1, u)
            with pe.Fori(2, PAIRS) as n:
                for u in range(2):
                    j_transpose(n, u, False)
                for u in range(2):
                    j_project(n, u, False)
            pe.wait_ge(s_qkv_sb, 6 * PAIRS)
            pe.wait_ge(s_z[1], STEPS + 1)
            pe.wait_ge(s_xT[0], PAIRS)
            pe.wait_ge(s_xT[1], PAIRS)

            def j_queries(b, y=None):
                pe.wait_ge(j_qdup, b + 1)
                for c in range(2):
                    if c == 1 and y is not None:
                        pe.wait_ge(j_gelu[0], y + 1)
                    split_heads(qpad, c, M_BANK[JQ_AT[c]], j_qT_ps)

            def j_keys(b, y=None):
                pe.wait_ge(j_kdup, b + 1)
                for c in range(2):
                    if c == 1:
                        pe.wait_ge(j_qT, half_of(b, 0))
                    elif y is not None:
                        pe.wait_ge(j_gelu[1], y + 1)
                    split_heads(kpad, c, M_BANK[JK_AT[c]], j_kT_ps)

            def split_heads(pad, c, dst, done):
                for g in range(2):
                    for h in range(2):
                        h0 = JR * (2 * c + g)
                        i = t.transpose(dst[0:JR * PADH, (2 * g + h) * NH:(2 * g + h + 1) * NH],
                                        pad[:, h, h0:h0 + JR].rearrange("p r c d -> p (r c d)"), ident[0:NH, 0:NH])
                i.then_inc(done, 1)

            def j_transpose_attention(y, last=False):
                pe.wait_ge(j_att, y + 1)
                if not last:
                    pe.wait_ge(j_kl, half_of(y + 1, 1))
                transposed(jatt, M_BANK[2], NH, j_aT_ps)

            def j_project_out(y):
                pe.wait_ge(j_aT, y + 1)
                for h in range(2):
                    for k in range(KT):
                        i = t.matmul(M_BANK[0][0:NH, h * D:(h + 1) * D], jaT[0:kdim(k), k, h * NH:(h + 1) * NH], jwo[0:kdim(k), k, :],
                                     start=(k == 0), stop=(k == 1))
                i.then_inc(j_wo_ps, 1)

            def j_mlp_in(y):
                pe.wait_ge(j_n1, y + 1)
                transposed(jn1, M_BANK[2], NH, j_x1T_ps)

            def j_mlp_up(y, c):
                if c == 0:
                    pe.wait_ge(j_x1T, y + 1)
                    pe.wait_ge(j_out, y + 1)
                for q in range(3):
                    m = 3 * c + q
                    for k in range(KT):
                        i = t.matmul(M_BANK[JUP_AT[c]][:, q * 2 * NH:(q + 1) * 2 * NH], jw1[0:kdim(k), k, m * 128:(m + 1) * 128],
                                     jx1T[0:kdim(k), k, :], start=(k == 0), stop=(k == 1))
                i.then_inc(j_up[c], 1)

            def j_mlp_down(y, h, b=None):
                if h == 0:
                    pe.wait_ge(j_gelu[0], y + 1)
                    pe.wait_ge(j_gelu[1], y + 1)
                    if b is not None:
                        pe.wait_ge(j_qT, half_of(b, 1))
                for c in range(FC):
                    i = t.matmul(M_BANK[1][0:NH, h * D:(h + 1) * D], jf[:, c, h * NH:(h + 1) * NH], jw2[:, c, :],
                                 start=(c == 0), stop=(c == FC - 1))
                if h == 1:
                    i.then_inc(j_down, 1)

            def j_scores(b, i, first):
                g, half = i // 2, i % 2
                if i == 0:
                    pe.wait_ge(j_qT, half_of(b, 1))
                    pe.wait_ge(j_kl, half_of(b, 1))
                if i >= 2:
                    pe.wait_ge(j_centred, nth(b, i - 2))
                elif not first:
                    pe.wait_ge(j_centred, nth(b - 1, i + JS - 2))
                for part, keys in enumerate((jk_hi, jk_lo)):
                    m = t.matmul(S_BANK[i % 2][0:NH, 0:JR * 2 * NH], jqT[:, g, half * NH:(half + 1) * NH],
                                 keys[:, g, :, :].rearrange("p r t -> p (r t)"), start=(part == 0), stop=(part == 1))
                m.then_inc(j_score, 1)

            def j_transpose_probs(b, i):
                pe.wait_ge(j_prob_s, nth(b, i))
                for r in range(JR):
                    for k in range(2):
                        m = t.transpose(T_BANK[i % 2][0:NH, (2 * r + k) * NH:(2 * r + k + 1) * NH], jps[i % 4][:, r, k * NH:(k + 1) * NH], ident[0:NH, 0:NH])
                m.then_inc(j_pT_ps, 1)

            def j_weigh(b, i, first):
                g, half = i // 2, i % 2
                if i == 0:
                    pe.wait_ge(j_va, b + 1)
                    if not first:
                        pe.wait_ge(j_att, b)
                pe.wait_ge(j_pT, nth(b, i))
                for r in range(JR):
                    for k in range(2):
                        c = (half * H + JR * g + r) * VA
                        m = t.matmul(O_BANK[0:NH, c:c + VA], jpT[i % 2][:, r, k, :], jva[:, k, JR * g + r, :], start=(k == 0), stop=(k == 1))
                m.then_inc(j_pv, 1)

            def j_step(b, first, last=False):
                y = None if first else b - 1
                if not first:
                    j_transpose_attention(y)
                j_transpose_probs(b, 0)
                j_scores(b, 2, first)
                if not first:
                    j_project_out(y)
                j_weigh(b, 0, first)
                j_transpose_probs(b, 1)
                j_scores(b, 3, first)
                j_weigh(b, 1, first)
                j_transpose_probs(b, 2)
                j_scores(b, 4, first)
                if not first:
                    j_mlp_in(y)
                j_weigh(b, 2, first)
                j_transpose_probs(b, 3)
                j_scores(b, 5, first)
                if not first:
                    j_mlp_up(y, 0)
                j_weigh(b, 3, first)
                j_transpose_probs(b, 4)
                j_scores(b, 6, first)
                if not first:
                    j_mlp_up(y, 1)
                j_weigh(b, 4, first)
                j_transpose_probs(b, 5)
                j_scores(b, 7, first)
                if not last:
                    j_queries(b + 1, y)
                j_weigh(b, 5, first)
                if not last:
                    j_keys(b + 1, y)
                j_transpose_probs(b, 6)
                j_weigh(b, 6, first)
                j_transpose_probs(b, 7)
                if not first:
                    j_mlp_down(y, 0, None if last else b + 1)
                j_weigh(b, 7, first)
                if not last:
                    j_scores(b + 1, 0, False)
                if not first:
                    j_mlp_down(y, 1)
                if not last:
                    j_scores(b + 1, 1, False)

            j_queries(0)
            j_keys(0)
            j_scores(0, 0, True)
            j_scores(0, 1, True)
            j_step(0, True)
            with pe.Fori(1, B - 1) as b:
                j_step(b, False)
            j_step(B - 1, False, last=True)
            j_transpose_attention(B - 1, last=True)
            j_project_out(B - 1)
            j_mlp_in(B - 1)
            for c in range(2):
                j_mlp_up(B - 1, c)
            for h in range(2):
                j_mlp_down(B - 1, h)


def kernel(**inputs):
    import concourse.bacc as bacc
    from concourse.bass_utils import run_bass_kernel_spmd

    g = {k: np.asarray(v) for k, v in inputs.items()}

    def tiles(w, bias=None):
        o = np.zeros((KD + 1, KT, w.shape[1]), w.dtype)
        o[0:KD] = w.reshape(KT, KD, -1).transpose(1, 0, 2)
        if bias is not None:
            o[KD, 1] = bias
        return o

    def heads(w):
        o = w.reshape(w.shape[:-1] + (H, HD))
        return np.concatenate([o, o], -1).reshape(w.shape[:-1] + (QKP,))

    def txt(n):
        return g["L0_txt_" + n]

    side = IMG_SIDE // PATCH
    at = np.searchsorted(np.arange(1 / 32, 1, 1 / 32, dtype=np.float32), np.arange(0, 1 - 1e-6, 1 / side, dtype=np.float32), side="right")
    pos_rows = g["L0_tok_pos_table"][(at[:, None] * 32 + at).reshape(-1)]
    arrays = {
        "ids": g["x_txt"].T,
        "mask": g["mask_BS_i1_0"],
        "ident": np.eye(128, dtype=np.float32),
        "low_rows": -(np.arange(128)[:, None] % PADH // HD).astype(np.float32),
        "patches": g["x"].reshape(B, CH, side, PATCH, side, PATCH).transpose(1, 3, 5, 0, 2, 4).reshape(PW, B * NI),
        "conv_w": g["L0_tok_conv_w"].reshape(D, PW).T,
        "conv_b": g["L0_tok_conv_b"].reshape(1, D),
        "img_pos": np.concatenate([pos_rows, pos_rows]),
        "emb_word": txt("emb_word"),
        "emb_pos": txt("emb_pos")[0:T],
        "emb_ln": np.stack([txt("emb_ln_s"), txt("emb_ln_b")]),
        "wqkv": np.stack([np.concatenate([tiles(heads(txt("Wq")[l]), heads(txt("bq")[l])), tiles(heads(txt("Wk")[l]), heads(txt("bk")[l])),
                                          tiles(txt("Wv")[l], txt("bv")[l])], 2) for l in range(L)]),
        "wo": np.stack([tiles(txt("Wo")[l], txt("bo")[l]) for l in range(L)]),
        "w1": np.stack([tiles(txt("W1")[l], txt("b1")[l]) for l in range(L)]),
        "w2": txt("W2"),
        "b2": txt("b2"),
        "ln1": np.stack([txt("ln1_s"), txt("ln1_b")], 1),
        "ln2": np.stack([txt("ln2_s"), txt("ln2_b")], 1),
        "jwqkv": tiles(np.concatenate([g["L0_attn_w_q"].T, g["L0_attn_w_k"].T, g["L0_attn_w_v"].T], 1))[0:KD],
        "jwo": tiles(g["L0_attn_w_o"].T, g["L0_attn_b_o"]),
        "jw1": tiles(g["L0_ffn_in_weight"].T, g["L0_ffn_in_bias"]),
        "jw2": g["L0_ffn_out_weight"],
    }
    arrays = {f"in_{k}": np.ascontiguousarray(v) for k, v in arrays.items()}
    nc = bacc.Bacc("TRN2", target_bir_lowering=False, num_devices=1)
    aps = {k[3:]: nc.dram_tensor(k, v.shape, mybir.dt.from_np(v.dtype), kind="ExternalInput").ap() for k, v in arrays.items()}
    out = nc.dram_tensor("out", (B, N, D), F32, kind="ExternalOutput").ap()
    program(nc, aps, out)
    r = run_bass_kernel_spmd(nc, [arrays], core_ids=[0])
    return r.results[0]["out"]
```

```python
from contextlib import ExitStack

import numpy as np

import concourse.bass as bass
from concourse import mybir

F32 = mybir.dt.float32
F32R = mybir.dt.float32r
I32 = mybir.dt.int32
U32 = mybir.dt.uint32
ALU = mybir.AluOpType
ACT = mybir.ActivationFunctionType
AX_X = mybir.AxisListType.X

B, T, D, H, HD, L, FF = 8, 128, 192, 12, 16, 4, 768
IMG_SIDE, PATCH, CH = 96, 16, 3
NI = (IMG_SIDE // PATCH) ** 2
N = NI + T
NH = N // 2
KT, KD = 2, 96
HG, R, PADH = 3, 4, 32
QKP = HG * R * PADH
FC = FF // 128
PW = CH * PATCH * PATCH
PC = PW // 128
IT, IP = 4, 2 * NI
PAIRS = B // 2
STEPS = L * PAIRS
W = 64
VA = HD + 1
SCALE = 0.25
MASKED = -1e30
PADKEYS = W
EPS_TXT, EPS_JOINT = 1e-12, 1e-5
VOCAB = 8000
TS = 6
JG, JR = 4, 3
JS = 2 * JG


def program(nc, a_, out):
    ctx = ExitStack()
    with ctx:
        def sb(name, shape, dt=F32):
            return ctx.enter_context(nc.sbuf_tensor(name, shape, dt))

        def sem(name):
            return ctx.enter_context(nc.semaphore(name))

        def sems(name, n):
            return [sem(f"{name}{i}") for i in range(n)]

        joined = nc.dram_tensor("joined", (B, N, D), F32, kind="Internal").ap()
        qkv_dram = [nc.dram_tensor(f"{n}_dram", (B, N * D), F32, kind="Internal").ap() for n in "qkv"]

        ident = sb("ident", [128, 128])
        ones_row = sb("ones_row", [1, 128])
        neg_half = sb("neg_half", [128, 2])
        eps = sb("eps", [128, 2, 2])
        table = sb("table", [1, 1])
        tick = sb("tick", [128, 1])
        wqkv = sb("wqkv", [KD + 1, KT, 2 * QKP + D])
        wo = sb("wo", [KD + 1, KT, D])
        w1 = sb("w1", [KD + 1, KT, FF])
        w2 = sb("w2", [128, FC, D])
        b2 = sb("b2", [128, D])
        ln1 = sb("ln1", [128, 2, D])
        ln2 = sb("ln2", [128, 2, D])
        jwqkv = sb("jwqkv", [KD, KT, 3 * D])
        jwo = sb("jwo", [KD + 1, KT, D])
        jw1 = sb("jw1", [KD + 1, KT, FF])
        jw2 = sb("jw2", [128, FC, D])

        ids = sb("ids", [T, B], I32)
        ids_low = sb("ids_low", [T, B], I32)
        ids_up = sb("ids_up", [T, B], I32)
        rows = sb("rows", [T, B], I32)
        emb_pos = sb("emb_pos", [T, D])
        emb_ln = sb("emb_ln", [T, 2, D])
        e_stats = sb("e_stats", [T, B, 6])
        e_mv = sb("e_mv", [T, B, 2])
        e_var = sb("e_var", [T, B])
        e_rstd = sb("e_rstd", [T, B])
        mask0 = sb("mask0", [128, B, T])
        mask = sb("mask", [128, STEPS, 2, T])
        conv_b = sb("conv_b", [1, D])
        img_pos = sb("img_pos", [IP, D])
        img = sb("img", [IP, IT, D])

        hid = sb("hid", [128, STEPS + PAIRS, 2, D])
        free = hid[:].rearrange("p s u d -> p (s u d)")

        def borrowed(slot, n):
            return free[:, slot * 2 * D:slot * 2 * D + n]

        words = borrowed(4, B * D).rearrange("p (b d) -> p b d", b=B)
        patches = borrowed(8, PC * IT * IP).rearrange("p (c t) -> p c t", c=PC)
        conv_w = borrowed(13, PC * D).rearrange("p (c d) -> p c d", c=PC)
        key_mask = borrowed(16, B * T).bitcast(I32).rearrange("p (b t) -> p b t", b=B)
        pair_in = sb("pair_in", [128, 2, D])
        hT = sb("hT", [KD + 1, KT, 2 * T])
        q_hi = sb("q_hi", [128, HG, 2 * T], F32R)
        qT = sb("qT", [128, HG, 2 * T], F32R)
        k_hi = sb("k_hi", [128, HG, 2, R, T], F32R)
        k_lo = sb("k_lo", [128, HG, 2, R, T], F32R)
        low_rows = sb("low_rows", [128, 1])
        va = sb("va", [128, 2, H, VA])
        ps = [sb(f"ps{i}", [128, R, T]) for i in range(TS)]
        pT = [sb(f"pT{i}", [128, R, T]) for i in range(2)]
        mx = sb("mx", [128, 2, H])
        pad_sum = sb("pad_sum", [128, 2, H])
        den = sb("den", [128, 2, H])
        rden = sb("rden", [128, 2, H])
        att = sb("att", [128, 2, D])
        aT = sb("aT", [KD + 1, KT, 2 * T])
        z1 = sb("z1", [128, 2, D])
        z2 = sb("z2", [128, 2, D])
        n1 = sb("n1", [128, 2, D])
        n2 = sb("n2", [128, 2, D])
        h1 = sb("h1", [128, 2, D])
        h1b = sb("h1b", [128, 2, D])
        h1T = sb("h1T", [KD + 1, KT, 2 * T])
        f = sb("f", [128, FC, 2 * T])
        st = [sb(f"st{i}", [128, 2, 6]) for i in range(2)]
        mv = [sb(f"mv{i}", [128, 2, 2]) for i in range(2)]
        ve = [sb(f"ve{i}", [128, 2]) for i in range(2)]
        rs = [sb(f"rs{i}", [128, 2]) for i in range(2)]

        x = hid[0:NH, 0:B, :, :]
        xst = [sb(f"xst{i}", [NH, 2, 6]) for i in range(2)]
        xmv = [sb(f"xmv{i}", [NH, 2, 2]) for i in range(2)]
        xve = [sb(f"xve{i}", [NH, 2]) for i in range(2)]
        xrs = [sb(f"xrs{i}", [NH, 2]) for i in range(2)]
        xn = [sb(f"xn{i}", [NH, 2, D]) for i in range(2)]
        xT = [sb(f"xT{i}", [KD, KT, 2 * NH]) for i in range(2)]
        qkv = [sb(f"qkv{i}", [NH, 2, D]) for i in range(6)]
        joint = free[0:NH, B * 2 * D:]
        raw = [joint[:, i * 2 * D:(i + 1) * 2 * D].rearrange("p (h u d) -> p h u d", h=H, u=2) for i in range(3)]
        qpad, kpad = (joint[:, (3 + 2 * i) * 2 * D:(5 + 2 * i) * 2 * D].rearrange("p (u h c d) -> p u h c d", u=2, h=H, c=2) for i in range(2))
        jva = sb("jva", [NH, 2, H, VA])
        jq_hi, jqT = (q_[:].rearrange("p g t -> p (g t)")[0:JR * PADH, 0:JG * 2 * NH].rearrange("p (g t) -> p g t", g=JG) for q_ in (q_hi, qT))
        jk_hi, jk_lo = (k_[:].rearrange("p g u r t -> p (g u r t)")[0:JR * PADH, 0:JG * JR * 2 * NH]
                        .rearrange("p (g r t) -> p g r t", g=JG, r=JR) for k_ in (k_hi, k_lo))
        jps = [p_[:].rearrange("p r t -> p (r t)")[0:NH, 0:JR * 2 * NH].rearrange("p (r t) -> p r t", r=JR) for p_ in ps[0:4]]
        jpT = [p_[:].rearrange("p r t -> p (r t)")[0:NH, 0:JR * 2 * NH].rearrange("p (r k t) -> p r k t", r=JR, k=2) for p_ in pT]
        zeros = sb("zeros", [NH, HD])
        jmx = sb("jmx", [NH, JS, JR])
        jrden = sb("jrden", [NH, 2, H])
        jatt = sb("jatt", [NH, 2, D])
        jaT = aT[:, :, 0:2 * NH]
        jz1 = sb("jz1", [NH, 2, D])
        jz2 = sb("jz2", [NH, 2, D])
        jn1 = sb("jn1", [NH, 2, D])
        jx1T = h1T[:, :, 0:2 * NH]
        jf = f[:, :, 0:2 * NH]
        jout = sb("jout", [NH, 2, D])

        bank = [ctx.enter_context(nc.psum_tensor(f"bank{i}", [128, 512], F32)) for i in range(8)]
        S_BANK, T_BANK, O_BANK, M_BANK = bank[0:2], bank[2:4], bank[4], bank[5:8]
        UP_AT = (0, 2, 1)

        def qk_bank(s, hg):
            return 2 if isinstance(s, int) and s == 0 and hg == 2 else (1, 0, 0)[hg]

        JUP_AT, JQ_AT, JK_AT = (2, 0), (1, 2), (0, 1)
        JQKV_AT = [M_BANK[i] for i in (2, 0, 1, 2, 0, 2)]

        s_ids, s_embtab, s_mask, s_patches, s_conv, s_const = (sem(f"s_{n}_loaded") for n in (
            "ids", "embtab", "mask", "patches", "conv", "const"))
        s_jw = sem("s_joint_weights_loaded")
        s_words = sems("s_words_loaded", PAIRS)
        dma_w = {n: sem(f"s_dma_{n}") for n in ("wqkv", "wo", "ln1", "w1", "w2", "ln2")}
        ok_w = {n: sem(f"s_ok_{n}") for n in ("wqkv", "wo", "ln1", "w1", "w2", "ln2")}
        s_ident, s_vset, s_pset = sem("s_ident"), sem("s_vector_constants"), sem("s_pool_constants")
        s_ids_step, s_rows = sem("s_ids_step"), sem("s_rows_ready")
        s_e = sems("s_embedding_step", 5)
        s_img_ps = sems("s_img_psum", 2)
        s_evar, s_erstd = sem("s_evar"), sem("s_erstd")
        s_mask0, s_band, s_mask_ok = sem("s_mask0"), sem("s_band"), sem("s_mask_ready")
        s_img = [sem(f"s_img_ready{i}") for i in range(2)]
        s_img_out, s_img_stored = sem("s_img_out"), sem("s_img_stored")
        s_hid = sem("s_hid_ready")
        s_pair_in, s_hT_ps, s_hT = sem("s_pair_in"), sem("s_hT_psum"), sem("s_hT")
        s_qk_ps, s_kh, s_qk = sem("s_qk_psum"), sem("s_qk_high"), sem("s_qk_split")

        def qk(s, hg):
            return HG * s + hg + 1

        s_v_ps, s_va = sem("s_v_psum"), sem("s_va")
        s_score, s_masked, s_max, s_centred, s_prob, s_pT_ps, s_pT, s_pv = (sem(f"s_{n}") for n in (
            "score", "masked", "max", "centred", "prob", "pT_psum", "pT", "pv"))

        def group(s, i):
            return TS * s + i + 1
        s_norm = sems("s_norm", 3)
        s_att, s_aT_ps, s_aT, s_wo_ps = sem("s_att"), sem("s_aT_psum"), sem("s_aT"), sem("s_wo_psum")
        s_z = sems("s_z", 2)
        s_st, s_mv, s_ve, s_rs = sems("s_stats", 2), sems("s_mean_var", 2), sems("s_var_eps", 2), sems("s_rstd", 2)
        s_scl = sems("s_scaled", 2)
        s_h1, s_h1b, s_h1T_ps, s_h1T = sem("s_h1"), sem("s_h1_with_bias"), sem("s_h1T_psum"), sem("s_h1T")
        s_up, s_gelu, s_down = sems("s_up_psum", 3), sems("s_gelu", 3), sem("s_down_psum")
        s_x = sem("s_x_loaded")
        s_xn, s_xT_ps, s_xT = sems("s_xn", 2), sems("s_xT_psum", 2), sems("s_xT", 2)
        s_xst, s_xmv, s_xve, s_xrs = sems("s_xst", 2), sems("s_xmv", 2), sems("s_xve", 2), sems("s_xrs", 2)
        s_qkv_ps, s_qkv_sb = sem("s_qkv_psum"), sem("s_qkv_sbuf")

        def sixth(n, i):
            return 6 * n + i + 1

        s_qkv_stored = sems("s_qkv_stored", 6)
        s_heads = [sem(f"s_{n}_heads_loaded") for n in "qkv"]
        s_stored = sem("s_result_stored")

        j_qdup, j_kdup, j_va = sem("j_q_doubled"), sem("j_k_doubled"), sem("j_values")
        j_qT_ps, j_kT_ps, j_qh, j_qT, j_kh, j_kl = (sem(f"j_{n}") for n in (
            "qT_ps", "kT_ps", "q_high", "qT", "k_high", "k_low"))
        j_score, j_max, j_centred, j_prob_s, j_pT_ps, j_pT, j_pv = (sem(f"j_{n}") for n in (
            "score", "max", "centred", "prob", "pT_ps", "pT", "pv"))

        def half_of(b, c):
            return 2 * b + c + 1

        def nth(b, i):
            return JS * b + i + 1

        j_rden, j_att, j_aT_ps, j_aT, j_wo_ps = (sem(f"j_{n}") for n in ("rden", "att", "aT_ps", "aT", "wo_ps"))
        j_z2 = sem("j_z1_kept")
        j_z1, j_st, j_mv, j_ve, j_rs, j_n1 = (sem(f"j_{n}") for n in ("z1", "stats", "mean_var", "var_eps", "rstd", "n1"))
        j_x1T_ps, j_x1T, j_down = (sem(f"j_{n}") for n in ("x1T_ps", "x1T", "down"))
        j_out = sem("j_out")
        j_up, j_gelu = sems("j_up", 2), sems("j_gelu", 2)

        block = ctx.enter_context(nc.Block())

        @block.sync
        def _(sp):
            sp.dma_start(ids[:], a_["ids"]).then_inc(s_ids, 16)
            sp.dma_start(emb_pos[:], a_["emb_pos"]).then_inc(s_embtab, 16)
            sp.dma_start(emb_ln[:], a_["emb_ln"].partition_broadcast(T)).then_inc(s_embtab, 16)
            sp.dma_start(key_mask, a_["mask"].partition_broadcast(128)).then_inc(s_mask, 16)
            sp.dma_start(ident[:], a_["ident"]).then_inc(s_ident, 16)
            sp.dma_start(low_rows[:], a_["low_rows"]).then_inc(s_ident, 16)

            weights = (("wqkv", s_qk_ps), ("wo", s_wo_ps), ("ln1", s_h1), ("w1", s_up[2]), ("w2", s_z[1]), ("ln2", s_hid))
            before = {"ln2": PAIRS, "w2": 1}
            each = {"wqkv": HG}

            def load(name, l):
                if name == "w2":
                    sp.dma_start(w2[:], a_["w2"][bass.ds(l, 1)].rearrange("o (c p) d -> p (o c) d", p=128)).then_inc(dma_w[name], 16)
                    sp.dma_start(b2[:], a_["b2"][bass.ds(l, 1), :].partition_broadcast(128).rearrange("p o d -> p (o d)")).then_inc(dma_w[name], 16)
                elif name in ("ln1", "ln2"):
                    src = a_[name][bass.ds(l, 1)].rearrange("o a d -> (o a) d").partition_broadcast(128)
                    sp.dma_start({"ln1": ln1, "ln2": ln2}[name][:], src).then_inc(dma_w[name], 16)
                else:
                    dst = {"wqkv": wqkv, "wo": wo, "w1": w1}[name]
                    sp.dma_start(dst[:], a_[name][bass.ds(l, 1)].rearrange("o p k d -> (o p) k d")).then_inc(dma_w[name], 16)

            load("wqkv", 0)
            sp.wait_ge(s_words[0], 32)
            sp.dma_start(patches, a_["patches"].rearrange("(c p) t -> p c t", p=128)).then_inc(s_patches, 16)
            sp.dma_start(conv_w, a_["conv_w"].rearrange("(c p) t -> p c t", p=128)).then_inc(s_conv, 16)
            sp.dma_start(conv_b[:], a_["conv_b"]).then_inc(s_conv, 16)
            sp.dma_start(img_pos[:], a_["img_pos"]).then_inc(s_conv, 16)
            for name, _ in weights[1:]:
                load(name, 0)
            for name, _ in weights:
                sp.wait_ge(dma_w[name], 32 if name == "w2" else 16)
                sp.sem_inc(ok_w[name], PAIRS)
            sp.dma_start(jwqkv[:], a_["jwqkv"]).then_inc(s_jw, 16)
            sp.dma_start(jwo[:], a_["jwo"]).then_inc(s_jw, 16)
            sp.dma_start(jw1[:], a_["jw1"]).then_inc(s_jw, 16)
            sp.dma_start(jw2[:], a_["jw2"].rearrange("(c p) d -> p c d", p=128)).then_inc(s_jw, 16)
            sp.wait_ge(s_img[0], 1)
            sp.wait_ge(s_img[1], 1)
            batch_of = joined.rearrange("(t u) n d -> u n t d", u=2)
            for u in range(2):
                sp.dma_start(batch_of[u, 0:NI], img[u * NI:(u + 1) * NI, :, :]).then_inc(s_img_stored, 16)
            with sp.Fori(1, L) as l:
                for name, last_use in weights:
                    sp.wait_ge(last_use, PAIRS * each.get(name, 1) * l + before.get(name, 0))
                    load(name, l)
                    sp.wait_ge(dma_w[name], (l + 1) * (32 if name == "w2" else 16))
                    sp.sem_inc(ok_w[name], PAIRS)

            def to_joined(p):
                sp.wait_ge(s_hid, STEPS + p + 1)
                for b in (2 * p, 2 * p + 1):
                    sp.dma_start(joined[b, NI:N], hid[:, STEPS + p, b % 2, :]).then_inc(s_img_stored, 16)
                sp.wait_ge(s_img_stored, 16 * (2 + 2 * p + 2))
                for b in (2 * p, 2 * p + 1):
                    sp.dma_start(x[:, b], joined[b].rearrange("(p u) d -> p u d", u=2)).then_inc(s_x, 16)
                sp.wait_ge(s_x, 32 * p + 32)

            def store_qkv(p):
                for u in range(2):
                    for j in range(3):
                        sp.wait_ge(s_qkv_sb, sixth(p, 3 * u + j))
                        sp.dma_start(qkv_dram[j][2 * p + u].rearrange("(p c) -> p c", c=2 * D),
                                     qkv[3 * u + j][:].rearrange("p u d -> p (u d)")).then_inc(s_qkv_stored[3 * u + j], 16)

            def load_heads(b):
                for j in range(3):
                    src = qkv_dram[j][bass.ds(b, 1), :].rearrange("o (h p c) -> p (o h) c", h=H, c=2 * HD)
                    sp.dma_start(raw[j].rearrange("p h u d -> p h (u d)"), src).then_inc(s_heads[j], 16)

            to_joined(0)
            to_joined(1)
            store_qkv(0)
            for i in range(3):
                sp.wait_ge(s_qkv_stored[i], 16)
            sp.wait_ge(s_z[0], STEPS)
            load_heads(0)
            to_joined(2)
            store_qkv(1)
            for i in range(3, 6):
                sp.wait_ge(s_qkv_stored[i], 16)

            def next_heads(b):
                sp.wait_ge(j_qdup, b + 1)
                sp.wait_ge(j_kdup, b + 1)
                sp.wait_ge(j_va, b + 1)
                load_heads(b + 1)

            next_heads(0)
            to_joined(3)
            store_qkv(2)
            store_qkv(3)
            for i in range(6):
                sp.wait_ge(s_qkv_stored[i], 16 * PAIRS)
            next_heads(1)
            with sp.Fori(2, B - 1) as b:
                next_heads(b)
                sp.wait_ge(j_out, b)
                sp.dma_start(out[bass.ds(b - 2, 1)].rearrange("o (p u) d -> p (o u) d", u=2), jout[:]).then_inc(s_stored, 16)
            for b in range(B - 3, B):
                sp.wait_ge(j_out, b + 2)
                sp.dma_start(out[b].rearrange("(p u) d -> p u d", u=2), jout[:]).then_inc(s_stored, 16)
            sp.wait_ge(s_stored, 16 * B)

        @block.gpsimd
        def _(pool):
            g = nc.gpsimd
            def gather(p):
                for b in (2 * p, 2 * p + 1):
                    g.indirect_dma_start(words[:, b, :], None, a_["emb_word"],
                                         bass.IndirectOffsetOnAxis(ap=rows[:, b:b + 1].bitcast(U32), axis=0)
                                         ).then_inc(s_words[p], 16)

            def e_rstd_of(p):
                pool.wait_ge(s_e[2], p + 1)
                g.tensor_scalar(e_var[:, 2 * p:2 * p + 2], e_mv[:, 2 * p:2 * p + 2, 1], EPS_TXT, None, ALU.add).then_inc(s_evar, 1)
                pool.wait_ge(s_evar, p + 1)
                g.tensor_tensor(e_rstd[:, 2 * p:2 * p + 2], e_var[:, 2 * p:2 * p + 2], neg_half[:, 0:2], ALU.pow).then_inc(s_erstd, 1)

            def stage(s):
                pool.wait_ge(s_hid, s + 1)
                if not isinstance(s, int) or s > 1:
                    pool.wait_ge(s_hT_ps, s)
                g.tensor_copy(pair_in[:], hid[:, bass.ds(s, 1), :, :].rearrange("p o u d -> p (o u) d")).then_inc(s_pair_in, 1)

            def rstd(which, done):
                pool.wait_ge(s_mv[which], done)
                g.tensor_tensor(ve[which][:], mv[which][:, :, 1], eps[:, 0, :], ALU.add).then_inc(s_ve[which], 1)
                pool.wait_ge(s_ve[which], done)
                g.tensor_tensor(rs[which][:], ve[which][:], neg_half[:, 0:2], ALU.pow).then_inc(s_rs[which], 1)

            def centre_steps(s, lo, hi):
                for i in range(lo, hi):
                    hg, u = i // 2, i % 2
                    pool.wait_ge(s_max, group(s, i))
                    m = mx[:, u, R * hg:R * hg + R].unsqueeze(2).to_broadcast([128, R, T])
                    g.tensor_tensor(ps[i][:], ps[i][:], m, ALU.subtract).then_inc(s_centred, 1)

            def with_bias(y):
                pool.wait_ge(s_h1, y + 1)
                pool.wait_ge(ok_w["w2"], y + 1)
                pool.wait_ge(s_z[1], y + 1)
                g.tensor_tensor(h1b[:], h1[:], b2[:].unsqueeze(1).to_broadcast([128, 2, D]), ALU.add).then_inc(s_h1b, 1)

            def step(s, first=False, second=False, last=False):
                centre_steps(s, 2, 4)
                if first:
                    e_rstd_of(2)
                else:
                    rstd(0, s)
                centre_steps(s, 4, 5)
                if not first and not second:
                    rstd(1, s - 1)
                centre_steps(s, 5, TS)
                if first:
                    e_rstd_of(3)
                if not first:
                    with_bias(s - 1)
                if not last:
                    centre_steps(s + 1, 0, 2)
                if not last and (not isinstance(s, int) or s + 2 < STEPS):
                    stage(s + 2)

            pool.wait_ge(s_rows, 1)
            gather(0)
            g.memset(eps[:, 0, :], EPS_TXT)
            g.memset(eps[:, 1, :], EPS_JOINT)
            g.memset(neg_half[:], -0.5).then_inc(s_pset, 1)
            gather(1)
            pool.wait_ge(s_pset, 1)
            pool.wait_ge(s_mask0, 1)
            g.affine_select(out=mask0[:], in_=mask0[:], pattern=[[0, B], [-1, T]], compare_op=ALU.is_ge,
                            fill=MASKED, base=W, channel_multiplier=1).then_inc(s_band, 1)
            e_rstd_of(0)
            pool.wait_ge(s_band, 1)
            g.affine_select(out=mask0[:], in_=mask0[:], pattern=[[0, B], [1, T]], compare_op=ALU.is_ge,
                            fill=MASKED, base=W, channel_multiplier=-1).then_inc(s_band, 1)
            e_rstd_of(1)
            gather(2)
            gather(3)
            g.memset(k_lo[:].bitcast(F32), 0.0).then_inc(s_pset, 1)
            stage(1)
            g.memset(zeros[:], 0.0)
            g.memset(jva[:], 1.0)
            centre_steps(0, 0, 2)
            step(0, first=True)
            step(1, second=True)
            with pool.Fori(2, STEPS - 1) as s:
                step(s)
            step(STEPS - 1, last=True)

            def x_rstd(p):
                for u in range(2):
                    pool.wait_ge(s_xmv[u], p + 1)
                    g.tensor_tensor(xve[u][:], xmv[u][:, :, 1], eps[0:NH, 1, :], ALU.add).then_inc(s_xve[u], 1)
                    pool.wait_ge(s_xve[u], p + 1)
                    g.tensor_tensor(xrs[u][:], xve[u][:], neg_half[0:NH, 0:2], ALU.pow).then_inc(s_xrs[u], 1)

            x_rstd(0)
            pool.wait_ge(s_score, group(STEPS - 1, TS - 1))
            g.memset(k_hi[:].bitcast(F32), 0.0)
            g.memset(k_lo[:].bitcast(F32), 0.0).then_inc(s_pset, 1)
            rstd(0, STEPS)
            x_rstd(1)
            rstd(1, STEPS - 1)
            with_bias(STEPS - 1)

            def doubled(b, first):
                for j, (pad, done, used) in enumerate(((qpad, j_qdup, j_qT_ps), (kpad, j_kdup, j_kT_ps))):
                    pool.wait_ge(s_heads[j], 16 * b + 16)
                    if not first:
                        pool.wait_ge(used, 2 * b)
                    for u in range(2):
                        twice = raw[j][:, :, u, :].unsqueeze(2).to_broadcast([NH, H, 2, HD])
                        i = g.tensor_tensor(pad[:, u], twice, zeros[:].unsqueeze(1).unsqueeze(1).to_broadcast([NH, H, 2, HD]), ALU.add)
                    i.then_inc(done, 1)

            def values(b, first):
                pool.wait_ge(s_heads[2], 16 * b + 16)
                if not first:
                    pool.wait_ge(j_pv, JS * b)
                g.tensor_tensor(jva[:, :, :, 0:HD].rearrange("p u h d -> p h u d"), raw[2],
                                zeros[:].unsqueeze(1).unsqueeze(1).to_broadcast([NH, H, 2, HD]), ALU.add).then_inc(j_va, 1)

            def j_rstd(y):
                pool.wait_ge(j_mv, y + 1)
                g.tensor_tensor(xve[0][:], xmv[0][:, :, 1], eps[0:NH, 1, :], ALU.add).then_inc(j_ve, 1)
                pool.wait_ge(j_ve, y + 1)
                g.tensor_tensor(xrs[0][:], xve[0][:], neg_half[0:NH, 0:2], ALU.pow).then_inc(j_rs, 1)

            doubled(0, True)
            values(0, True)
            x_rstd(2)
            rstd(1, STEPS)
            x_rstd(3)
            doubled(1, False)
            values(1, False)

            def keep_z(y, first=False):
                pool.wait_ge(j_out, y + 1)
                pool.wait_ge(j_z1, y + 1)
                g.tensor_tensor(jz2[:], jz1[:], zeros[:, 0:1].unsqueeze(1).to_broadcast([NH, 2, D]), ALU.add).then_inc(j_z2, 1)

            with pool.Fori(1, B - 1) as b:
                j_rstd(b - 1)
                doubled(b + 1, False)
                keep_z(b - 1)
                values(b + 1, False)
            j_rstd(B - 2)
            keep_z(B - 2)
            j_rstd(B - 1)
            keep_z(B - 1)

        @block.scalar
        def _(act):
            a = nc.scalar

            def qk_high(s, hg, first):
                act.wait_ge(s_qk_ps, qk(s, hg))
                if not first:
                    act.wait_ge(s_score, group(s - 1, 2 * hg + 1))
                ps_ = M_BANK[qk_bank(s, hg)]
                a.activation(q_hi[:, hg, :], ps_[:, 0:2 * T], ACT.Copy)
                for r in range(R):
                    rows_ = slice(PADH * r, PADH * r + PADH)
                    i = a.activation(k_hi[rows_, hg, :, r, :], ps_[rows_, 2 * T:4 * T].rearrange("p (u t) -> p u t", u=2), ACT.Copy)
                i.then_inc(s_kh, 1)

            def values(s, first):
                act.wait_ge(s_v_ps, s + 1)
                if not first:
                    act.wait_ge(s_pv, group(s - 1, TS - 1))
                a.activation(va[:, :, :, 0:HD], M_BANK[2][:, 0:2 * D].rearrange("p (u h d) -> p u h d", u=2, h=H), ACT.Copy).then_inc(s_va, 1)

            def transposed_attention(y, first):
                act.wait_ge(s_aT_ps, y + 1)
                if not first:
                    act.wait_ge(s_wo_ps, y)
                a.activation(aT[0:KD, :, :], M_BANK[1][0:KD, :].rearrange("p (k t) -> p k t", k=KT), ACT.Copy).then_inc(s_aT, 1)

            def gelu(y, c, first=False):
                act.wait_ge(s_up[c], y + 1)
                if c == 0 and not first:
                    act.wait_ge(s_down, y)
                a.activation(f[:, 2 * c:2 * c + 2, :], M_BANK[UP_AT[c]][:, :].rearrange("p (c t) -> p c t", c=2), ACT.Gelu).then_inc(s_gelu[c], 1)

            def prob(s, i):
                act.wait_ge(s_centred, group(s, i))
                a.activation(ps[i][:], ps[i][:], ACT.Exp, scale=SCALE).then_inc(s_prob, 1)

            def prob_T(s, i, first):
                act.wait_ge(s_pT_ps, group(s, i))
                if i >= 2:
                    act.wait_ge(s_pv, group(s, i - 2))
                elif not first:
                    act.wait_ge(s_pv, group(s - 1, i + TS - 2))
                a.activation(pT[i % 2][:], T_BANK[i % 2][:, :].rearrange("p (r t) -> p r t", r=R), ACT.Copy).then_inc(s_pT, 1)

            def step(s, first, second=False, last=False):
                if not first:
                    transposed_attention(s - 1, second)
                prob(s, 1)
                prob_T(s, 0, first)
                prob(s, 2)
                prob_T(s, 1, first)
                prob(s, 3)
                prob_T(s, 2, first)
                prob(s, 4)
                if first:
                    masks(slice(1, L))
                prob_T(s, 3, first)
                prob(s, 5)
                if not first:
                    gelu(s - 1, 0, second)
                if not last:
                    qk_high(s + 1, 0, False)
                prob_T(s, 4, first)
                if not first:
                    gelu(s - 1, 1)
                if not last:
                    qk_high(s + 1, 1, False)
                prob_T(s, 5, first)
                if not first:
                    gelu(s - 1, 2)
                if not last:
                    prob(s + 1, 0)
                    values(s + 1, False)
                    qk_high(s + 1, 2, False)

            act.wait_ge(s_z[1], 1)
            a.activation(table[:], ones_row[0:1, 0:1], ACT.Exp)

            def masks(layers):
                rest = mask[:].rearrange("p (l q) u t -> p l (q u) t", l=L)[:, layers]
                a.activation(rest, mask0[:].unsqueeze(1).to_broadcast([128, layers.stop - layers.start, B, T]), ACT.Copy).then_inc(s_mask_ok, 1)

            act.wait_ge(s_vset, 1)
            qk_high(0, 0, True)
            qk_high(0, 1, True)
            act.wait_ge(s_band, 2)
            masks(slice(0, 1))
            qk_high(0, 2, True)
            prob(0, 0)
            values(0, True)
            step(0, True)
            step(1, False, second=True)
            with act.Fori(2, STEPS - 1) as s:
                step(s, False)
            step(STEPS - 1, False, last=True)
            transposed_attention(STEPS - 1, False)

            def qkv_out(p, lo, hi, first=False, at=tuple(bank[2 + i % 3] for i in range(6))):
                for i in range(lo, hi):
                    act.wait_ge(s_qkv_ps, sixth(p, i))
                    if not first:
                        act.wait_ge(s_qkv_stored[i], 16 * p)
                    a.activation(qkv[i][:], at[i][0:NH, 0:2 * D].rearrange("p (h d) -> p h d", h=2), ACT.Copy).then_inc(s_qkv_sb, 1)

            qkv_out(0, 0, 6, True)
            qkv_out(1, 0, 3)
            for c in range(3):
                gelu(STEPS - 1, c)
            qkv_out(1, 3, 6)

            def j_transposed_attention(y, first):
                act.wait_ge(j_aT_ps, y + 1)
                if not first:
                    act.wait_ge(j_wo_ps, y)
                a.activation(jaT[0:KD, :, :], M_BANK[0][0:KD, 0:4 * NH].rearrange("p (k t) -> p k t", k=KT), ACT.Copy).then_inc(j_aT, 1)

            def j_q_high(b, first):
                for c in range(2):
                    act.wait_ge(j_qT_ps, half_of(b, c))
                    if c == 0 and not first:
                        act.wait_ge(j_score, nth(b - 1, JS - 1))
                    a.activation(jq_hi[:, 2 * c:2 * c + 2, :], M_BANK[JQ_AT[c]][0:JR * PADH, 0:4 * NH].rearrange("p (g t) -> p g t", g=2),
                                 ACT.Copy).then_inc(j_qh, 1)

            def j_k_high(b, c):
                act.wait_ge(j_kT_ps, half_of(b, c))
                for r in range(JR):
                    rows_ = slice(PADH * r, PADH * r + PADH)
                    i = a.activation(jk_hi[rows_, 2 * c:2 * c + 2, r, :], M_BANK[JK_AT[c]][rows_, 0:4 * NH].rearrange("p (g t) -> p g t", g=2), ACT.Copy)
                i.then_inc(j_kh, 1)

            def j_prob(b, i):
                act.wait_ge(j_centred, nth(b, i))
                a.activation(jps[i % 4], jps[i % 4], ACT.Exp, scale=SCALE).then_inc(j_prob_s, 1)

            def j_prob_T(b, i, first):
                act.wait_ge(j_pT_ps, nth(b, i))
                if i >= 2 or not first:
                    act.wait_ge(j_pv, JS * b + i - 1)
                a.activation(jpT[i % 2], T_BANK[i % 2][0:NH, 0:JR * 2 * NH].rearrange("p (r k t) -> p r k t", r=JR, k=2), ACT.Copy).then_inc(j_pT, 1)

            def j_gelu_of(y, c, first=False):
                act.wait_ge(j_up[c], y + 1)
                if c == 0 and not first:
                    act.wait_ge(j_down, y)
                a.activation(jf[:, 3 * c:3 * c + 3, :], M_BANK[JUP_AT[c]][:, 0:6 * NH].rearrange("p (c t) -> p c t", c=3), ACT.Gelu).then_inc(j_gelu[c], 1)

            def j_step(b, first, second=False, last=False):
                if not first:
                    j_transposed_attention(b - 1, second)
                j_prob(b, 1)
                j_prob_T(b, 0, first)
                j_prob(b, 2)
                j_prob_T(b, 1, first)
                j_prob(b, 3)
                j_prob_T(b, 2, first)
                j_prob(b, 4)
                j_prob_T(b, 3, first)
                j_prob(b, 5)
                if first:
                    qkv_out(3, 0, 3, at=JQKV_AT)
                j_prob_T(b, 4, first)
                j_prob(b, 6)
                j_prob_T(b, 5, first)
                if not last:
                    j_q_high(b + 1, False)
                j_prob(b, 7)
                j_prob_T(b, 6, first)
                if not last:
                    j_k_high(b + 1, 0)
                    j_k_high(b + 1, 1)
                if first:
                    qkv_out(3, 3, 4, at=JQKV_AT)
                else:
                    j_gelu_of(b - 1, 0, second)
                j_prob_T(b, 7, first)
                if first:
                    qkv_out(3, 4, 6, at=JQKV_AT)
                else:
                    j_gelu_of(b - 1, 1)
                if not last:
                    j_prob(b + 1, 0)

            act.wait_ge(s_pset, 3)
            qkv_out(2, 0, 3)
            j_q_high(0, True)
            j_k_high(0, 0)
            j_k_high(0, 1)
            qkv_out(2, 3, 6)
            j_prob(0, 0)
            j_step(0, True)
            j_step(1, False, second=True)
            with act.Fori(2, B - 1) as b:
                j_step(b, False)
            j_step(B - 1, False, last=True)
            j_transposed_attention(B - 1, False)
            j_gelu_of(B - 1, 0)
            j_gelu_of(B - 1, 1)

        @block.vector
        def _(dve):
            v = nc.vector
            v.memset(ones_row[:], 1.0).then_inc(s_z[1], 1)
            v.memset(tick[:], 0.0).then_inc(j_out, 1)
            dve.wait_ge(s_ids, 16)
            v.tensor_scalar(ids_low[:], ids[:], 0, VOCAB, ALU.is_lt, ALU.mult).then_inc(s_ids_step, 1)
            dve.wait_ge(s_ids_step, 1)
            v.tensor_tensor(ids_up[:], ids[:], ids_low[:], ALU.add).then_inc(s_ids_step, 1)
            dve.wait_ge(s_ids_step, 2)
            v.tensor_scalar(rows[:], ids_up[:], VOCAB - 1, 0, ALU.min, ALU.max).then_inc(s_rows, 1)
            v.memset(va[:, :, :, HD:VA], 1.0)
            v.memset(k_hi[:].bitcast(F32), 0.0)
            for t_ in (hT, aT, h1T):
                i = v.memset(t_[KD:KD + 1, :, :], 1.0)
            i.then_inc(s_vset, 1)

            def embed_sum(p):
                two = slice(2 * p, 2 * p + 2)
                dve.wait_ge(s_words[p], 32)
                v.tensor_tensor(words[:, two, :], words[:, two, :], emb_pos[:].unsqueeze(1).to_broadcast([T, 2, D]), ALU.add).then_inc(s_e[0], 1)
                dve.wait_ge(s_e[0], p + 1)
                for b in (2 * p, 2 * p + 1):
                    i = v.bn_stats(e_stats[:, b, :], words[:, b, :])
                i.then_inc(s_e[1], 1)
                dve.wait_ge(s_e[1], p + 1)
                for b in (2 * p, 2 * p + 1):
                    i = v.bn_aggr(e_mv[:, b, :], e_stats[:, b, :])
                i.then_inc(s_e[2], 1)

            def embed_norm(p):
                dve.wait_ge(s_e[2], p + 1)
                for b in (2 * p, 2 * p + 1):
                    i = v.scalar_tensor_tensor(words[:, b, :], words[:, b, :], e_mv[:, b, 0:1], emb_ln[:, 0, :], ALU.subtract, ALU.mult)
                i.then_inc(s_e[3], 1)
                dve.wait_ge(s_e[3], p + 1)
                dve.wait_ge(s_erstd, p + 1)
                for b in (2 * p, 2 * p + 1):
                    i = v.scalar_tensor_tensor(hid[:, p, b % 2, :], words[:, b, :], e_rstd[:, b:b + 1], emb_ln[:, 1, :], ALU.mult, ALU.add)
                i.then_inc(s_hid, 1)

            dve.wait_ge(s_mask, 16)
            v.tensor_scalar(mask0[:], key_mask, 0, MASKED, ALU.is_le, ALU.mult).then_inc(s_mask0, 1)
            dve.wait_ge(s_embtab, 32)
            embed_sum(0)
            embed_norm(0)
            embed_sum(1)

            def hT_copy(s, first):
                dve.wait_ge(s_hT_ps, s + 1)
                if not first:
                    dve.wait_ge(s_v_ps, s)
                v.tensor_copy(hT[0:KD, :, :], M_BANK[2][0:KD, :].rearrange("p (k t) -> p k t", k=KT)).then_inc(s_hT, 1)

            def qk_split(s, hg):
                ps_ = M_BANK[qk_bank(s, hg)]
                dve.wait_ge(s_kh, qk(s, hg))
                v.scalar_tensor_tensor(qT[:, hg, :], q_hi[:, hg, :].bitcast(F32), low_rows[:, 0:1], ps_[:, 0:2 * T], ALU.mult, ALU.add)
                for r in range(R):
                    rows_ = slice(PADH * r, PADH * r + PADH)
                    i = v.tensor_tensor(k_lo[rows_, hg, :, r, :], ps_[rows_, 2 * T:4 * T].rearrange("p (u t) -> p u t", u=2),
                                        k_hi[rows_, hg, :, r, :].bitcast(F32), ALU.subtract)
                i.then_inc(s_qk, 1)

            def mask_and_max(s, i, first):
                hg, u = i // 2, i % 2
                dve.wait_ge(s_score, group(s, i))
                if not first:
                    dve.wait_ge(s_pT_ps, group(s - 1, i))
                m = mask[:, bass.ds(s, 1), u, :].to_broadcast([128, R, T])
                v.tensor_tensor(ps[i][:], S_BANK[i % 2][:, :].rearrange("p (r t) -> p r t", r=R), m, ALU.add).then_inc(s_masked, 1)
                dve.wait_ge(s_masked, group(s, i))
                v.tensor_reduce(mx[:, u, R * hg:R * hg + R], ps[i][:], AX_X, ALU.max).then_inc(s_max, 1)

            def padded_keys(s):
                dve.wait_ge(s_max, group(s, TS - 1))
                v.tensor_scalar(pad_sum[:], mx[:], 0.5 * MASKED, float(PADKEYS), ALU.is_lt, ALU.mult).then_inc(s_norm[0], 1)

            def normalise(s, first):
                dve.wait_ge(s_norm[0], s + 1)
                dve.wait_ge(s_pv, group(s, TS - 1))
                o = O_BANK[:, 0:2 * H * VA].rearrange("p (u h d) -> p u h d", u=2, h=H)
                v.tensor_tensor(den[:], o[:, :, :, HD], pad_sum[:], ALU.add).then_inc(s_norm[1], 1)
                dve.wait_ge(s_norm[1], s + 1)
                v.reciprocal(rden[:], den[:]).then_inc(s_norm[2], 1)
                dve.wait_ge(s_norm[2], s + 1)
                if not first:
                    dve.wait_ge(s_aT_ps, s)
                v.tensor_tensor(att[:].rearrange("p u (h d) -> p (u h) d", h=H),
                                O_BANK[:, 0:2 * H * VA].rearrange("p (u h d) -> p (u h) d", u=2, h=H)[:, :, 0:HD],
                                rden[:].rearrange("p u h -> p (u h)").unsqueeze(2).to_broadcast([128, 2 * H, HD]), ALU.mult).then_inc(s_att, 1)

            def residual(w, y, ps_, other):
                v.tensor_tensor((z1, z2)[w][:], ps_[:, 0:2 * D].rearrange("p (u d) -> p u d", u=2), other, ALU.add).then_inc(s_z[w], 1)

            def stats(w, y):
                dve.wait_ge(s_z[w], y + 1 + w)
                for u in range(2):
                    i = v.bn_stats(st[w][:, u, :], (z1, z2)[w][:, u, :])
                i.then_inc(s_st[w], 1)
                dve.wait_ge(s_st[w], y + 1)
                v.memset(tick[:], 0.0)
                for u in range(2):
                    i = v.bn_aggr(mv[w][:, u, :], st[w][:, u, :])
                i.then_inc(s_mv[w], 1)

            def centred_and_scaled(w, y, ln):
                z, n_ = (z1, z2)[w], (n1, n2)[w]
                dve.wait_ge(s_mv[w], y + 1)
                dve.wait_ge(ok_w[("ln1", "ln2")[w]], y + 1)
                for u in range(2):
                    i = v.scalar_tensor_tensor(n_[:, u, :], z[:, u, :], mv[w][:, u, 0:1], ln[:, 0, :], ALU.subtract, ALU.mult)
                i.then_inc(s_scl[w], 1)

            def divided_and_shifted(w, y, ln, dst, done):
                n_ = (n1, n2)[w]
                dve.wait_ge(s_scl[w], y + 1)
                dve.wait_ge(s_rs[w], y + 1)
                for u in range(2):
                    i = v.scalar_tensor_tensor(dst(u), n_[:, u, :], rs[w][:, u:u + 1], ln[:, 1, :], ALU.mult, ALU.add)
                i.then_inc(done, 1)

            def first_sum(y):
                dve.wait_ge(s_wo_ps, y + 1)
                residual(0, y, M_BANK[2], hid[:, bass.ds(y, 1), :, :].rearrange("p o u d -> p (o u) d"))
                stats(0, y)

            def first_norm(y, first):
                centred_and_scaled(0, y, ln1)
                if not first:
                    dve.wait_ge(s_h1T_ps, y)
                    dve.wait_ge(s_h1b, y)
                divided_and_shifted(0, y, ln1, lambda u: h1[:, u, :], s_h1)

            def h1T_copy(y, first):
                dve.wait_ge(s_h1T_ps, y + 1)
                if not first:
                    dve.wait_ge(s_up[2], y)
                v.tensor_copy(h1T[0:KD, :, :], M_BANK[1][0:KD, :].rearrange("p (k t) -> p k t", k=KT)).then_inc(s_h1T, 1)

            def second_sum(y):
                dve.wait_ge(s_down, y + 1)
                dve.wait_ge(s_h1b, y + 1)
                residual(1, y, M_BANK[0], h1b[:])

            def second_norm(y):
                centred_and_scaled(1, y, ln2)
                divided_and_shifted(1, y, ln2, lambda u: hid[:, bass.ds(y + PAIRS, 1), u, :].rearrange("p o d -> p (o d)"), s_hid)

            def step(s, first, second=False, last=False):
                mask_and_max(s, 2, first)
                mask_and_max(s, 3, first)
                if not first:
                    first_sum(s - 1)
                    first_norm(s - 1, second)
                if first:
                    embed_sum(2)
                mask_and_max(s, 4, first)
                if first:
                    embed_norm(2)
                if not first and not second:
                    second_sum(s - 2)
                if not first:
                    h1T_copy(s - 1, second)
                if not first and not second:
                    stats(1, s - 2)
                if not last:
                    hT_copy(s + 1, False)
                mask_and_max(s, 5, first)
                if first:
                    embed_sum(3)
                padded_keys(s)
                if not first and not second:
                    second_norm(s - 2)
                if first:
                    for c in range(2):
                        dve.wait_ge(s_img_ps[c], 1)
                        v.tensor_tensor(img[:, 2 * c:2 * c + 2, :], M_BANK[c][0:IP, 0:2 * D].rearrange("p (c d) -> p c d", c=2),
                                        img_pos[:].unsqueeze(1).to_broadcast([IP, 2, D]), ALU.add).then_inc(s_img[c], 1)
                    embed_norm(3)
                if not last:
                    qk_split(s + 1, 0)
                    mask_and_max(s + 1, 0, False)
                    qk_split(s + 1, 1)
                else:
                    for u in range(2):
                        x_stats(u, u, 0)
                normalise(s, first)
                if not last:
                    mask_and_max(s + 1, 1, False)
                    qk_split(s + 1, 2)

            def x_stats(u, b, n):
                for h in range(2):
                    i = v.bn_stats(xst[u][:, h, :], x[:, bass.ds(b, 1), h, :].rearrange("p o d -> p (o d)"))
                i.then_inc(s_xst[u], 1)
                dve.wait_ge(s_xst[u], n + 1)
                v.memset(tick[:], 0.0)
                for h in range(2):
                    i = v.bn_aggr(xmv[u][:, h, :], xst[u][:, h, :])
                i.then_inc(s_xmv[u], 1)

            def x_apply(u, b, n, first):
                dve.wait_ge(s_xmv[u], n + 1)
                dve.wait_ge(s_xrs[u], n + 1)
                if not first:
                    dve.wait_ge(s_xT_ps[u], n)
                for h in range(2):
                    i = v.tensor_scalar(xn[u][:, h, :], x[:, bass.ds(b, 1), h, :].rearrange("p o d -> p (o d)"),
                                        xmv[u][:, h, 0:1], xrs[u][:, h:h + 1], ALU.subtract, ALU.mult)
                i.then_inc(s_xn[u], 1)

            def x_T(u, n, first, src=None):
                dve.wait_ge(s_xT_ps[u], n + 1)
                if not first:
                    dve.wait_ge(s_qkv_ps, sixth(n - 1, 3 * u + 2))
                v.tensor_copy(xT[u][:], (src or bank[u])[0:KD, 0:4 * NH].rearrange("p (k t) -> p k t", k=KT)).then_inc(s_xT[u], 1)

            hT_copy(0, True)
            embed_norm(1)
            dve.wait_ge(s_pset, 2)
            qk_split(0, 0)
            qk_split(0, 1)
            dve.wait_ge(s_mask_ok, 1)
            mask_and_max(0, 0, True)
            qk_split(0, 2)
            mask_and_max(0, 1, True)
            step(0, True)
            dve.wait_ge(s_mask_ok, 2)
            step(1, False, second=True)
            with dve.Fori(2, STEPS - 1) as s:
                step(s, False)
            dve.wait_ge(s_x, 32)
            step(STEPS - 1, False, last=True)
            for u in range(2):
                x_apply(u, u, 0, True)
            for u in range(2):
                x_T(u, 0, True)
            first_sum(STEPS - 1)
            dve.wait_ge(s_x, 64)
            for u in range(2):
                x_stats(u, 2 + u, 1)
            first_norm(STEPS - 1, False)
            second_sum(STEPS - 2)
            stats(1, STEPS - 2)
            for u in range(2):
                x_apply(u, 2 + u, 1, False)
            h1T_copy(STEPS - 1, False)
            second_norm(STEPS - 2)
            for u in range(2):
                x_T(u, 1, False)
            dve.wait_ge(s_x, 96)
            for u in range(2):
                x_stats(u, 4 + u, 2)
            for u in range(2):
                x_apply(u, 4 + u, 2, False)
            for u in range(2):
                x_T(u, 2, False)
            second_sum(STEPS - 1)
            stats(1, STEPS - 1)
            second_norm(STEPS - 1)

            def j_q_split(b):
                for c in range(2):
                    dve.wait_ge(j_qh, half_of(b, c))
                    v.scalar_tensor_tensor(jqT[:, 2 * c:2 * c + 2, :], jq_hi[:, 2 * c:2 * c + 2, :].bitcast(F32), low_rows[0:JR * PADH, 0:1],
                                           M_BANK[JQ_AT[c]][0:JR * PADH, 0:4 * NH].rearrange("p (g t) -> p g t", g=2), ALU.mult, ALU.add).then_inc(j_qT, 1)

            def j_k_split(b, c):
                dve.wait_ge(j_kh, half_of(b, c))
                for r in range(JR):
                    rows_ = slice(PADH * r, PADH * r + PADH)
                    i = v.tensor_tensor(jk_lo[rows_, 2 * c:2 * c + 2, r, :], M_BANK[JK_AT[c]][rows_, 0:4 * NH].rearrange("p (g t) -> p g t", g=2),
                                        jk_hi[rows_, 2 * c:2 * c + 2, r, :].bitcast(F32), ALU.subtract)
                i.then_inc(j_kl, 1)

            def j_centre(b, i, first):
                dve.wait_ge(j_score, nth(b, i))
                s_ = S_BANK[i % 2][0:NH, 0:JR * 2 * NH].rearrange("p (r t) -> p r t", r=JR)
                v.tensor_reduce(jmx[:, i, :], s_, AX_X, ALU.max).then_inc(j_max, 1)
                dve.wait_ge(j_max, JS * b + i + 1)
                if i >= 4:
                    dve.wait_ge(j_pT_ps, nth(b, i - 4))
                elif not first:
                    dve.wait_ge(j_pT_ps, nth(b - 1, i + JS - 4))
                v.tensor_tensor(jps[i % 4], s_, jmx[:, i, :].unsqueeze(2).to_broadcast([NH, JR, 2 * NH]), ALU.subtract).then_inc(j_centred, 1)

            def j_normalise(b, first):
                dve.wait_ge(j_pv, JS * (b + 1))
                o = O_BANK[0:NH, 0:2 * H * VA].rearrange("p (u h d) -> p u h d", u=2, h=H)
                v.reciprocal(jrden[:], o[:, :, :, HD]).then_inc(j_rden, 1)
                dve.wait_ge(j_rden, b + 1)
                if not first:
                    dve.wait_ge(j_aT_ps, b)
                v.tensor_tensor(jatt[:].rearrange("p u (h d) -> p (u h) d", h=H),
                                O_BANK[0:NH, 0:2 * H * VA].rearrange("p (u h d) -> p (u h) d", u=2, h=H)[:, :, 0:HD],
                                jrden[:].rearrange("p u h -> p (u h)").unsqueeze(2).to_broadcast([NH, 2 * H, HD]), ALU.mult).then_inc(j_att, 1)

            def j_first_sum(y, first=False):
                if not first:
                    dve.wait_ge(j_z2, y)
                    dve.wait_ge(j_n1, y)
                dve.wait_ge(j_wo_ps, y + 1)
                v.tensor_tensor(jz1[:], M_BANK[1][0:NH, 0:2 * D].rearrange("p (h d) -> p h d", h=2),
                                x[:, bass.ds(y, 1), :, :].rearrange("p o h d -> p (o h) d"), ALU.add).then_inc(j_z1, 1)
                dve.wait_ge(j_z1, y + 1)
                for h in range(2):
                    i = v.bn_stats(xst[0][:, h, :], jz1[:, h, :])
                i.then_inc(j_st, 1)
                dve.wait_ge(j_st, y + 1)
                v.memset(tick[:], 0.0)
                for h in range(2):
                    i = v.bn_aggr(xmv[0][:, h, :], xst[0][:, h, :])
                i.then_inc(j_mv, 1)

            def j_norm(y, first):
                dve.wait_ge(j_mv, y + 1)
                dve.wait_ge(j_rs, y + 1)
                if not first:
                    dve.wait_ge(j_x1T_ps, y)
                for h in range(2):
                    i = v.tensor_scalar(jn1[:, h, :], jz1[:, h, :], xmv[0][:, h, 0:1], xrs[0][:, h:h + 1], ALU.subtract, ALU.mult)
                i.then_inc(j_n1, 1)

            def j_x1T_copy(y, first):
                dve.wait_ge(j_x1T_ps, y + 1)
                if not first:
                    dve.wait_ge(j_up[1], y)
                v.tensor_copy(jx1T[0:KD, :, :], M_BANK[0][0:KD, 0:4 * NH].rearrange("p (k t) -> p k t", k=KT)).then_inc(j_x1T, 1)

            def j_second_sum(y, first):
                dve.wait_ge(j_down, y + 1)
                dve.wait_ge(j_z2, y + 1)
                if not first:
                    dve.wait_ge(s_stored, 16 * y)
                v.tensor_tensor(jout[:], M_BANK[2][0:NH, 0:2 * D].rearrange("p (h d) -> p h d", h=2), jz2[:], ALU.add).then_inc(j_out, 1)

            def j_step(b, first=False, second=False, last=False):
                j_centre(b, 2, first)
                if first:
                    dve.wait_ge(s_x, 128)
                    for u in range(2):
                        x_stats(u, 6 + u, 3)
                if not first:
                    j_first_sum(b - 1, second)
                j_centre(b, 3, first)
                if first:
                    for u in range(2):
                        x_apply(u, 6 + u, 3, False)
                if not first:
                    j_norm(b - 1, second)
                j_centre(b, 4, first)
                if first:
                    for u in range(2):
                        x_T(u, 3, False, M_BANK[u])
                if not first:
                    j_x1T_copy(b - 1, second)
                j_centre(b, 5, first)
                if not first and not second:
                    j_second_sum(b - 2, isinstance(b, int) and b == 2)
                j_centre(b, 6, first)
                j_centre(b, 7, first)
                if not last:
                    j_q_split(b + 1)
                    j_k_split(b + 1, 0)
                    j_k_split(b + 1, 1)
                j_normalise(b, first)
                if not last:
                    j_centre(b + 1, 0, False)
                    j_centre(b + 1, 1, False)

            j_q_split(0)
            j_k_split(0, 0)
            j_k_split(0, 1)
            j_centre(0, 0, True)
            j_centre(0, 1, True)
            j_step(0, first=True)
            j_step(1, second=True)
            j_step(2)
            with dve.Fori(3, B - 1) as b:
                j_step(b)
            j_step(B - 1, last=True)
            j_first_sum(B - 1)
            j_second_sum(B - 2, False)
            j_norm(B - 1, False)
            j_x1T_copy(B - 1, False)
            j_second_sum(B - 1, False)

        @block.tensor
        def _(pe):
            t = nc.tensor
            pe.wait_ge(s_vset, 1)
            pe.wait_ge(s_ident, 32)

            def embed_patches(c):
                if c == 0:
                    pe.wait_ge(s_patches, 16)
                    pe.wait_ge(s_conv, 48)
                    pe.wait_ge(s_qk, qk(0, 2))
                o = M_BANK[c // 2][0:IP, (c % 2) * D:(c % 2 + 1) * D]
                for k in range(PC):
                    t.matmul(o, patches[:, k, c * IP:(c + 1) * IP], conv_w[:, k, :], start=(k == 0), stop=False)
                i = t.matmul(o, ones_row[0:1, 0:IP], conv_b[:], start=False, stop=True)
                if c % 2:
                    i.then_inc(s_img_ps[c // 2], 1)

            def transposed(src, dst, n, done):
                for k in range(KT):
                    for u in range(2):
                        i = t.transpose(dst[0:KD, (2 * k + u) * n:(2 * k + u + 1) * n], src[:, u, k * KD:(k + 1) * KD], ident[0:n, 0:n])
                i.then_inc(done, 1)

            def kdim(k):
                return KD + k

            def project_in(s, y=None):
                if isinstance(s, int) and s == 0:
                    pe.wait_ge(s_hid, 1)
                else:
                    pe.wait_ge(s_pair_in, s)
                if y is not None:
                    pe.wait_ge(s_z[0], y + 1)
                transposed(hid[:, 0] if isinstance(s, int) and s == 0 else pair_in, M_BANK[2], T, s_hT_ps)

            def project_qk(s, hg, y=None):
                if hg == 0:
                    pe.wait_ge(s_hT, s + 1)
                    pe.wait_ge(ok_w["wqkv"], s + 1)
                if y is None and isinstance(s, int) and s == 1 and hg < 2:
                    pe.wait_ge(s_img[1 - hg], 1)
                if hg == 0 and y is not None:
                    pe.wait_ge(s_h1T, y + 1)
                if hg == 1 and y is not None:
                    pe.wait_ge(s_gelu[0], y + 1)
                for j in range(2):
                    c = j * QKP + hg * 128
                    for k in range(KT):
                        i = t.matmul(M_BANK[qk_bank(s, hg)][:, j * 2 * T:(j + 1) * 2 * T], wqkv[0:kdim(k), k, c:c + 128],
                                     hT[0:kdim(k), k, :], start=(k == 0), stop=(k == 1))
                i.then_inc(s_qk_ps, 1)

            def project_v(s, y=None):
                if y is not None:
                    pe.wait_ge(s_gelu[1], y + 1)
                for u in range(2):
                    for k in range(KT):
                        i = t.matmul(M_BANK[2][:, u * D:(u + 1) * D], hT[0:kdim(k), k, u * T:(u + 1) * T],
                                     wqkv[0:kdim(k), k, 2 * QKP:2 * QKP + D], start=(k == 0), stop=(k == 1))
                i.then_inc(s_v_ps, 1)

            def score(s, i, first):
                hg, u = i // 2, i % 2
                if u == 0:
                    pe.wait_ge(s_qk, qk(s, hg))
                if i >= 2:
                    pe.wait_ge(s_masked, group(s, i - 2))
                elif not first:
                    pe.wait_ge(s_masked, group(s - 1, i + TS - 2))
                for part, keys in enumerate((k_hi, k_lo)):
                    m = t.matmul(S_BANK[i % 2][:, :], qT[:, hg, u * T:(u + 1) * T], keys[:, hg, u, :, :].rearrange("p r t -> p (r t)"),
                                 start=(part == 0), stop=(part == 1))
                m.then_inc(s_score, 1)

            def transpose_probs(s, i):
                pe.wait_ge(s_prob, group(s, i))
                for r in range(R):
                    m = t.transpose(T_BANK[i % 2][:, r * T:(r + 1) * T], ps[i][:, r, :], ident[:])
                m.then_inc(s_pT_ps, 1)

            def weigh(s, i, first):
                hg, u = i // 2, i % 2
                if i == 0:
                    pe.wait_ge(s_va, s + 1)
                    if not first:
                        pe.wait_ge(s_att, s)
                pe.wait_ge(s_pT, group(s, i))
                for r in range(R):
                    h = R * hg + r
                    m = t.matmul(O_BANK[:, (u * H + h) * VA:(u * H + h + 1) * VA], pT[i % 2][:, r, :], va[:, u, h, :], start=True, stop=True)
                m.then_inc(s_pv, 1)

            def transpose_attention(y):
                pe.wait_ge(s_att, y + 1)
                if isinstance(y, int) and y == 0:
                    pe.wait_ge(s_qk, qk(1, 0))
                else:
                    pe.wait_ge(s_gelu[2], y)
                transposed(att, M_BANK[1], T, s_aT_ps)

            def project_out(y, last=False):
                pe.wait_ge(s_aT, y + 1)
                pe.wait_ge(ok_w["wo"], y + 1)
                if not last:
                    pe.wait_ge(s_va, y + 2)
                for u in range(2):
                    for k in range(KT):
                        i = t.matmul(M_BANK[2][:, u * D:(u + 1) * D], aT[0:kdim(k), k, u * T:(u + 1) * T], wo[0:kdim(k), k, :],
                                     start=(k == 0), stop=(k == 1))
                i.then_inc(s_wo_ps, 1)

            def mlp_in(y):
                pe.wait_ge(s_h1, y + 1)
                transposed(h1, M_BANK[1], T, s_h1T_ps)

            def mlp_up(y, c, s=None):
                if c == 0:
                    pe.wait_ge(s_h1T, y + 1)
                    pe.wait_ge(ok_w["w1"], y + 1)
                    pe.wait_ge(s_z[1], y + 1)
                if c == 1 and s is not None:
                    pe.wait_ge(s_hT, s + 1)
                if c == 2 and s is not None:
                    pe.wait_ge(s_qk, qk(s, 0))
                for q in range(2):
                    m = 2 * c + q
                    for k in range(KT):
                        i = t.matmul(M_BANK[UP_AT[c]][:, q * 2 * T:(q + 1) * 2 * T], w1[0:kdim(k), k, m * 128:(m + 1) * 128],
                                     h1T[0:kdim(k), k, :], start=(k == 0), stop=(k == 1))
                i.then_inc(s_up[c], 1)

            def mlp_down(y, u):
                if u == 0:
                    for c in range(3):
                        pe.wait_ge(s_gelu[c], y + 1)
                    pe.wait_ge(ok_w["w2"], y + 1)
                    if isinstance(y, int) and y >= STEPS - 2:
                        pass
                    else:
                        pe.wait_ge(s_qk, qk(y + 2, 2))
                for c in range(FC):
                    i = t.matmul(M_BANK[0][:, u * D:(u + 1) * D], f[:, c, u * T:(u + 1) * T], w2[:, c, :], start=(c == 0), stop=(c == FC - 1))
                if u == 1:
                    i.then_inc(s_down, 1)

            def step(s, first=False, second=False, last=False):
                y = None if first else s - 1
                z = None if first or second else s - 2
                if y is not None:
                    transpose_attention(y)
                score(s, 2, first)
                transpose_probs(s, 0)
                score(s, 3, first)
                if y is not None:
                    project_out(y)
                weigh(s, 0, first)
                transpose_probs(s, 1)
                score(s, 4, first)
                if first:
                    embed_patches(0)
                if z is not None:
                    mlp_down(z, 0)
                weigh(s, 1, first)
                transpose_probs(s, 2)
                score(s, 5, first)
                if first:
                    embed_patches(1)
                if z is not None:
                    mlp_down(z, 1)
                if y is not None:
                    mlp_in(y)
                if not last:
                    project_in(s + 1, y)
                weigh(s, 2, first)
                if first:
                    embed_patches(2)
                transpose_probs(s, 3)
                if first:
                    embed_patches(3)
                nxt = None if last else s + 1
                if y is not None:
                    mlp_up(y, 0)
                weigh(s, 3, first)
                if not last:
                    project_qk(s + 1, 0, y)
                transpose_probs(s, 4)
                if y is not None:
                    mlp_up(y, 1, nxt)
                if not last:
                    project_qk(s + 1, 1, y)
                weigh(s, 4, first)
                if not last:
                    score(s + 1, 0, False)
                transpose_probs(s, 5)
                if y is not None:
                    mlp_up(y, 2, nxt)
                weigh(s, 5, first)
                if not last:
                    score(s + 1, 1, False)
                    project_v(s + 1, y)
                    pe.wait_ge(s_qk, qk(s + 1, 1))
                    project_qk(s + 1, 2)

            project_in(0)
            for hg in range(HG):
                project_qk(0, hg)
            score(0, 0, True)
            score(0, 1, True)
            pe.wait_ge(s_qk, qk(0, 2))
            project_v(0)
            step(0, first=True)
            step(1, second=True)
            with pe.Fori(2, STEPS - 1) as s:
                step(s)
            step(STEPS - 1, last=True)

            def j_transpose(n, u, first, dst=None):
                pe.wait_ge(s_xn[u], n + 1)
                if first:
                    pe.wait_ge(s_masked, group(STEPS - 1, TS - 2 + u))
                transposed(xn[u], dst or bank[u], NH, s_xT_ps[u])

            def j_project_last(j):
                if j == 0:
                    pe.wait_ge(s_xT[1], PAIRS)
                    pe.wait_ge(j_qT, half_of(1, 1))
                elif j == 1:
                    pe.wait_ge(j_kl, half_of(1, 0))
                else:
                    pe.wait_ge(s_qkv_sb, sixth(PAIRS - 1, 3))
                for h in range(2):
                    for k in range(KT):
                        i = t.matmul(JQKV_AT[3 + j][0:NH, h * D:(h + 1) * D], xT[1][:, k, h * NH:(h + 1) * NH],
                                     jwqkv[:, k, j * D:(j + 1) * D], start=(k == 0), stop=(k == 1))
                i.then_inc(s_qkv_ps, 1)

            def j_project(n, u, first, at=bank[2:5]):
                pe.wait_ge(s_xT[u], n + 1)
                if first and u == 0:
                    pe.wait_ge(s_pT, group(STEPS - 1, TS - 1))
                    pe.wait_ge(s_att, STEPS)
                for j in range(3):
                    if n == PAIRS - 1:
                        if u == 0:
                            pe.wait_ge(j_kl, 2)
                            pe.wait_ge(s_xT[1], n + 1)
                    if not (first and u == 0):
                        pe.wait_ge(s_qkv_sb, 6 * n + 3 * u + j - 2)
                    for h in range(2):
                        for k in range(KT):
                            i = t.matmul(at[j][0:NH, h * D:(h + 1) * D], xT[u][:, k, h * NH:(h + 1) * NH],
                                         jwqkv[:, k, j * D:(j + 1) * D], start=(k == 0), stop=(k == 1))
                    i.then_inc(s_qkv_ps, 1)

            pe.wait_ge(s_jw, 64)
            for u in range(2):
                j_transpose(0, u, True)
            transpose_attention(STEPS - 1)
            j_project(0, 0, True)
            project_out(STEPS - 1, last=True)
            for u in range(2):
                mlp_down(STEPS - 2, u)
            j_project(0, 1, True)
            mlp_in(STEPS - 1)
            for u in range(2):
                j_transpose(1, u, False)
            mlp_up(STEPS - 1, 0)
            mlp_up(STEPS - 1, 1)
            j_project(1, 0, False)
            mlp_up(STEPS - 1, 2)
            j_project(1, 1, False)
            for u in range(2):
                j_transpose(2, u, False)
            for u in range(2):
                mlp_down(STEPS - 1, u)

            def j_queries(b, z=None):
                pe.wait_ge(j_qdup, b + 1)
                if isinstance(b, int) and b == 0:
                    pe.wait_ge(s_gelu[2], STEPS)
                    pe.wait_ge(s_z[1], STEPS + 1)
                if isinstance(b, int) and b == 1:
                    pe.wait_ge(s_qkv_sb, sixth(PAIRS - 1, 2))
                for c in range(2):
                    if c == 1 and z is not None:
                        pe.wait_ge(j_out, z + 2)
                    split_heads(qpad, c, M_BANK[JQ_AT[c]], j_qT_ps)

            def j_keys(b, c):
                if c == 0:
                    pe.wait_ge(j_kdup, b + 1)
                else:
                    pe.wait_ge(j_qT, half_of(b, 0))
                split_heads(kpad, c, M_BANK[JK_AT[c]], j_kT_ps)

            def split_heads(pad, c, dst, done):
                for g in range(2):
                    for h in range(2):
                        h0 = JR * (2 * c + g)
                        i = t.transpose(dst[0:JR * PADH, (2 * g + h) * NH:(2 * g + h + 1) * NH],
                                        pad[:, h, h0:h0 + JR].rearrange("p r c d -> p (r c d)"), ident[0:NH, 0:NH])
                i.then_inc(done, 1)

            def j_transpose_attention(y, first=False):
                pe.wait_ge(j_att, y + 1)
                if first:
                    pe.wait_ge(j_kl, half_of(1, 0))
                else:
                    pe.wait_ge(j_gelu[1], y)
                transposed(jatt, M_BANK[0], NH, j_aT_ps)

            def j_project_out(y, last=False):
                pe.wait_ge(j_aT, y + 1)
                if not last:
                    pe.wait_ge(j_kl, half_of(y + 1, 1))
                for h in range(2):
                    for k in range(KT):
                        i = t.matmul(M_BANK[1][0:NH, h * D:(h + 1) * D], jaT[0:kdim(k), k, h * NH:(h + 1) * NH], jwo[0:kdim(k), k, :],
                                     start=(k == 0), stop=(k == 1))
                i.then_inc(j_wo_ps, 1)

            def j_mlp_in(y):
                pe.wait_ge(j_n1, y + 1)
                transposed(jn1, M_BANK[0], NH, j_x1T_ps)

            def j_mlp_up(y, c, nxt=None):
                if c == 0:
                    pe.wait_ge(j_x1T, y + 1)
                    if nxt is not None:
                        pe.wait_ge(j_qT, half_of(nxt, 1))
                    else:
                        pe.wait_ge(j_out, y + 1)
                elif nxt is not None:
                    pe.wait_ge(j_kl, half_of(nxt, 0))
                for q in range(3):
                    m = 3 * c + q
                    for k in range(KT):
                        i = t.matmul(M_BANK[JUP_AT[c]][:, q * 2 * NH:(q + 1) * 2 * NH], jw1[0:kdim(k), k, m * 128:(m + 1) * 128],
                                     jx1T[0:kdim(k), k, :], start=(k == 0), stop=(k == 1))
                i.then_inc(j_up[c], 1)

            def j_mlp_down(y, part):
                h, lo = part // 2, part % 2 * FC // 2
                if part == 0:
                    pe.wait_ge(j_gelu[0], y + 1)
                    pe.wait_ge(j_gelu[1], y + 1)
                for c in range(lo, lo + FC // 2):
                    i = t.matmul(M_BANK[2][0:NH, h * D:(h + 1) * D], jf[:, c, h * NH:(h + 1) * NH], jw2[:, c, :],
                                 start=(c == 0), stop=(c == FC - 1))
                if part == 3:
                    i.then_inc(j_down, 1)

            def j_scores(b, i, first):
                g, half = i // 2, i % 2
                if i == 0:
                    pe.wait_ge(j_qT, half_of(b, 1))
                    pe.wait_ge(j_kl, half_of(b, 1))
                if i >= 2:
                    pe.wait_ge(j_centred, nth(b, i - 2))
                elif not first:
                    pe.wait_ge(j_centred, nth(b - 1, i + JS - 2))
                for part, keys in enumerate((jk_hi, jk_lo)):
                    m = t.matmul(S_BANK[i % 2][0:NH, 0:JR * 2 * NH], jqT[:, g, half * NH:(half + 1) * NH],
                                 keys[:, g, :, :].rearrange("p r t -> p (r t)"), start=(part == 0), stop=(part == 1))
                m.then_inc(j_score, 1)

            def j_transpose_probs(b, i):
                pe.wait_ge(j_prob_s, nth(b, i))
                for r in range(JR):
                    for k in range(2):
                        m = t.transpose(T_BANK[i % 2][0:NH, (2 * r + k) * NH:(2 * r + k + 1) * NH], jps[i % 4][:, r, k * NH:(k + 1) * NH], ident[0:NH, 0:NH])
                m.then_inc(j_pT_ps, 1)

            def j_weigh(b, i, first):
                g, half = i // 2, i % 2
                if i == 0:
                    pe.wait_ge(j_va, b + 1)
                    if not first:
                        pe.wait_ge(j_att, b)
                pe.wait_ge(j_pT, nth(b, i))
                for r in range(JR):
                    for k in range(2):
                        c = (half * H + JR * g + r) * VA
                        m = t.matmul(O_BANK[0:NH, c:c + VA], jpT[i % 2][:, r, k, :], jva[:, k, JR * g + r, :], start=(k == 0), stop=(k == 1))
                m.then_inc(j_pv, 1)

            def j_step(b, first=False, second=False, last=False):
                y = None if first else b - 1
                z = None if first or second else b - 2
                nxt = None if last else b + 1
                if z is not None:
                    j_mlp_down(z, 0)
                    j_mlp_down(z, 1)
                if second:
                    pe.wait_ge(s_qkv_sb, 6 * PAIRS)
                if not first:
                    j_transpose_attention(y, second)
                j_transpose_probs(b, 0)
                j_scores(b, 2, first)
                if not first:
                    j_project_out(y, last)
                j_transpose_probs(b, 1)
                j_weigh(b, 0, first)
                j_scores(b, 3, first)
                j_transpose_probs(b, 2)
                j_weigh(b, 1, first)
                j_scores(b, 4, first)
                if z is not None:
                    j_mlp_down(z, 2)
                if first:
                    pe.wait_ge(j_kl, 2)
                    for u in range(2):
                        j_transpose(PAIRS - 1, u, False, M_BANK[u])
                else:
                    j_mlp_in(y)
                j_transpose_probs(b, 3)
                j_weigh(b, 2, first)
                j_scores(b, 5, first)
                if first:
                    j_project(PAIRS - 1, 0, False, JQKV_AT[0:3])
                if z is not None:
                    j_mlp_down(z, 3)
                j_transpose_probs(b, 4)
                j_weigh(b, 3, first)
                j_scores(b, 6, first)
                j_transpose_probs(b, 5)
                j_weigh(b, 4, first)
                j_scores(b, 7, first)
                if last:
                    j_mlp_up(y, 0)
                else:
                    j_queries(b + 1, z)
                j_transpose_probs(b, 6)
                j_weigh(b, 5, first)
                if not last:
                    j_keys(b + 1, 0)
                    j_keys(b + 1, 1)
                if first:
                    j_project_last(0)
                elif last:
                    j_mlp_up(y, 1)
                else:
                    j_mlp_up(y, 0, nxt)
                j_transpose_probs(b, 7)
                j_weigh(b, 6, first)
                if first:
                    j_project_last(1)
                elif not last:
                    j_mlp_up(y, 1, nxt)
                j_weigh(b, 7, first)
                if first:
                    j_project_last(2)
                if not last:
                    j_scores(b + 1, 0, False)
                    j_scores(b + 1, 1, False)

            j_project(2, 0, False)
            j_queries(0)
            j_keys(0, 0)
            j_keys(0, 1)
            j_project(2, 1, False)
            pe.wait_ge(s_xT[0], 3)
            pe.wait_ge(s_xT[1], 3)
            j_scores(0, 0, True)
            j_scores(0, 1, True)
            pe.wait_ge(s_qkv_sb, 6 * 3)
            j_step(0, first=True)
            j_step(1, second=True)
            with pe.Fori(2, B - 1) as b:
                j_step(b)
            j_step(B - 1, last=True)
            j_mlp_down(B - 2, 0)
            j_transpose_attention(B - 1)
            j_mlp_down(B - 2, 1)
            j_project_out(B - 1, last=True)
            j_mlp_down(B - 2, 2)
            j_mlp_down(B - 2, 3)
            j_mlp_in(B - 1)
            for c in range(2):
                j_mlp_up(B - 1, c)
            for part in range(4):
                j_mlp_down(B - 1, part)


def kernel(**inputs):
    import concourse.bacc as bacc
    from concourse.bass_utils import run_bass_kernel_spmd

    g = {k: np.asarray(v) for k, v in inputs.items()}

    def tiles(w, bias=None):
        o = np.zeros((KD + 1, KT, w.shape[1]), w.dtype)
        o[0:KD] = w.reshape(KT, KD, -1).transpose(1, 0, 2)
        if bias is not None:
            o[KD, 1] = bias
        return o

    def heads(w):
        o = w.reshape(w.shape[:-1] + (H, HD))
        return np.concatenate([o, o], -1).reshape(w.shape[:-1] + (QKP,))

    def txt(n):
        return g["L0_txt_" + n]

    side = IMG_SIDE // PATCH
    at = np.searchsorted(np.arange(1 / 32, 1, 1 / 32, dtype=np.float32), np.arange(0, 1 - 1e-6, 1 / side, dtype=np.float32), side="right")
    pos_rows = g["L0_tok_pos_table"][(at[:, None] * 32 + at).reshape(-1)]
    arrays = {
        "ids": g["x_txt"].T,
        "mask": g["mask_BS_i1_0"],
        "ident": np.eye(128, dtype=np.float32),
        "low_rows": -(np.arange(128)[:, None] % PADH // HD).astype(np.float32),
        "patches": g["x"].reshape(B, CH, side, PATCH, side, PATCH).transpose(1, 3, 5, 0, 2, 4).reshape(PW, B * NI),
        "conv_w": g["L0_tok_conv_w"].reshape(D, PW).T,
        "conv_b": g["L0_tok_conv_b"].reshape(1, D),
        "img_pos": np.concatenate([pos_rows, pos_rows]),
        "emb_word": txt("emb_word"),
        "emb_pos": txt("emb_pos")[0:T],
        "emb_ln": np.stack([txt("emb_ln_s"), txt("emb_ln_b")]),
        "wqkv": np.stack([np.concatenate([tiles(heads(txt("Wq")[l]), heads(txt("bq")[l])), tiles(heads(txt("Wk")[l]), heads(txt("bk")[l])),
                                          tiles(txt("Wv")[l], txt("bv")[l])], 2) for l in range(L)]),
        "wo": np.stack([tiles(txt("Wo")[l], txt("bo")[l]) for l in range(L)]),
        "w1": np.stack([tiles(txt("W1")[l], txt("b1")[l]) for l in range(L)]),
        "w2": txt("W2"),
        "b2": txt("b2"),
        "ln1": np.stack([txt("ln1_s"), txt("ln1_b")], 1),
        "ln2": np.stack([txt("ln2_s"), txt("ln2_b")], 1),
        "jwqkv": tiles(np.concatenate([g["L0_attn_w_q"].T, g["L0_attn_w_k"].T, g["L0_attn_w_v"].T], 1))[0:KD],
        "jwo": tiles(g["L0_attn_w_o"].T, g["L0_attn_b_o"]),
        "jw1": tiles(g["L0_ffn_in_weight"].T, g["L0_ffn_in_bias"]),
        "jw2": g["L0_ffn_out_weight"],
    }
    arrays = {f"in_{k}": np.ascontiguousarray(v) for k, v in arrays.items()}
    nc = bacc.Bacc("TRN2", target_bir_lowering=False, num_devices=1)
    aps = {k[3:]: nc.dram_tensor(k, v.shape, mybir.dt.from_np(v.dtype), kind="ExternalInput").ap() for k, v in arrays.items()}
    out = nc.dram_tensor("out", (B, N, D), F32, kind="ExternalOutput").ap()
    program(nc, aps, out)
    r = run_bass_kernel_spmd(nc, [arrays], core_ids=[0])
    return r.results[0]["out"]
```
